# Optimizing a Trainium2 kernel written in Bass

```python
import numpy as np
import jax
import jax.numpy as jnp

def _softmax(x, axis=-1):
    return jax.nn.softmax(x, axis=axis)

def _gelu(x):
    return jax.nn.gelu(x, approximate=True)

def _silu(x):
    return jax.nn.silu(x)

def _sigmoid(x):
    return jax.nn.sigmoid(x)

def _layernorm(x, axis=-1, eps=1e-05):
    m = jnp.mean(x, axis=axis, keepdims=True)
    v = jnp.var(x, axis=axis, keepdims=True)
    return (x - m) / jnp.sqrt(v + eps)

def _scatter_add(tgt, idx, src, axis=0):
    return tgt.at[idx].add(src)

def _segment_sum(src, seg, n):
    return jax.ops.segment_sum(src, seg, n)
kernel_name = 'mk_xattn_seq_d2_seqx_r8_74cde1'

def setup_inputs(seed: int=0):
    np.random.seed(seed)
    _w = jnp.asarray

    def _rec_inputs():
        import jax
        import jax.numpy as jnp
        _rk = jax.random.key(seed)
        x = -0.0002928 + 1 * jax.random.normal(jax.random.fold_in(_rk, 1), (16, 128, 256), jnp.float32)
        _lenS = 128 - jax.random.randint(jax.random.fold_in(_rk, 7), (16,), 0, max(1, 128 // 4) + 1, jnp.int32)
        _lenS2 = 128 - jax.random.randint(jax.random.fold_in(_rk, 8), (16,), 0, max(1, 128 // 4) + 1, jnp.int32)
        _ctx_2048P = jax.random.normal(jax.random.fold_in(_rk, 11), (16, 16, 256), jnp.float32)
        _ctx_2048c = jax.random.dirichlet(jax.random.fold_in(_rk, 511), 0.3 * jnp.ones((16,), jnp.float32), (16, 128))
        _ctx_2048t = jnp.einsum('bsk,bkd->bsd', _ctx_2048c, _ctx_2048P)
        _ctx_2048t = _ctx_2048t * jax.lax.rsqrt(jnp.mean(jnp.square(_ctx_2048t)) + 1e-12) * 0.953939
        ctx_2048 = -1.39393e-06 + 0.999914 * (_ctx_2048t + 0.3 * jax.random.normal(jax.random.fold_in(_rk, 611), (16, 128, 256), jnp.float32))
        _validS = jnp.arange(128)[None, :] < _lenS[:, None]
        _validS2 = jnp.arange(128)[None, :] < _lenS2[:, None]
        _causal = jnp.tril(jnp.ones((128, 128), dtype=bool))
        mask_1x1xSxS2_fc1 = jnp.where(jnp.broadcast_to(_validS2[0:1, None, None, :], (1, 1, 128, 128)), 1.0, 0.0).astype(jnp.float32)
        mask_Bx1xSxS2_ff1 = jnp.where(jnp.ones((16, 1, 128, 128), dtype=bool), 1.0, 0.0).astype(jnp.float32)
        return (x, ctx_2048, mask_1x1xSxS2_fc1, mask_Bx1xSxS2_ff1)
    x, ctx_2048, mask_1x1xSxS2_fc1, mask_Bx1xSxS2_ff1 = _rec_inputs()

    def _L0_xattn_setup():
        import jax, jax.numpy as jnp
        import numpy as np
        H = 256
        NH = 16
        HD = H // NH
        EPS = 1e-05

        def gelu(x):
            return 0.5 * x * (1.0 + jnp.tanh(0.7978845608028654 * x * (1.0 + 0.044715 * x * x)))

        def layernorm(x, scale, bias):
            m = jnp.mean(x, axis=-1, keepdims=True)
            v = jnp.mean(jnp.square(x - m), axis=-1, keepdims=True)
            return (x - m) * jax.lax.rsqrt(v + EPS) * scale + bias

        def split_heads(x):
            b, s, _ = x.shape
            return x.reshape(b, s, NH, HD).transpose(0, 2, 1, 3)

        def merge_heads(x):
            b, nh, s, hd = x.shape
            return x.transpose(0, 2, 1, 3).reshape(b, s, nh * hd)

        def attention(q, k, v, mask):
            scores = jnp.einsum('bhqd,bhkd->bhqk', q, k) / jnp.sqrt(jnp.float32(HD))
            scores = scores * mask - 10000.0 * (1.0 - mask)
            probs = jax.nn.softmax(scores, axis=-1)
            return jnp.einsum('bhqk,bhkd->bhqd', probs, v)
        key = jax.random.key(seed)
        ks = jax.random.split(key, 16)
        b, s, t = (2, 128, 128)
        w = lambda k, i, o: jax.random.normal(k, (i, o), jnp.float32) * 0.02
        inp = {'hidden_states': jax.random.normal(ks[0], (b, s, H), jnp.float32), 'encoder_states': jax.random.normal(ks[1], (b, t, H), jnp.float32), 'ltor_mask': jnp.tril(jnp.ones((1, 1, s, s), jnp.float32)), 'cross_mask': jnp.ones((b, 1, s, t), jnp.float32), 'ln1_s': jnp.ones((H,), jnp.float32), 'ln1_b': jnp.zeros((H,), jnp.float32), 'w_qkv': w(ks[2], H, 3 * H), 'b_qkv': jnp.zeros((3 * H,), jnp.float32), 'w_ao': w(ks[3], H, H), 'b_ao': jnp.zeros((H,), jnp.float32), 'ln2_s': jnp.ones((H,), jnp.float32), 'ln2_b': jnp.zeros((H,), jnp.float32), 'w_q': w(ks[4], H, H), 'b_q': jnp.zeros((H,), jnp.float32), 'w_kv': w(ks[5], H, 2 * H), 'b_kv': jnp.zeros((2 * H,), jnp.float32), 'w_co': w(ks[6], H, H), 'b_co': jnp.zeros((H,), jnp.float32), 'ln3_s': jnp.ones((H,), jnp.float32), 'ln3_b': jnp.zeros((H,), jnp.float32), 'w1': w(ks[7], H, 4 * H), 'b1': jnp.zeros((4 * H,), jnp.float32), 'w2': w(ks[8], 4 * H, H), 'b2': jnp.zeros((H,), jnp.float32)}
        return inp
    _L0_xattn_all = _L0_xattn_setup()
    _L0_xattn_in = {k: v for k, v in _L0_xattn_all.items() if k in ('ln1_s', 'ln1_b', 'w_qkv', 'b_qkv', 'w_ao', 'b_ao', 'ln2_s', 'ln2_b', 'w_q', 'b_q', 'w_kv', 'b_kv', 'w_co', 'b_co', 'ln3_s', 'ln3_b', 'w1', 'b1', 'w2', 'b2')}
    del _L0_xattn_all

    def _L1_xattn_setup():
        import jax, jax.numpy as jnp
        import numpy as np
        B, L, E, H = (4, 64, 256, 32)
        S = E // H
        EXTRA_MAA, EXTRA_DECAY = (32, 64)
        EPS = 1e-05

        def _ln(x, w, b):
            m = jnp.mean(x, axis=-1, keepdims=True)
            v = jnp.mean((x - m) ** 2, axis=-1, keepdims=True)
            return (x - m) * jax.lax.rsqrt(v + EPS) * w + b

        def _token_shift(xn, prev_row):
            first = (prev_row - xn[:, 0])[:, None]
            rest = xn[:, :-1] - xn[:, 1:]
            return jnp.concatenate([first, rest], axis=1)
        key = jax.random.key(seed)
        ks = jax.random.split(key, 24)
        rn = lambda k, shp, s=1.0: jax.random.normal(k, shp, dtype=jnp.float32) * s
        return dict(x=rn(ks[0], (B, L, E)), state=rn(ks[1], (B, 2 + S, E), 0.1), ln1_w=jnp.ones((E,), jnp.float32), ln1_b=jnp.zeros((E,), jnp.float32), ln2_w=jnp.ones((E,), jnp.float32), ln2_b=jnp.zeros((E,), jnp.float32), maa_x=rn(ks[2], (E,), 0.02), maa_w1=rn(ks[3], (E, 5 * EXTRA_MAA), 0.02), maa_w2=rn(ks[4], (5, EXTRA_MAA, E), 0.02), maa_stack=rn(ks[5], (5, E), 0.02), time_decay=rn(ks[6], (E,), 0.5), decay_w1=rn(ks[7], (E, EXTRA_DECAY), 0.02), decay_w2=rn(ks[8], (EXTRA_DECAY, E), 0.02), faaaa=rn(ks[9], (H, S), 0.1), Wr=rn(ks[10], (E, E), 0.02), Wk=rn(ks[11], (E, E), 0.02), Wv=rn(ks[12], (E, E), 0.02), Wg=rn(ks[13], (E, E), 0.02), Wo=rn(ks[14], (E, E), 0.02), gn_w=jnp.ones((E,), jnp.float32), gn_b=jnp.zeros((E,), jnp.float32), ffn_maa_k=rn(ks[15], (E,), 0.02), ffn_maa_r=rn(ks[16], (E,), 0.02), ffn_Wk=rn(ks[17], (E, E), 0.02), ffn_Wr=rn(ks[18], (E, E), 0.02), ffn_Wv=rn(ks[19], (E, E), 0.02), i=0)
    _L1_xattn_all = _L1_xattn_setup()
    _L1_xattn_in = {k: v for k, v in _L1_xattn_all.items() if k in ('ln1_w', 'ln1_b', 'ln2_w', 'ln2_b', 'maa_x', 'maa_w1', 'maa_w2', 'maa_stack', 'time_decay', 'decay_w1', 'decay_w2', 'faaaa', 'Wr', 'Wk', 'Wv', 'Wg', 'Wo', 'gn_w', 'gn_b', 'ffn_maa_k', 'ffn_maa_r', 'ffn_Wk', 'ffn_Wr', 'ffn_Wv')}
    del _L1_xattn_all
    return {'x': x, 'ctx_2048': ctx_2048, 'mask_1x1xSxS2_fc1': mask_1x1xSxS2_fc1, 'mask_Bx1xSxS2_ff1': mask_Bx1xSxS2_ff1, 'L0_xattn_ln1_s': _L0_xattn_in['ln1_s'], 'L0_xattn_ln1_b': _L0_xattn_in['ln1_b'], 'L0_xattn_w_qkv': _L0_xattn_in['w_qkv'], 'L0_xattn_b_qkv': _L0_xattn_in['b_qkv'], 'L0_xattn_w_ao': _L0_xattn_in['w_ao'], 'L0_xattn_b_ao': _L0_xattn_in['b_ao'], 'L0_xattn_ln2_s': _L0_xattn_in['ln2_s'], 'L0_xattn_ln2_b': _L0_xattn_in['ln2_b'], 'L0_xattn_w_q': _L0_xattn_in['w_q'], 'L0_xattn_b_q': _L0_xattn_in['b_q'], 'L0_xattn_w_kv': _L0_xattn_in['w_kv'], 'L0_xattn_b_kv': _L0_xattn_in['b_kv'], 'L0_xattn_w_co': _L0_xattn_in['w_co'], 'L0_xattn_b_co': _L0_xattn_in['b_co'], 'L0_xattn_ln3_s': _L0_xattn_in['ln3_s'], 'L0_xattn_ln3_b': _L0_xattn_in['ln3_b'], 'L0_xattn_w1': _L0_xattn_in['w1'], 'L0_xattn_b1': _L0_xattn_in['b1'], 'L0_xattn_w2': _L0_xattn_in['w2'], 'L0_xattn_b2': _L0_xattn_in['b2'], 'L1_xattn_ln1_w': _L1_xattn_in['ln1_w'], 'L1_xattn_ln1_b': _L1_xattn_in['ln1_b'], 'L1_xattn_ln2_w': _L1_xattn_in['ln2_w'], 'L1_xattn_ln2_b': _L1_xattn_in['ln2_b'], 'L1_xattn_maa_x': _L1_xattn_in['maa_x'], 'L1_xattn_maa_w1': _L1_xattn_in['maa_w1'], 'L1_xattn_maa_w2': _L1_xattn_in['maa_w2'], 'L1_xattn_maa_stack': _L1_xattn_in['maa_stack'], 'L1_xattn_time_decay': _L1_xattn_in['time_decay'], 'L1_xattn_decay_w1': _L1_xattn_in['decay_w1'], 'L1_xattn_decay_w2': _L1_xattn_in['decay_w2'], 'L1_xattn_faaaa': _L1_xattn_in['faaaa'], 'L1_xattn_Wr': _L1_xattn_in['Wr'], 'L1_xattn_Wk': _L1_xattn_in['Wk'], 'L1_xattn_Wv': _L1_xattn_in['Wv'], 'L1_xattn_Wg': _L1_xattn_in['Wg'], 'L1_xattn_Wo': _L1_xattn_in['Wo'], 'L1_xattn_gn_w': _L1_xattn_in['gn_w'], 'L1_xattn_gn_b': _L1_xattn_in['gn_b'], 'L1_xattn_ffn_maa_k': _L1_xattn_in['ffn_maa_k'], 'L1_xattn_ffn_maa_r': _L1_xattn_in['ffn_maa_r'], 'L1_xattn_ffn_Wk': _L1_xattn_in['ffn_Wk'], 'L1_xattn_ffn_Wr': _L1_xattn_in['ffn_Wr'], 'L1_xattn_ffn_Wv': _L1_xattn_in['ffn_Wv']}

def reference(x, ctx_2048, mask_1x1xSxS2_fc1, mask_Bx1xSxS2_ff1, L0_xattn_ln1_s, L0_xattn_ln1_b, L0_xattn_w_qkv, L0_xattn_b_qkv, L0_xattn_w_ao, L0_xattn_b_ao, L0_xattn_ln2_s, L0_xattn_ln2_b, L0_xattn_w_q, L0_xattn_b_q, L0_xattn_w_kv, L0_xattn_b_kv, L0_xattn_w_co, L0_xattn_b_co, L0_xattn_ln3_s, L0_xattn_ln3_b, L0_xattn_w1, L0_xattn_b1, L0_xattn_w2, L0_xattn_b2, L1_xattn_ln1_w, L1_xattn_ln1_b, L1_xattn_ln2_w, L1_xattn_ln2_b, L1_xattn_maa_x, L1_xattn_maa_w1, L1_xattn_maa_w2, L1_xattn_maa_stack, L1_xattn_time_decay, L1_xattn_decay_w1, L1_xattn_decay_w2, L1_xattn_faaaa, L1_xattn_Wr, L1_xattn_Wk, L1_xattn_Wv, L1_xattn_Wg, L1_xattn_Wo, L1_xattn_gn_w, L1_xattn_gn_b, L1_xattn_ffn_maa_k, L1_xattn_ffn_maa_r, L1_xattn_ffn_Wk, L1_xattn_ffn_Wr, L1_xattn_ffn_Wv):
    import jax
    import jax.numpy as jnp

    def _L0_xattn_ref(hidden_states, encoder_states, ltor_mask, cross_mask, ln1_s, ln1_b, w_qkv, b_qkv, w_ao, b_ao, ln2_s, ln2_b, w_q, b_q, w_kv, b_kv, w_co, b_co, ln3_s, ln3_b, w1, b1, w2, b2):
        import jax, jax.numpy as jnp
        import numpy as np
        H = 256
        NH = 16
        HD = H // NH
        EPS = 1e-05

        def gelu(x):
            return 0.5 * x * (1.0 + jnp.tanh(0.7978845608028654 * x * (1.0 + 0.044715 * x * x)))

        def layernorm(x, scale, bias):
            m = jnp.mean(x, axis=-1, keepdims=True)
            v = jnp.mean(jnp.square(x - m), axis=-1, keepdims=True)
            return (x - m) * jax.lax.rsqrt(v + EPS) * scale + bias

        def split_heads(x):
            b, s, _ = x.shape
            return x.reshape(b, s, NH, HD).transpose(0, 2, 1, 3)

        def merge_heads(x):
            b, nh, s, hd = x.shape
            return x.transpose(0, 2, 1, 3).reshape(b, s, nh * hd)

        def attention(q, k, v, mask):
            scores = jnp.einsum('bhqd,bhkd->bhqk', q, k) / jnp.sqrt(jnp.float32(HD))
            scores = scores * mask - 10000.0 * (1.0 - mask)
            probs = jax.nn.softmax(scores, axis=-1)
            return jnp.einsum('bhqk,bhkd->bhqd', probs, v)
        ln_out = layernorm(hidden_states, ln1_s, ln1_b)
        qkv = ln_out @ w_qkv + b_qkv
        q, k, v = jnp.split(qkv, 3, axis=-1)
        ctx = merge_heads(attention(split_heads(q), split_heads(k), split_heads(v), ltor_mask))
        attn_out = ctx @ w_ao + b_ao
        x = hidden_states + attn_out
        ln_out = layernorm(x, ln2_s, ln2_b)
        q = ln_out @ w_q + b_q
        kv = encoder_states @ w_kv + b_kv
        k, v = jnp.split(kv, 2, axis=-1)
        ctx = merge_heads(attention(split_heads(q), split_heads(k), split_heads(v), cross_mask))
        cross_out = ctx @ w_co + b_co
        x = x + cross_out
        ln_out = layernorm(x, ln3_s, ln3_b)
        mlp_out = gelu(ln_out @ w1 + b1) @ w2 + b2
        return x + mlp_out

    def _L1_xattn_ref(x, state, ln1_w, ln1_b, ln2_w, ln2_b, maa_x, maa_w1, maa_w2, maa_stack, time_decay, decay_w1, decay_w2, faaaa, Wr, Wk, Wv, Wg, Wo, gn_w, gn_b, ffn_maa_k, ffn_maa_r, ffn_Wk, ffn_Wr, ffn_Wv, i):
        import jax, jax.numpy as jnp
        import numpy as np
        B, L, E, H = (4, 64, 256, 32)
        S = E // H
        EXTRA_MAA, EXTRA_DECAY = (32, 64)
        EPS = 1e-05

        def _ln(x, w, b):
            m = jnp.mean(x, axis=-1, keepdims=True)
            v = jnp.mean((x - m) ** 2, axis=-1, keepdims=True)
            return (x - m) * jax.lax.rsqrt(v + EPS) * w + b

        def _token_shift(xn, prev_row):
            first = (prev_row - xn[:, 0])[:, None]
            rest = xn[:, :-1] - xn[:, 1:]
            return jnp.concatenate([first, rest], axis=1)
        b, l = (x.shape[0], x.shape[1])
        i0 = (2 + S) * i + 0
        i1 = (2 + S) * i + 1
        xn = _ln(x, ln1_w, ln1_b)
        sx = _token_shift(xn, state[:, i1])
        xxx = jnp.tanh((xn + sx * maa_x) @ maa_w1).reshape(b, l, 5, 1, EXTRA_MAA)
        xxx = jnp.matmul(xxx, maa_w2).reshape(b, l, 5, E)
        x5 = xn[:, :, None] + sx[:, :, None] * (maa_stack + xxx)
        w = jnp.exp(-jnp.exp(time_decay + jnp.tanh(x5[:, :, 1] @ decay_w1) @ decay_w2))
        w = w.reshape(b, l, H, S)
        r = (x5[:, :, 3] @ Wr.T).reshape(b, l, H, S)
        k = (x5[:, :, 0] @ Wk.T).reshape(b, l, H, S)
        v = (x5[:, :, 2] @ Wv.T).reshape(b, l, H, S)
        g = jax.nn.silu(x5[:, :, 4] @ Wg.T)
        s0 = state[:, (2 + S) * i + 2:(2 + S) * (i + 1)].reshape(b, H, S, S)
        u = faaaa[None, :, :, None]

        def step(s, rkvw):
            r_t, k_t, v_t, w_t = rkvw
            a = k_t[:, :, :, None] * v_t[:, :, None, :]
            out = jnp.einsum('bhk,bhkd->bhd', r_t, u * a + s)
            return (a + w_t[:, :, :, None] * s, out)
        xs = tuple((jnp.moveaxis(t, 1, 0) for t in (r, k, v, w)))
        _, outs = jax.lax.scan(step, s0, xs)
        att = jnp.moveaxis(outs, 0, 1).reshape(b, l, E)
        a4 = att.reshape(b, l, H, S)
        m = jnp.mean(a4, axis=-1, keepdims=True)
        var = jnp.mean((a4 - m) ** 2, axis=-1, keepdims=True)
        att = ((a4 - m) * jax.lax.rsqrt(var + EPS)).reshape(b, l, E) * gn_w + gn_b
        x = x + att * g @ Wo.T
        xn2 = _ln(x, ln2_w, ln2_b)
        sx2 = _token_shift(xn2, state[:, i0])
        xk = xn2 + sx2 * ffn_maa_k
        xr = xn2 + sx2 * ffn_maa_r
        rr = jax.nn.sigmoid(xr @ ffn_Wr.T)
        kk = jnp.square(jax.nn.relu(xk @ ffn_Wk.T))
        x = x + rr * (kk @ ffn_Wv.T)
        return x
    x = _L0_xattn_ref(x, ctx_2048, mask_1x1xSxS2_fc1, mask_Bx1xSxS2_ff1, L0_xattn_ln1_s, L0_xattn_ln1_b, L0_xattn_w_qkv, L0_xattn_b_qkv, L0_xattn_w_ao, L0_xattn_b_ao, L0_xattn_ln2_s, L0_xattn_ln2_b, L0_xattn_w_q, L0_xattn_b_q, L0_xattn_w_kv, L0_xattn_b_kv, L0_xattn_w_co, L0_xattn_b_co, L0_xattn_ln3_s, L0_xattn_ln3_b, L0_xattn_w1, L0_xattn_b1, L0_xattn_w2, L0_xattn_b2)
    x = _L1_xattn_ref(x, ctx_2048, L1_xattn_ln1_w, L1_xattn_ln1_b, L1_xattn_ln2_w, L1_xattn_ln2_b, L1_xattn_maa_x, L1_xattn_maa_w1, L1_xattn_maa_w2, L1_xattn_maa_stack, L1_xattn_time_decay, L1_xattn_decay_w1, L1_xattn_decay_w2, L1_xattn_faaaa, L1_xattn_Wr, L1_xattn_Wk, L1_xattn_Wv, L1_xattn_Wg, L1_xattn_Wo, L1_xattn_gn_w, L1_xattn_gn_b, L1_xattn_ffn_maa_k, L1_xattn_ffn_maa_r, L1_xattn_ffn_Wk, L1_xattn_ffn_Wr, L1_xattn_ffn_Wv, 0)
    return x

_drawn_inputs = setup_inputs


def setup_inputs(seed=0):
    import zlib

    import numpy as np

    out = dict(_drawn_inputs(seed))
    spreads = {'L0_xattn_ln1_s': (1.0, 0.6),
     'L0_xattn_ln1_b': (0.0, 0.757),
     'L0_xattn_b_qkv': (0.0, 0.269),
     'L0_xattn_b_ao': (0.0, 0.1),
     'L0_xattn_ln2_s': (1.0, 0.6),
     'L0_xattn_ln2_b': (0.0, 2.0),
     'L0_xattn_b_q': (0.0, 2.0),
     'L0_xattn_b_kv': (0.0, 0.28),
     'L0_xattn_b_co': (0.0, 0.1),
     'L0_xattn_ln3_s': (1.0, 0.6),
     'L0_xattn_ln3_b': (0.0, 0.649),
     'L0_xattn_b1': (0.0, 0.1),
     'L0_xattn_b2': (0.0, 0.1),
     'L1_xattn_ln1_w': (1.0, 0.598),
     'L1_xattn_ln1_b': (0.0, 0.562),
     'L1_xattn_ln2_w': (1.0, 0.6),
     'L1_xattn_ln2_b': (0.0, 0.8),
     'L1_xattn_gn_w': (1.0, 0.6),
     'L1_xattn_gn_b': (0.0, 0.8)}
    factors = {'L0_xattn_w_qkv': 4.089,
     'L0_xattn_w_q': 8.0,
     'L1_xattn_maa_x': 8.0,
     'L1_xattn_maa_w1': 7.811,
     'L1_xattn_maa_w2': 7.965,
     'L1_xattn_maa_stack': 8.0,
     'L1_xattn_time_decay': 2.876,
     'L1_xattn_decay_w1': 8.0,
     'L1_xattn_decay_w2': 8.0,
     'L1_xattn_faaaa': 5.906,
     'L1_xattn_ffn_maa_k': 8.0,
     'L1_xattn_ffn_maa_r': 8.0,
     'L1_xattn_ffn_Wk': 2.923,
     'L1_xattn_ffn_Wr': 8.0,
     'L1_xattn_ffn_Wv': 2.725}
    for name, (base, spread) in spreads.items():
        noise = np.random.default_rng([zlib.crc32(name.encode()), seed]).standard_normal(out[name].shape)
        drawn = base * np.exp(spread * noise) if base else spread * noise
        out[name] = jnp.asarray(drawn.astype(out[name].dtype))
    for name, factor in factors.items():
        out[name] = (out[name] * factor).astype(out[name].dtype)
    return out
```

```python
from contextlib import ExitStack

import numpy as np

import concourse.bass as bass
from concourse import mybir

F32 = mybir.dt.float32
I32 = mybir.dt.int32
ALU = mybir.AluOpType
ACT = mybir.ActivationFunctionType
AX_X = mybir.AxisListType.X

B, T, C = 16, 128, 256
P = 128
CT = C // P
NH, HD = 16, 16
RH, RS = 32, 8
F = 4 * C
FT = F // P
MIX, ME = 5, 32
DE = 64
GRP, GH = 4, 4
EPS = 1e-5
GELU_C, GELU_A = 0.7978845608028654, 0.044715

WEIGHTS = [("qkv", CT * 3 * C), ("ao", CT * C), ("q", CT * C), ("kv", CT * 2 * C), ("co", CT * C),
           ("w1", CT * F), ("w2", FT * C), ("maa1", CT * C), ("maa2", MIX * C), ("dec1", CT * DE), ("dec2", C),
           ("r", CT * C), ("k", CT * C), ("v", CT * C), ("g", CT * C),
           ("o", CT * C), ("fk", CT * C), ("fr", CT * C), ("fv", CT * C)]
W_AT, W_END = {}, 0
for _name, _n in WEIGHTS:
    W_AT[_name] = W_END
    W_END += _n
W_CUT1, W_CUT2 = W_AT["w1"], W_AT["o"]

COLS = [("ln1_s", 2), ("ln1_b", 2), ("bq0", 2), ("bk0", 2), ("ln2_s", 2), ("ln2_b", 2), ("bq1", 2), ("bk1", 2),
        ("ln3_s", 2), ("ln3_b", 2), ("b1", 8), ("r1_w", 2), ("r1_b", 2), ("maa_x", 2), ("stack", 10), ("td", 2),
        ("u", 2), ("r2_w", 2), ("r2_b", 2), ("fmk", 2), ("fmr", 2)]
C_AT, C_END = {}, 0
for _name, _n in COLS:
    C_AT[_name] = C_END
    C_END += _n
ROWS = ["bv0", "ao", "bv1", "co", "b2", "gn_w", "gn_b"]
K_ID, K_SEL, K_PAR, K_POW, K_END = 0, P, P + 32, P + 34, P + 35

MIX_TURNS = [(1, 0), (3, 2), (4,)]

SP_ORDER = [
    ("a_load", 0, 0), ("d_store", 0, 2)]
PE_ORDER = [
    ("d_vturn", 0, 2), ("b_turn", 0, 1), ("a_turn", 0, 0), ("b_mlp1", 0, 1), ("a_val", 0, 0), ("a_key", 0, 0),
    ("a_query", 0, 0), ("b_mlp1", 1, 1), ("d_vturn", 1, 2), ("a_scores", (0, 0), 0), ("a_scores", (0, 1), 0),
    ("d_vturn", 2, 2), ("a_scores", (0, 2), 0), ("a_scores", (0, 3), 0), ("d_vturn", 3, 2), ("b_mlp2", 0, 1),
    ("a_enc_turn", 0, 0), ("a_prob_turn", (0, 0), 0), ("a_val", 1, 0), ("b_turn", 1, 1), ("d_own", 0, 2),
    ("a_prob_turn", (0, 1), 0), ("a_prob_turn", (0, 2), 0), ("a_key", 1, 0), ("a_prob_turn", (0, 3), 0), ("b_low1",
    0, 1), ("a_pv", 0, 0), ("b_low2", 0, 1), ("a_out", 0, 0), ("d_read", 0, 2), ("b_low2", 1, 1), ("d_oturn", 0, 2),
    ("a_turn", 1, 0), ("a_query", 1, 0), ("b_low2", 2, 1), ("a_scores", (1, 0), 0), ("b_decay1", 0, 1), ("a_scores",
    (1, 1), 0), ("a_scores", (1, 2), 0), ("d_yturn", 0, 2), ("a_scores", (1, 3), 0), ("d_out", 0, 2), ("b_keyrec",
    0, 1), ("b_decay2", 0, 1), ("a_prob_turn", (1, 0), 0), ("d_turn", 0, 2), ("a_prob_turn", (1, 1), 0),
    ("b_valgate", 0, 1), ("a_prob_turn", (1, 2), 0), ("d_keyrec", 0, 2), ("a_prob_turn", (1, 3), 0), ("a_pv", 1, 0),
    ("d_val", 0, 2), ("a_out", 1, 0)]
DVE_ORDER = [
    ("b_stats", 0, 1), ("a_stats", 0, 0), ("b_normal", 0, 1), ("a_normal", 0, 0), ("a_val", 0, 0), ("b_hidden", 0,
    1), ("d_ruk", 0, 2), ("a_key", 0, 0), ("d_outer", 0, 2), ("b_affine", 0, 1), ("b_hidden", 1, 1), ("d_outer", 1,
    2), ("b_affine", 1, 1), ("a_mask", (0, 0), 0), ("b_gelu", 0, 1), ("d_outer", 2, 2), ("b_gelu", 1, 1), ("a_mask",
    (0, 1), 0), ("a_maxima", (0, 0), 0), ("a_mask", (0, 2), 0), ("d_outer", 3, 2), ("a_maxima", (0, 1), 0),
    ("a_inverse", (0, 0), 0), ("a_mask", (0, 3), 0), ("a_maxima", (0, 2), 0), ("a_inverse", (0, 1), 0), ("b_sum", 0,
    1), ("b_stats", 1, 1), ("a_maxima", (0, 3), 0), ("a_inverse", (0, 2), 0), ("b_normal", 1, 1), ("d_scan", 0, 2),
    ("a_inverse", (0, 3), 0), ("d_own", 0, 2), ("b_shift", 0, 1), ("d_scan", 1, 2), ("d_rstate", 0, 2), ("a_val", 1,
    0), ("a_key", 1, 0), ("b_streams", 0, 1), ("a_sum", 0, 0), ("a_stats", 1, 0), ("a_normal", 1, 0), ("d_centre",
    0, 2), ("b_streams", 1, 1), ("d_deviate", 0, 2), ("b_streams", 2, 1), ("a_mask", (1, 0), 0), ("d_gated", 0, 2),
    ("a_mask", (1, 1), 0), ("a_maxima", (1, 0), 0), ("a_mask", (1, 2), 0), ("a_maxima", (1, 1), 0), ("a_inverse",
    (1, 0), 0), ("a_mask", (1, 3), 0), ("a_maxima", (1, 2), 0), ("d_sum", 0, 2), ("a_inverse", (1, 1), 0),
    ("a_maxima", (1, 3), 0), ("d_normal", 0, 2), ("a_inverse", (1, 2), 0), ("d_shift", 0, 2), ("a_inverse", (1, 3),
    0), ("d_final", 0, 2), ("a_sum", 1, 0), ("b_gate", 0, 1)]
ACT_ORDER = [
    ("b_scale", 0, 1), ("a_scale", 0, 0), ("b_square", 0, 1), ("a_query", 0, 0), ("b_square", 1, 1), ("b_tanhs", 0,
    1), ("b_tanhs", 1, 1), ("a_exps", (0, 0), 0), ("a_exps", (0, 1), 0), ("a_exps", (0, 2), 0), ("a_enc_copy", 0,
    0), ("a_prob_copy", (0, 0), 0), ("a_exps", (0, 3), 0), ("b_scale", 1, 1), ("a_prob_copy", (0, 1), 0),
    ("a_prob_copy", (0, 2), 0), ("a_prob_copy", (0, 3), 0), ("b_low", 0, 1), ("a_ctx_copy", 0, 0), ("d_ocopy", 0,
    2), ("a_scale", 1, 0), ("a_query", 1, 0), ("b_decay1", 0, 1), ("d_ycopy", 0, 2), ("a_exps", (1, 0), 0),
    ("a_exps", (1, 1), 0), ("b_keyrec", 0, 1), ("a_exps", (1, 2), 0), ("b_decay2", 0, 1), ("a_prob_copy", (1, 0),
    0), ("d_scale", 0, 2), ("a_exps", (1, 3), 0), ("a_prob_copy", (1, 1), 0), ("b_decays", 0, 1), ("a_prob_copy",
    (1, 2), 0), ("a_prob_copy", (1, 3), 0), ("d_keyrec", 0, 2), ("a_ctx_copy", 1, 0), ("b_valgate", 0, 1)]
POOL_ORDER = [
    ("b_root", 0, 1), ("a_root", 0, 0), ("a_addbias", 0, 0), ("d_first_states", 0, 2), ("b_addbias", 0, 1),
    ("b_cubes", 0, 1), ("b_cubes", 1, 1), ("a_addmask", (0, 0), 0), ("a_addmask", (0, 1), 0), ("a_addmask", (0, 2),
    0), ("a_divide", (0, 0), 0), ("a_addmask", (0, 3), 0), ("a_divide", (0, 1), 0), ("b_root", 1, 1), ("a_divide",
    (0, 2), 0), ("a_divide", (0, 3), 0), ("d_rstate", 0, 2), ("a_before", 0, 0), ("a_root", 1, 0), ("d_squares", 0,
    2), ("b_addnorm", 0, 1), ("b_addnorm", 1, 1), ("b_addnorm", 2, 1), ("a_addmask", (1, 0), 0), ("a_addmask", (1,
    1), 0), ("a_addmask", (1, 2), 0), ("a_divide", (1, 0), 0), ("a_addmask", (1, 3), 0), ("d_root", 0, 2),
    ("a_divide", (1, 1), 0), ("d_before", 0, 2), ("a_divide", (1, 2), 0), ("a_addbias", 1, 0), ("a_divide", (1, 3),
    0), ("d_relu2", 0, 2)]

LAG = max(lag for order in (SP_ORDER, PE_ORDER, DVE_ORDER, ACT_ORDER, POOL_ORDER) for _, _, lag in order)
PEEL = LAG + 1


def build(nc, x, enc, mask_self, mask_cross, weights, cols, rows, consts, out):
    with ExitStack() as ctx:
        def sb(name, shape):
            return ctx.enter_context(nc.sbuf_tensor(name, [P, *shape], F32))

        def pb(name, shape):
            return ctx.enter_context(nc.psum_tensor(name, [P, *shape], F32))

        X = sb("X", [B, C])
        MASK = sb("MASK", [B + 1, T])
        MADD = sb("MADD", [B + 1, T])
        S0 = sb("S0", [B, CT, RS])
        PREV = sb("PREV", [B, CT, 2])
        W = sb("W", [W_END])
        CRAW = sb("CRAW", [P])
        COL = sb("COL", [C_END])
        ROW = sb("ROW", [len(ROWS), C])
        CST = sb("CST", [K_END])
        QB = sb("QB", [2, 2, CT])
        A_ST, A_MV, A_RS = sb("A_ST", [6]), sb("A_MV", [2]), sb("A_RS", [1])
        A_N = sb("A_N", [C])
        A_LT = sb("A_LT", [CT, T])
        ENC = sb("ENC", [C])
        A_ET = sb("A_ET", [CT, T])
        QP = sb("QP", [2, CT, T])
        KT = sb("KT", [CT, T])
        VP = sb("VP", [NH // 2, 2, 2 * HD])
        SC = sb("SC", [GRP, GH, T])
        NMX, SUM, RINV = sb("NMX", [NH]), sb("SUM", [NH]), sb("RINV", [NH])
        PT = sb("PT", [GRP, GH, T])
        CTX = sb("CTX", [CT, T])
        B_ST, B_MV, B_RS = sb("B_ST", [6]), sb("B_MV", [2]), sb("B_RS", [1])
        B_N = sb("B_N", [C])
        B_LT = sb("B_LT", [CT, T])
        HX, HQ, HG = sb("HX", [FT, T]), sb("HQ", [FT, T]), sb("HG", [FT, T])
        XN, SX, XX = sb("XN", [CT, T + 1]), sb("SX", [CT, T]), sb("XX", [CT, T])
        MT = sb("MT", [CT, T])
        MX = sb("MX", [MIX, CT, T])
        DT, EW = sb("DT", [T]), sb("EW", [CT, T])
        TG = sb("TG", [C])
        W8 = sb("W8", [CT, RS, T])
        KR = sb("KR", [2, CT, T])
        V8 = sb("V8", [CT, RS, P // RS, RS])
        G = sb("G", [C])
        AJ = sb("AJ", [CT, RS, T])
        SS = sb("SS", [CT, RS, T])
        RK = sb("RK", [CT, T])
        O, OQ = sb("O", [C]), sb("OQ", [C])
        OH = sb("OH", [GH, T])
        CV = sb("CV", [C])
        GM, GV, GE = sb("GM", [RH]), sb("GV", [RH]), sb("GE", [RH])
        GY, GT = sb("GY", [RH]), sb("GT", [RH])
        Y = sb("Y", [C])
        YT = sb("YT", [CT, T])
        D_ST, D_MV, D_RS = sb("D_ST", [6]), sb("D_MV", [2]), sb("D_RS", [1])
        D_N = sb("D_N", [C])
        XM, SM, XK, XR = sb("XM", [CT, T + 1]), sb("SM", [CT, T]), sb("XK", [CT, T]), sb("XR", [CT, T])
        RL, KK = sb("RL", [CT, T]), sb("KK", [CT, T])
        RR = sb("RR", [C])

        PS_S = pb("PS_S", [GRP, GH, T])
        PS_T = pb("PS_T", [2, 512])
        PS_B = pb("PS_B", [512])
        PS_D = pb("PS_D", [512])

        def sem(name):
            return ctx.enter_context(nc.semaphore(name))

        in_enc = sem("in_enc")
        a_stat = sem("a_stat")
        a_var = sem("a_var")
        a_rstd = sem("a_rstd")
        a_nrm = sem("a_nrm")
        a_lnps = sem("a_lnps")
        a_ln = sem("a_ln")
        a_bias = sem("a_bias")
        a_encps = sem("a_encps")
        a_enc = sem("a_enc")
        a_prev = sem("a_prev")
        a_vps = sem("a_vps")
        a_kps = sem("a_kps")
        a_qps = sem("a_qps")
        a_v = sem("a_v")
        a_k = sem("a_k")
        a_q = sem("a_q")
        a_score = sem("a_score")
        a_masked = sem("a_masked")
        a_added = sem("a_added")
        a_max = sem("a_max")
        a_exp = sem("a_exp")
        a_inv = sem("a_inv")
        a_prob = sem("a_prob")
        a_turned = sem("a_turned")
        a_pt = sem("a_pt")
        a_pvps = sem("a_pvps")
        a_ctx = sem("a_ctx")
        a_ops = sem("a_ops")
        a_res = sem("a_res")
        b_stat = sem("b_stat")
        b_var = sem("b_var")
        b_rstd = sem("b_rstd")
        b_nrm = sem("b_nrm")
        b_lnps = sem("b_lnps")
        b_ln = sem("b_ln")
        b_bias = sem("b_bias")
        b_up = sem("b_up")
        b_hx = sem("b_hx")
        b_sq = sem("b_sq")
        b_aff = sem("b_aff")
        b_cube = sem("b_cube")
        b_tanh = sem("b_tanh")
        b_hg = sem("b_hg")
        b_dnps = sem("b_dnps")
        b_res = sem("b_res")
        b_first = sem("b_first")
        b_sx = sem("b_sx")
        b_xx = sem("b_xx")
        b_m1ps = sem("b_m1ps")
        b_mt = sem("b_mt")
        b_m2ps = sem("b_m2ps")
        b_mix = sem("b_mix")
        b_mx = sem("b_mx")
        b_d1ps = sem("b_d1ps")
        b_dt = sem("b_dt")
        b_d2ps = sem("b_d2ps")
        b_ew = sem("b_ew")
        b_w8 = sem("b_w8")
        b_krps = sem("b_krps")
        b_kr = sem("b_kr")
        b_vgps = sem("b_vgps")
        b_v = sem("b_v")
        b_tg = sem("b_tg")
        b_g = sem("b_g")
        d_s0 = sem("d_s0")
        d_vps = sem("d_vps")
        d_a = sem("d_a")
        d_s = sem("d_s")
        d_rs = sem("d_rs")
        d_rk = sem("d_rk")
        d_cps = sem("d_cps")
        d_cv = sem("d_cv")
        d_ops = sem("d_ops")
        d_oh = sem("d_oh")
        d_otps = sem("d_otps")
        d_o = sem("d_o")
        d_m = sem("d_m")
        d_cen = sem("d_cen")
        d_sq = sem("d_sq")
        d_v = sem("d_v")
        d_gr = sem("d_gr")
        d_n = sem("d_n")
        d_gw = sem("d_gw")
        d_gb = sem("d_gb")
        d_y = sem("d_y")
        d_yps = sem("d_yps")
        d_yt = sem("d_yt")
        d_wops = sem("d_wops")
        d_res = sem("d_res")
        d_stat = sem("d_stat")
        d_var = sem("d_var")
        d_rstd = sem("d_rstd")
        d_nrm = sem("d_nrm")
        d_lnps = sem("d_lnps")
        d_ln = sem("d_ln")
        d_first = sem("d_first")
        d_sx = sem("d_sx")
        d_xkr = sem("d_xkr")
        d_krps = sem("d_krps")
        d_relu = sem("d_relu")
        d_kk = sem("d_kk")
        d_rr = sem("d_rr")
        d_fps = sem("d_fps")
        d_f = sem("d_f")
        d_fin = sem("d_fin")
        in_first = sem("in_first")
        in_rest = sem("in_rest")
        in_wb = sem("in_wb")
        in_wd = sem("in_wd")
        set_col = sem("set_col")
        set_dve = sem("set_dve")
        set_pool = sem("set_pool")
        passed_dve = sem("passed_dve")
        passed_pool = sem("passed_pool")
        stored = sem("stored")

        IN_FIRST, IN_REST, IN_WB, IN_WD = 16 * 7, 16 * 4, 16, 16

        ident = CST[:, K_ID:K_ID + P]
        hsel = CST[:, K_SEL:K_SEL + P // RS]
        hsel32 = CST[:, K_SEL:K_SEL + 32]

        def bank(g):
            return PS_S[:, g].rearrange("p j n -> p (j n)")[:, 0:C]

        def w(name, kt, n, lo, hi):
            at = W_AT[name] + kt * n
            return W[:, at + lo:at + hi]

        def col(name, k=0, n=1):
            return COL[:, C_AT[name] + k:C_AT[name] + k + n]

        def row(name):
            return ROW[:, ROWS.index(name), :]

        def over_tokens(ap, n, m=T):
            return ap.unsqueeze(2).to_broadcast([P, n, m])

        def over_heads(ap):
            return ap.unsqueeze(1).to_broadcast([P, GH, T])

        def heads(ap):
            return ap.rearrange("p (h d) -> p h d", d=RS)

        def tiles(ap):
            return ap.rearrange("p (t n) -> p t n", t=CT)

        def run(pieces, order, i):
            for name, arg, lag in order:
                if isinstance(i, int) and not 0 <= i - lag < B:
                    continue
                pieces[name](i - lag, arg)

        def later(b, a=0):
            return not (isinstance(b, int) and b == 0 and a == 0)

        def named(*functions):
            return {f.__name__: f for f in functions}

        block = ctx.enter_context(nc.Block())

        @block.sync
        def _(sp):
            sp.dma_start(CST[:, :], consts).then_inc(in_first, 16)
            sp.dma_start(CRAW[0:C_END, :], cols).then_inc(in_first, 16)
            sp.dma_start(X[:, 0, :], x[0]).then_inc(in_first, 16)
            sp.dma_start(W[:, 0:W_AT["ao"]], weights[:, 0:W_AT["ao"]]).then_inc(in_first, 16)
            sp.dma_start(MASK[:, B, :], mask_self).then_inc(in_first, 16)
            sp.dma_start(ROW[:, :, :], rows.unsqueeze(0).to_broadcast([P, len(ROWS), C])).then_inc(in_first, 16)
            sp.dma_start(W[:, W_AT["ao"]:W_CUT1], weights[:, W_AT["ao"]:W_CUT1]).then_inc(in_first, 16)
            sp.dma_start(MASK[:, 0:B, :], mask_cross.rearrange("b q k -> q b k")).then_inc(in_rest, 16)
            sp.dma_start(X[:, 1:B, :], x[1:B].rearrange("b s c -> s b c")).then_inc(in_rest, 16)
            sp.dma_start(W[:, W_CUT1:W_CUT2], weights[:, W_CUT1:W_CUT2]).then_inc(in_wb, 16)
            flat = enc[:, 2:2 + RS, :].rearrange("b s c -> b (s c)")
            with nc.allow_non_contiguous_dma(reason="32-byte pieces of the first states"):
                for t in range(CT):
                    sp.dma_start(S0[:, :, t, :],
                                 flat[:, t * P * RS:(t + 1) * P * RS].rearrange("b (p d) -> p b d", d=RS))\
                      .then_inc(in_rest, 16)
            sp.dma_start(W[:, W_CUT2:W_END], weights[:, W_CUT2:W_END]).then_inc(in_wd, 16)

            def d_store(b, _):
                sp.wait_ge(d_fin, b + 1)
                sp.dma_start(out[b], X[:, b, :]).then_inc(stored, 16)

            def a_load(b, _):
                sp.wait_ge(a_encps, b)
                sp.dma_start(ENC[:, :], enc[b]).then_inc(in_enc, 16)

            pieces = named(a_load, d_store)
            for i in range(PEEL):
                run(pieces, SP_ORDER, i)
            with sp.Fori(PEEL, B) as i:
                run(pieces, SP_ORDER, i)
            for i in range(B, B + LAG):
                run(pieces, SP_ORDER, i)
            sp.wait_ge(stored, 16 * B)

        @block.tensor
        def _(pe):
            pe.wait_ge(in_first, IN_FIRST)
            pe.transpose(PS_D[:, 0:C_END], CRAW[0:C_END, :], CST[0:C_END, K_ID:K_ID + C_END]).then_inc(set_col, 1)

            def turn(dst, src):
                for t in range(CT):
                    last = pe.transpose(dst[:, t * P:(t + 1) * P], src[:, t * P:(t + 1) * P], ident)
                return last

            def to_channels(dst, name, n, lo, rhs, count=CT):
                for m in range(count):
                    for kt in range(CT):
                        last = pe.matmul(dst[:, m * T:(m + 1) * T], w(name, kt, n, lo + m * P, lo + (m + 1) * P),
                                         rhs[:, kt, 0:T], start=(kt == 0), stop=(kt == CT - 1))
                return last

            def to_tokens(dst, name, n, lo, lhs, kts=CT):
                for kt in range(kts):
                    last = pe.matmul(dst, lhs[:, kt, 0:T], w(name, kt, n, lo, lo + C),
                                     start=(kt == 0), stop=(kt == kts - 1))
                return last

            def a_enc_turn(b, _):
                pe.wait_ge(in_enc, 16 * b + 16)
                pe.wait_ge(a_masked, 8 * b + 4)
                turn(bank(3), ENC).then_inc(a_encps, 1)

            def a_turn(b, a):
                pe.wait_ge(a_nrm, 2 * b + a + 1)
                if a:
                    pe.wait_ge(a_enc, b + 1)
                else:
                    pe.wait_ge(a_masked, 8 * b)
                turn(bank(3), A_N).then_inc(a_lnps, 1)

            def a_val(b, a):
                if a:
                    pe.wait_ge(a_enc, b + 1)
                    to_tokens(bank(0), "kv", 2 * C, C, A_ET).then_inc(a_vps, 1)
                else:
                    pe.wait_ge(a_ln, 2 * b + 1)
                    to_tokens(bank(0), "qkv", 3 * C, 2 * C, A_LT).then_inc(a_vps, 1)

            def a_key(b, a):
                if a:
                    pe.wait_ge(a_enc, b + 1)
                    to_channels(bank(1), "kv", 2 * C, 0, A_ET).then_inc(a_kps, 1)
                else:
                    pe.wait_ge(a_ln, 2 * b + 1)
                    to_channels(bank(1), "qkv", 3 * C, C, A_LT).then_inc(a_kps, 1)

            def a_query(b, a):
                pe.wait_ge(a_ln, 2 * b + a + 1)
                if a:
                    to_channels(bank(2), "q", C, 0, A_LT).then_inc(a_qps, 1)
                else:
                    to_channels(bank(2), "qkv", 3 * C, 0, A_LT).then_inc(a_qps, 1)

            def a_scores(b, arg):
                a, g = arg
                if g == 0:
                    pe.wait_ge(a_v, 2 * b + a + 1)
                    pe.wait_ge(a_k, 2 * b + a + 1)
                    pe.wait_ge(a_q, 2 * b + a + 1)
                for t in range(CT):
                    for par in range(2):
                        last = pe.matmul(PS_S[:, g, 2 * t + par, :], QP[32 * g:32 * g + 32, par, t, :],
                                         KT[32 * g:32 * g + 32, t, :], start=True, stop=True)
                last.then_inc(a_score, 1)

            def a_prob_turn(b, arg):
                a, g = arg
                pe.wait_ge(a_prob, 8 * b + 4 * a + g + 1)
                if g == 0:
                    pe.wait_ge(a_ctx, 2 * b + a)
                elif g == 1:
                    pe.wait_ge(a_res, 2 * b + a)
                else:
                    pe.wait_ge(a_pt, 8 * b + 4 * a + g - 1)
                for j in range(GH):
                    last = pe.transpose(PS_T[:, g % 2, j * T:(j + 1) * T], SC[:, g, j, :], ident)
                last.then_inc(a_turned, 1)

            def a_pv(b, a):
                pe.wait_ge(a_pt, 8 * b + 4 * a + 4)
                for t in range(CT):
                    for par in range(2):
                        for g in range(GRP):
                            last = pe.matmul(PS_T[32 * g:32 * g + 32, 0, t * T:(t + 1) * T],
                                             VP[:, GRP * t + g, par, :], PT[:, g, 2 * t + par, :],
                                             start=(par == 0), stop=(par == 1), skip_group_check=True)
                last.then_inc(a_pvps, 1)

            def a_out(b, a):
                pe.wait_ge(a_ctx, 2 * b + a + 1)
                to_tokens(PS_T[:, 1, 0:C], "co" if a else "ao", C, 0, CTX).then_inc(a_ops, 1)

            def b_turn(b, k):
                pe.wait_ge(b_nrm, 2 * b + k + 1)
                if k == 0:
                    pe.wait_ge(b_g, b)
                    pe.wait_ge(b_v, b)
                turn(PS_B[:, 0:C], B_N).then_inc(b_lnps, 1)

            def b_mlp1(b, k):
                if k == 0:
                    pe.wait_ge(b_ln, 2 * b + 1)
                else:
                    pe.wait_ge(b_hx, 2 * b + 1)
                to_channels(PS_B[:, :], "w1", F, k * (F // 2), B_LT, FT // 2).then_inc(b_up, 1)

            def b_mlp2(b, _):
                pe.wait_ge(b_hg, 2 * b + 2)
                to_tokens(PS_B[:, 0:C], "w2", C, 0, HG, FT).then_inc(b_dnps, 1)

            def b_low1(b, _):
                pe.wait_ge(b_xx, b + 1)
                to_channels(PS_B[:, 0:C], "maa1", C, 0, XX).then_inc(b_m1ps, 1)

            def b_low2(b, n):
                if n == 0:
                    pe.wait_ge(b_mt, b + 1)
                else:
                    pe.wait_ge(b_mix, 3 * b + n)
                for k, i in enumerate(MIX_TURNS[n]):
                    for m in range(CT):
                        last = pe.matmul(PS_B[:, k * C + m * T:k * C + (m + 1) * T],
                                         w("maa2", i, C, m * P, (m + 1) * P), MT[:, i * ME // P, :],
                                         start=True, stop=True)
                last.then_inc(b_m2ps, 1)

            def b_decay1(b, _):
                pe.wait_ge(b_mx, 3 * b + 1)
                pe.wait_ge(b_mix, 3 * b + 3)
                for kt in range(CT):
                    last = pe.matmul(PS_B[0:DE, 0:T], w("dec1", kt, DE, 0, DE), MX[:, 1, kt, :],
                                     start=(kt == 0), stop=(kt == CT - 1))
                last.then_inc(b_d1ps, 1)

            def b_keyrec(b, _):
                pe.wait_ge(b_mx, 3 * b + 2)
                pe.wait_ge(b_dt, b + 1)
                to_channels(PS_B[:, 0:C], "k", C, 0, MX[:, 0])
                to_channels(PS_B[:, C:2 * C], "r", C, 0, MX[:, 3]).then_inc(b_krps, 1)

            def b_decay2(b, _):
                pe.wait_ge(b_kr, b + 1)
                for m in range(CT):
                    last = pe.matmul(PS_B[:, m * T:(m + 1) * T], w("dec2", 0, C, m * P, (m + 1) * P)[0:DE],
                                     DT[0:DE, :], start=True, stop=True)
                last.then_inc(b_d2ps, 1)

            def b_valgate(b, _):
                pe.wait_ge(b_mx, 3 * b + 3)
                pe.wait_ge(b_ew, b + 1)
                to_tokens(PS_B[:, 0:C], "v", C, 0, MX[:, 2])
                to_tokens(PS_B[:, C:2 * C], "g", C, 0, MX[:, 4]).then_inc(b_vgps, 1)

            def d_vturn(b, n):
                t, half = n // 2, n % 2
                if n == 0:
                    pe.wait_ge(b_v, b + 1)
                    pe.wait_ge(d_f, b)
                else:
                    pe.wait_ge(d_a, 4 * b + n)
                for j in range(4):
                    last = pe.transpose(PS_D[:, j * T:(j + 1) * T],
                                        V8[:, t, 4 * half + j].rearrange("p h k -> p (h k)"), ident)
                last.then_inc(d_vps, 1)

            def d_own(b, _):
                pe.wait_ge(d_rk, b + 1)
                pe.wait_ge(d_a, 4 * b + 4)
                for t in range(CT):
                    last = pe.matmul(PS_D[:, t * (P // RS):(t + 1) * (P // RS)], RK[:, t, :], hsel,
                                     start=True, stop=True)
                last.then_inc(d_cps, 1)

            def d_read(b, _):
                pe.wait_ge(d_cv, b + 1)
                pe.wait_ge(d_rs, 2 * b + 2)
                for t in range(CT):
                    for half in range(2):
                        at = 32 * (2 * t + half)
                        last = pe.matmul(PS_D[at:at + 32, :], hsel32,
                                         SS[:, t, 4 * half:4 * half + 4, :].rearrange("p d n -> p (d n)"),
                                         start=True, stop=True, skip_group_check=True)
                last.then_inc(d_ops, 1)

            def d_oturn(b, _):
                pe.wait_ge(d_oh, b + 1)
                for j in range(4):
                    last = pe.transpose(PS_D[:, j * T:(j + 1) * T], OH[:, j, :], ident)
                last.then_inc(d_otps, 1)

            def d_yturn(b, _):
                pe.wait_ge(d_y, b + 1)
                turn(PS_D[:, 0:C], Y).then_inc(d_yps, 1)

            def d_out(b, _):
                pe.wait_ge(d_yt, b + 1)
                to_tokens(PS_D[:, 0:C], "o", C, 0, YT).then_inc(d_wops, 1)

            def d_turn(b, _):
                pe.wait_ge(d_nrm, b + 1)
                turn(PS_D[:, 0:C], D_N).then_inc(d_lnps, 1)

            def d_keyrec(b, _):
                pe.wait_ge(d_xkr, b + 1)
                to_channels(PS_D[:, 0:C], "fk", C, 0, XK)
                to_tokens(PS_D[:, C:2 * C], "fr", C, 0, XR).then_inc(d_krps, 1)

            def d_val(b, _):
                pe.wait_ge(d_kk, b + 1)
                pe.wait_ge(d_rr, b + 1)
                to_tokens(PS_D[:, 0:C], "fv", C, 0, KK).then_inc(d_fps, 1)

            pieces = named(a_enc_turn, a_turn, a_val, a_key, a_query, a_scores, a_prob_turn, a_pv, a_out,
                           b_turn, b_mlp1, b_mlp2, b_low1, b_low2, b_decay1, b_keyrec, b_decay2, b_valgate,
                           d_vturn, d_own, d_read, d_oturn, d_yturn, d_out, d_turn, d_keyrec, d_val)
            run(pieces, PE_ORDER, 0)
            pe.wait_ge(in_wb, IN_WB)
            pe.wait_ge(in_rest, IN_REST)
            run(pieces, PE_ORDER, 1)
            pe.wait_ge(in_wd, IN_WD)
            for i in range(2, PEEL):
                run(pieces, PE_ORDER, i)
            with pe.Fori(PEEL, B) as i:
                run(pieces, PE_ORDER, i)
            for i in range(B, B + LAG):
                run(pieces, PE_ORDER, i)

        @block.vector
        def _(dve):
            dve.memset(VP[:, :, :, :], 0.0)
            dve.memset(W8[:, :, :, 0:1], 0.0).then_inc(set_dve, 1)
            dve.wait_ge(set_col, 1)
            dve.tensor_copy(COL[:, :], PS_D[:, 0:C_END]).then_inc(set_dve, 1)
            dve.wait_ge(in_first, IN_FIRST)
            dve.wait_ge(set_dve, 2)
            for a in range(2):
                for par in range(2):
                    last = dve.tensor_scalar(QB[:, a, par, :], col(f"bq{a}", 0, 2), CST[:, K_PAR + par:K_PAR + par + 1],
                                             None, ALU.mult)
            last.then_inc(set_dve, 1)

            def row_stats(b, n, stat, var, ST, MV):
                dve.sem_inc(passed_dve, 1)
                dve.bn_stats(ST[:, :], X[:, b, :]).then_inc(stat, 1)
                dve.wait_ge(stat, 2 * n + 1)
                dve.sem_inc(passed_dve, 1)
                dve.bn_aggr(MV[:, :], ST[:, :]).then_inc(stat, 1)
                dve.wait_ge(stat, 2 * n + 2)
                dve.tensor_scalar(ST[:, 0:1], MV[:, 1:2], EPS, None, ALU.add).then_inc(var, 1)

            def normalise(b, MV, RS_, N):
                return dve.tensor_scalar(N[:, :], X[:, b, :], MV[:, 0:1], RS_[:, 0:1], ALU.subtract, ALU.mult)

            def a_stats(b, a):
                if a:
                    dve.wait_ge(a_res, 2 * b + 1)
                row_stats(b, 2 * b + a, a_stat, a_var, A_ST, A_MV)

            def a_normal(b, a):
                dve.wait_ge(a_rstd, 2 * b + a + 1)
                dve.wait_ge(a_lnps, 2 * b + a)
                normalise(b, A_MV, A_RS, A_N).then_inc(a_nrm, 1)

            def a_val(b, a):
                dve.wait_ge(a_vps, 2 * b + a + 1)
                dve.wait_ge(a_pvps, 2 * b + a)
                v = bank(0).rearrange("p (h q d) -> p h q d", q=2, d=HD)
                bias = row(f"bv{a}").rearrange("p (h q d) -> p h q d", q=2, d=HD)
                for q in range(2):
                    last = dve.tensor_tensor(VP[:, :, q, q * HD:(q + 1) * HD], v[:, :, q, :], bias[:, :, q, :],
                                             ALU.add)
                last.then_inc(a_v, 1)

            def a_key(b, a):
                dve.wait_ge(a_kps, 2 * b + a + 1)
                dve.tensor_tensor(KT[:, :, :], tiles(bank(1)), over_tokens(col(f"bk{a}", 0, 2), CT), ALU.add)\
                    .then_inc(a_k, 1)

            def a_mask(b, arg):
                a, g = arg
                dve.wait_ge(a_score, 8 * b + 4 * a + g + 1)
                if later(b, a):
                    dve.wait_ge(a_turned, 8 * b + 4 * a + g - 3)
                if not later(b) and a and g == 0:
                    dve.wait_ge(in_rest, IN_REST)
                mask = MASK[:, b, :] if a else MASK[:, B, :]
                dve.tensor_tensor(SC[:, g], PS_S[:, g], over_heads(mask), ALU.mult).then_inc(a_masked, 1)

            def a_maxima(b, arg):
                a, g = arg
                dve.wait_ge(a_added, 8 * b + 4 * a + g + 1)
                dve.tensor_reduce(NMX[:, GH * g:GH * g + GH], SC[:, g], AX_X, ALU.max, negate=True)\
                    .then_inc(a_max, 1)

            def a_inverse(b, arg):
                a, g = arg
                dve.wait_ge(a_exp, 8 * b + 4 * a + g + 1)
                dve.reciprocal(RINV[:, GH * g:GH * g + GH], SUM[:, GH * g:GH * g + GH]).then_inc(a_inv, 1)

            def a_sum(b, a):
                dve.wait_ge(a_ops, 2 * b + a + 1)
                dve.wait_ge(a_bias, 2 * b + a + 1)
                dve.tensor_tensor(X[:, b, :], PS_T[:, 1, 0:C], X[:, b, :], ALU.add).then_inc(a_res, 1)

            def b_stats(b, k):
                if k:
                    dve.wait_ge(b_res, b + 1)
                else:
                    dve.wait_ge(a_res, 2 * b + 2)
                row_stats(b, 2 * b + k, b_stat, b_var, B_ST, B_MV)

            def b_normal(b, k):
                dve.wait_ge(b_rstd, 2 * b + k + 1)
                normalise(b, B_MV, B_RS, B_N).then_inc(b_nrm, 1)

            def b_hidden(b, k):
                dve.wait_ge(b_up, 2 * b + k + 1)
                h = HX[:, k * FT // 2:(k + 1) * FT // 2, :]
                dve.tensor_tensor(h, PS_B[:, :].rearrange("p (m n) -> p m n", n=T),
                                  over_tokens(col("b1", k * FT // 2, FT // 2), FT // 2), ALU.add).then_inc(b_hx, 1)

            def b_affine(b, k):
                h = slice(k * FT // 2, (k + 1) * FT // 2)
                dve.wait_ge(b_sq, 2 * b + k + 1)
                dve.tensor_scalar(HQ[:, h, :], HQ[:, h, :], GELU_A * GELU_C, GELU_C, ALU.mult, ALU.add)\
                    .then_inc(b_aff, 1)

            def b_gelu(b, k):
                h = slice(k * FT // 2, (k + 1) * FT // 2)
                dve.wait_ge(b_tanh, 2 * b + k + 1)
                dve.scalar_tensor_tensor(HG[:, h, :], HQ[:, h, :], 1.0, HX[:, h, :], ALU.add, ALU.mult)\
                    .then_inc(b_hg, 1)

            def b_sum(b, _):
                dve.wait_ge(b_dnps, b + 1)
                dve.wait_ge(b_bias, b + 1)
                dve.tensor_tensor(X[:, b, :], PS_B[:, 0:C], X[:, b, :], ALU.add).then_inc(b_res, 1)

            def b_shift(b, _):
                dve.wait_ge(b_first, b + 1)
                dve.wait_ge(b_ln, 2 * b + 2)
                dve.tensor_tensor(SX[:, :, :], XN[:, :, 0:T], XN[:, :, 1:T + 1], ALU.subtract).then_inc(b_sx, 1)
                dve.wait_ge(b_sx, b + 1)
                for t in range(CT):
                    last = dve.scalar_tensor_tensor(XX[:, t, :], SX[:, t, :], col("maa_x", t), XN[:, t, 1:T + 1],
                                                    ALU.mult, ALU.add)
                last.then_inc(b_xx, 1)

            def b_streams(b, n):
                dve.wait_ge(b_m2ps, 3 * b + n + 1)
                for k, i in enumerate(MIX_TURNS[n]):
                    for t in range(CT):
                        at = k * C + t * T
                        last = dve.scalar_tensor_tensor(MX[:, i, t, :], PS_B[:, at:at + T], col("stack", 2 * i + t),
                                                        SX[:, t, :], ALU.add, ALU.mult)
                last.then_inc(b_mix, 1)

            def b_gate(b, _):
                dve.wait_ge(b_tg, b + 1)
                dve.wait_ge(d_y, b)
                dve.scalar_tensor_tensor(G[:, :], TG[:, :], 1.0, PS_B[:, C:2 * C], ALU.add, ALU.mult)\
                    .then_inc(b_g, 1)

            def d_outer(b, n):
                t, half = n // 2, n % 2
                dve.wait_ge(d_vps, 4 * b + n + 1)
                if n == 0:
                    dve.wait_ge(b_kr, b + 1)
                v = PS_D[:, :].rearrange("p (d n) -> p d n", n=T)
                k = KR[:, 0, t, 0:T - 1].unsqueeze(1).to_broadcast([P, 4, T - 1])
                dve.tensor_tensor(AJ[:, t, 4 * half:4 * half + 4, 1:T], v[:, :, 0:T - 1], k, ALU.mult)\
                    .then_inc(d_a, 1)

            def d_scan(b, t):
                if t == 0:
                    dve.wait_ge(d_s0, b + 1)
                    dve.wait_ge(b_w8, b + 1)
                dve.wait_ge(d_a, 4 * b + 2 * t + 2)
                dve.tensor_tensor_scan(SS[:, t].rearrange("p d n -> p (d n)"), W8[:, t].rearrange("p d n -> p (d n)"),
                                       AJ[:, t].rearrange("p d n -> p (d n)"), 0.0, ALU.mult, ALU.add)\
                    .then_inc(d_s, 1)

            def d_ruk(b, _):
                dve.wait_ge(b_kr, b + 1)
                for k in range(CT):
                    last = dve.scalar_tensor_tensor(RK[:, k, :], KR[:, 1, k, :], col("u", k), KR[:, 0, k, :],
                                                    ALU.mult, ALU.mult)
                last.then_inc(d_rk, 1)

            def d_rstate(b, _):
                dve.wait_ge(d_s, 2 * b + 1)
                r = KR[:, 1, 0, :].unsqueeze(1).to_broadcast([P, RS, T])
                dve.tensor_tensor(SS[:, 0], SS[:, 0], r, ALU.mult).then_inc(d_rs, 1)

            def d_own(b, _):
                dve.wait_ge(d_cps, b + 1)
                n = P // RS
                for t in range(CT):
                    last = dve.tensor_tensor(heads(CV[:, t * P:(t + 1) * P]),
                                             V8[:, t, :, :, 0].rearrange("p d h -> p h d"),
                                             over_tokens(PS_D[:, t * n:(t + 1) * n], n, RS), ALU.mult)
                last.then_inc(d_cv, 1)

            def d_centre(b, _):
                dve.wait_ge(d_otps, b + 1)
                o = PS_D[:, :].rearrange("p (j t e h) -> p t h e j", j=4, t=CT, e=2)
                for t in range(CT):
                    last = dve.tensor_tensor(O[:, t * P:(t + 1) * P].rearrange("p (h e j) -> p h e j", e=2, j=4),
                                             o[:, t, 0:P // RS],
                                             CV[:, t * P:(t + 1) * P].rearrange("p (h e j) -> p h e j", e=2, j=4),
                                             ALU.add)
                last.then_inc(d_o, 1)
                dve.wait_ge(d_o, b + 1)
                dve.tensor_reduce(GM[:, :], heads(O[:, :]), AX_X, ALU.add).then_inc(d_m, 1)
                dve.wait_ge(d_m, b + 1)
                dve.scalar_tensor_tensor(heads(O[:, :]), over_tokens(GM[:, :], RH, RS), -1.0 / RS, heads(O[:, :]),
                                         ALU.mult, ALU.add).then_inc(d_cen, 1)

            def d_deviate(b, _):
                dve.wait_ge(d_sq, b + 1)
                dve.tensor_reduce(GV[:, :], heads(OQ[:, :]), AX_X, ALU.add).then_inc(d_v, 1)
                dve.wait_ge(d_v, b + 1)
                dve.tensor_scalar(GE[:, :], GV[:, :], 1.0 / RS, EPS, ALU.mult, ALU.add).then_inc(d_gr, 1)
                dve.wait_ge(d_gr, 12 * b + 1)
                dve.tensor_scalar(GT[:, :].bitcast(I32), GE[:, :].bitcast(I32), 1, None, ALU.logical_shift_right)\
                    .then_inc(d_gr, 1)
                dve.wait_ge(d_gr, 12 * b + 2)
                dve.tensor_scalar(GY[:, :].bitcast(I32), GT[:, :].bitcast(I32), -1.0, float(0x5F3759DF),
                                  ALU.mult, ALU.add).then_inc(d_gr, 1)
                for n in range(3):
                    dve.wait_ge(d_gr, 12 * b + 3 * n + 3)
                    dve.scalar_tensor_tensor(GT[:, :], GY[:, :], -0.5, GE[:, :], ALU.mult, ALU.mult)\
                        .then_inc(d_gr, 1)
                    dve.wait_ge(d_gr, 12 * b + 3 * n + 4)
                    dve.tensor_tensor(GT[:, :], GT[:, :], GY[:, :], ALU.mult).then_inc(d_gr, 1)
                    dve.wait_ge(d_gr, 12 * b + 3 * n + 5)
                    dve.scalar_tensor_tensor(GY[:, :], GT[:, :], 1.5, GY[:, :], ALU.add, ALU.mult)\
                        .then_inc(d_gr, 1)

            def d_gated(b, _):
                dve.wait_ge(d_gr, 12 * b + 12)
                dve.tensor_tensor(heads(O[:, :]), heads(O[:, :]), over_tokens(GY[:, :], RH, RS), ALU.mult)\
                    .then_inc(d_n, 1)
                dve.wait_ge(d_n, b + 1)
                dve.tensor_tensor(O[:, :], O[:, :], row("gn_w"), ALU.mult).then_inc(d_gw, 1)
                dve.wait_ge(d_gw, b + 1)
                dve.tensor_tensor(O[:, :], O[:, :], row("gn_b"), ALU.add).then_inc(d_gb, 1)
                dve.wait_ge(d_gb, b + 1)
                dve.wait_ge(b_g, b + 1)
                dve.scalar_tensor_tensor(Y[:, :], O[:, :], 0.5, G[:, :], ALU.mult, ALU.mult).then_inc(d_y, 1)

            def d_sum(b, _):
                dve.wait_ge(d_wops, b + 1)
                dve.tensor_tensor(X[:, b, :], PS_D[:, 0:C], X[:, b, :], ALU.add).then_inc(d_res, 1)
                dve.wait_ge(d_res, b + 1)
                row_stats(b, b, d_stat, d_var, D_ST, D_MV)

            def d_normal(b, _):
                dve.wait_ge(d_rstd, b + 1)
                normalise(b, D_MV, D_RS, D_N).then_inc(d_nrm, 1)

            def d_shift(b, _):
                dve.wait_ge(d_first, b + 1)
                dve.wait_ge(d_ln, b + 1)
                dve.tensor_tensor(SM[:, :, :], XM[:, :, 0:T], XM[:, :, 1:T + 1], ALU.subtract).then_inc(d_sx, 1)
                dve.wait_ge(d_sx, b + 1)
                for dst, name in ((XK, "fmk"), (XR, "fmr")):
                    for t in range(CT):
                        last = dve.scalar_tensor_tensor(dst[:, t, :], SM[:, t, :], col(name, t), XM[:, t, 1:T + 1],
                                                        ALU.mult, ALU.add)
                last.then_inc(d_xkr, 1)

            def d_final(b, _):
                dve.wait_ge(d_rr, b + 1)
                dve.wait_ge(d_fps, b + 1)
                dve.scalar_tensor_tensor(RR[:, :], RR[:, :], 1.0, PS_D[:, 0:C], ALU.add, ALU.mult).then_inc(d_f, 1)
                dve.wait_ge(d_f, b + 1)
                dve.scalar_tensor_tensor(X[:, b, :], RR[:, :], 0.5, X[:, b, :], ALU.mult, ALU.add)\
                    .then_inc(d_fin, 1)

            pieces = named(a_stats, a_normal, a_val, a_key, a_mask, a_maxima, a_inverse, a_sum,
                           b_stats, b_normal, b_hidden, b_affine, b_gelu, b_sum, b_shift, b_streams, b_gate,
                           d_outer, d_scan, d_ruk, d_rstate, d_own, d_centre, d_deviate, d_gated, d_sum, d_normal,
                           d_shift, d_final)
            run(pieces, DVE_ORDER, 0)
            dve.wait_ge(in_rest, IN_REST)
            for i in range(1, PEEL):
                run(pieces, DVE_ORDER, i)
            with dve.Fori(PEEL, B) as i:
                run(pieces, DVE_ORDER, i)
            for i in range(B, B + LAG):
                run(pieces, DVE_ORDER, i)

        @block.scalar
        def _(act):
            act.wait_ge(in_first, IN_FIRST)
            act.wait_ge(set_dve, 3)

            def turned(dst, src, s, bias):
                for t in range(CT):
                    last = act.activation(dst[:, t, :], src[:, t * T:(t + 1) * T], ACT.Identity,
                                          bias=col(bias, t), scale=col(s, t))
                return last

            def a_enc_copy(b, _):
                act.wait_ge(a_encps, b + 1)
                act.wait_ge(a_prev, b)
                act.activation(A_ET[:, :, :], tiles(bank(3)), ACT.Copy).then_inc(a_enc, 1)

            def a_scale(b, a):
                act.wait_ge(a_lnps, 2 * b + a + 1)
                turned(A_LT, bank(3), f"ln{a + 1}_s", f"ln{a + 1}_b").then_inc(a_ln, 1)

            def a_query(b, a):
                act.wait_ge(a_qps, 2 * b + a + 1)
                for par in range(2):
                    for t in range(CT):
                        last = act.activation(QP[:, par, t, :], bank(2)[:, t * T:(t + 1) * T], ACT.Identity,
                                              bias=QB[:, a, par, t:t + 1], scale=CST[:, K_PAR + par:K_PAR + par + 1])
                last.then_inc(a_q, 1)

            def a_exps(b, arg):
                a, g = arg
                act.wait_ge(a_max, 8 * b + 4 * a + g + 1)
                for j in range(GH):
                    h = GH * g + j
                    last = act.activation(SC[:, g, j, :], SC[:, g, j, :], ACT.Exp, bias=NMX[:, h:h + 1],
                                          accum_out=SUM[:, h:h + 1])
                last.then_inc(a_exp, 1)

            def a_prob_copy(b, arg):
                a, g = arg
                act.wait_ge(a_turned, 8 * b + 4 * a + g + 1)
                act.activation(PT[:, g], PS_T[:, g % 2].rearrange("p (j n) -> p j n", n=T), ACT.Copy)\
                    .then_inc(a_pt, 1)

            def a_ctx_copy(b, a):
                act.wait_ge(a_pvps, 2 * b + a + 1)
                act.activation(CTX[:, :, :], tiles(PS_T[:, 0, 0:C]), ACT.Copy).then_inc(a_ctx, 1)

            def b_scale(b, k):
                act.wait_ge(b_lnps, 2 * b + k + 1)
                if k:
                    turned(XN[:, :, 1:T + 1], PS_B, "r1_w", "r1_b").then_inc(b_ln, 1)
                else:
                    turned(B_LT, PS_B, "ln3_s", "ln3_b").then_inc(b_ln, 1)

            def b_square(b, k):
                h = slice(k * FT // 2, (k + 1) * FT // 2)
                act.wait_ge(b_hx, 2 * b + k + 1)
                act.activation(HQ[:, h, :], HX[:, h, :], ACT.Square).then_inc(b_sq, 1)

            def b_tanhs(b, k):
                h = slice(k * FT // 2, (k + 1) * FT // 2)
                act.wait_ge(b_cube, 2 * b + k + 1)
                act.activation(HQ[:, h, :], HQ[:, h, :], ACT.Tanh).then_inc(b_tanh, 1)

            def b_low(b, _):
                act.wait_ge(b_m1ps, b + 1)
                act.activation(MT[:, :, :], tiles(PS_B[:, 0:C]), ACT.Tanh).then_inc(b_mt, 1)

            def b_decay1(b, _):
                act.wait_ge(b_d1ps, b + 1)
                act.activation(DT[0:DE, :], PS_B[0:DE, 0:T], ACT.Tanh).then_inc(b_dt, 1)

            def b_keyrec(b, _):
                act.wait_ge(b_krps, b + 1)
                act.wait_ge(d_rs, 2 * b)
                act.wait_ge(d_rk, b)
                act.activation(KR[:, :, :, :].rearrange("p a t n -> p (a t n)"), PS_B[:, :], ACT.Copy)\
                    .then_inc(b_kr, 1)

            def b_decay2(b, _):
                act.wait_ge(b_d2ps, b + 1)
                for t in range(CT):
                    last = act.activation(EW[:, t, :], PS_B[:, t * T:(t + 1) * T], ACT.Exp, bias=col("td", t))
                last.then_inc(b_ew, 1)

            def b_decays(b, _):
                act.wait_ge(b_ew, b + 1)
                act.wait_ge(d_s, 2 * b)
                for t in range(CT):
                    e = EW[:, t, 0:T - 1].unsqueeze(1).to_broadcast([P, RS, T - 1])
                    last = act.activation(W8[:, t, :, 1:T], e, ACT.Exp, scale=-1.0)
                last.then_inc(b_w8, 1)

            def b_valgate(b, _):
                act.wait_ge(b_vgps, b + 1)
                act.wait_ge(d_cv, b)
                for t in range(CT):
                    v = heads(PS_B[:, t * P:(t + 1) * P]).rearrange("p h d -> p d h").unsqueeze(3)
                    last = act.activation(V8[:, t], v.to_broadcast([P, RS, P // RS, RS]), ACT.Copy)
                last.then_inc(b_v, 1)
                act.activation(TG[:, :], PS_B[:, C:2 * C], ACT.Tanh, scale=0.5).then_inc(b_tg, 1)

            def d_ocopy(b, _):
                act.wait_ge(d_ops, b + 1)
                act.activation(OH[:, :, :].rearrange("p j n -> p (j n)"), PS_D[:, :], ACT.Copy).then_inc(d_oh, 1)

            def d_ycopy(b, _):
                act.wait_ge(d_yps, b + 1)
                act.activation(YT[:, :, :], tiles(PS_D[:, 0:C]), ACT.Copy).then_inc(d_yt, 1)

            def d_scale(b, _):
                act.wait_ge(d_lnps, b + 1)
                turned(XM[:, :, 1:T + 1], PS_D[:, 0:C], "r2_w", "r2_b").then_inc(d_ln, 1)

            def d_keyrec(b, _):
                act.wait_ge(d_krps, b + 1)
                act.activation(RL[:, :, :], tiles(PS_D[:, 0:C]), ACT.Relu).then_inc(d_relu, 1)
                act.activation(RR[:, :], PS_D[:, C:2 * C], ACT.Tanh, scale=0.5).then_inc(d_rr, 1)

            pieces = named(a_enc_copy, a_scale, a_query, a_exps, a_prob_copy, a_ctx_copy,
                           b_scale, b_square, b_tanhs, b_low, b_decay1, b_keyrec, b_decay2, b_decays, b_valgate,
                           d_ocopy, d_ycopy, d_scale, d_keyrec)
            for i in range(PEEL):
                run(pieces, ACT_ORDER, i)
            with act.Fori(PEEL, B) as i:
                run(pieces, ACT_ORDER, i)
            for i in range(B, B + LAG):
                run(pieces, ACT_ORDER, i)

        @block.gpsimd
        def _(pool):
            pool.wait_ge(in_first, IN_FIRST)
            pool.tensor_scalar(MADD[:, B, :], MASK[:, B, :], -1.0, 1.0, ALU.mult, ALU.add).then_inc(set_pool, 1)
            pool.wait_ge(set_pool, 1)
            pool.tensor_scalar(MADD[:, B, :], MADD[:, B, :], -10000.0, 0.0, ALU.mult, ALU.add)\
                .then_inc(set_pool, 1)

            def inverse_root(ST, RS_):
                return pool.tensor_tensor(RS_[:, 0:1], ST[:, 0:1], CST[:, K_POW:K_POW + 1], ALU.pow)

            def a_root(b, a):
                pool.wait_ge(a_var, 2 * b + a + 1)
                inverse_root(A_ST, A_RS).then_inc(a_rstd, 1)

            def a_addbias(b, a):
                pool.wait_ge(a_nrm, 2 * b + a + 1)
                pool.sem_inc(passed_pool, 1)
                pool.tensor_tensor(X[:, b, :], X[:, b, :], row("co" if a else "ao"), ALU.add).then_inc(a_bias, 1)

            def a_before(b, _):
                pool.wait_ge(a_enc, b + 1)
                pool.tensor_copy(PREV[:, b, :, :], A_ET[:, :, 0:2]).then_inc(a_prev, 1)

            def a_addmask(b, arg):
                a, g = arg
                if not later(b) and a and g == 0:
                    pool.wait_ge(in_rest, IN_REST)
                    pool.tensor_scalar(MADD[:, 0:B, :], MASK[:, 0:B, :], -1.0, 1.0, ALU.mult, ALU.add)\
                        .then_inc(set_pool, 1)
                    pool.wait_ge(set_pool, 3)
                    pool.tensor_scalar(MADD[:, 0:B, :], MADD[:, 0:B, :], -10000.0, 0.0, ALU.mult, ALU.add)\
                        .then_inc(set_pool, 1)
                    pool.wait_ge(set_pool, 4)
                pool.wait_ge(a_masked, 8 * b + 4 * a + g + 1)
                if a:
                    pool.sem_inc(passed_pool, 1)
                    pool.tensor_tensor(SC[:, g], SC[:, g], over_heads(MADD[:, b, :]), ALU.add).then_inc(a_added, 1)
                else:
                    pool.tensor_tensor(SC[:, g], SC[:, g], over_heads(MADD[:, B, :]), ALU.add).then_inc(a_added, 1)

            def a_divide(b, arg):
                a, g = arg
                pool.wait_ge(a_inv, 8 * b + 4 * a + g + 1)
                pool.tensor_tensor(SC[:, g], SC[:, g], over_tokens(RINV[:, GH * g:GH * g + GH], GH), ALU.mult)\
                    .then_inc(a_prob, 1)

            def b_root(b, k):
                pool.wait_ge(b_var, 2 * b + k + 1)
                inverse_root(B_ST, B_RS).then_inc(b_rstd, 1)

            def b_addbias(b, _):
                pool.wait_ge(b_nrm, 2 * b + 1)
                pool.sem_inc(passed_pool, 1)
                pool.tensor_tensor(X[:, b, :], X[:, b, :], row("b2"), ALU.add).then_inc(b_bias, 1)
                pool.wait_ge(b_sx, b)
                pool.wait_ge(a_prev, b + 1)
                pool.tensor_copy(XN[:, :, 0:1], PREV[:, b, :, 1:2]).then_inc(b_first, 1)

            def b_cubes(b, k):
                h = slice(k * FT // 2, (k + 1) * FT // 2)
                pool.wait_ge(b_aff, 2 * b + k + 1)
                pool.tensor_tensor(HQ[:, h, :], HQ[:, h, :], HX[:, h, :], ALU.mult).then_inc(b_cube, 1)

            def b_addnorm(b, n):
                pool.wait_ge(b_mix, 3 * b + n + 1)
                for i in MIX_TURNS[n]:
                    last = pool.tensor_tensor(MX[:, i], MX[:, i], XN[:, :, 1:T + 1], ALU.add)
                last.then_inc(b_mx, 1)

            def d_first_states(b, _):
                pool.wait_ge(d_s, 2 * b)
                pool.tensor_copy(AJ[:, :, :, 0:1], S0[:, b, :, :].unsqueeze(3)).then_inc(d_s0, 1)

            def d_rstate(b, _):
                pool.wait_ge(d_s, 2 * b + 2)
                r = KR[:, 1, 1, :].unsqueeze(1).to_broadcast([P, RS, T])
                pool.tensor_tensor(SS[:, 1], SS[:, 1], r, ALU.mult).then_inc(d_rs, 1)

            def d_squares(b, _):
                pool.wait_ge(d_cen, b + 1)
                pool.tensor_tensor(OQ[:, :], O[:, :], O[:, :], ALU.mult).then_inc(d_sq, 1)

            def d_root(b, _):
                pool.wait_ge(d_var, b + 1)
                inverse_root(D_ST, D_RS).then_inc(d_rstd, 1)

            def d_before(b, _):
                pool.wait_ge(d_sx, b)
                pool.tensor_copy(XM[:, :, 0:1], PREV[:, b, :, 0:1]).then_inc(d_first, 1)

            def d_relu2(b, _):
                pool.wait_ge(d_relu, b + 1)
                pool.tensor_tensor(KK[:, :, :], RL[:, :, :], RL[:, :, :], ALU.mult).then_inc(d_kk, 1)

            pieces = named(a_root, a_addbias, a_before, a_addmask, a_divide, b_root, b_addbias, b_cubes, b_addnorm,
                           d_first_states, d_rstate, d_squares, d_root, d_before, d_relu2)
            run(pieces, POOL_ORDER, 0)
            pool.wait_ge(in_wb, IN_WB)
            w2 = W[:, W_AT["w2"]:W_AT["w2"] + FT * C]
            pool.tensor_scalar(w2, w2, 0.5, 0.0, ALU.mult, ALU.add).then_inc(set_pool, 1)
            for i in range(1, PEEL):
                run(pieces, POOL_ORDER, i)
            with pool.Fori(PEEL, B) as i:
                run(pieces, POOL_ORDER, i)
            for i in range(B, B + LAG):
                run(pieces, POOL_ORDER, i)


def kernel(**inputs):
    import concourse.bacc as _bacc
    from concourse.bass_utils import run_bass_kernel_spmd as _run

    a = {k: np.asarray(v) for k, v in inputs.items()}

    def l0(n):
        return a["L0_xattn_" + n]

    def l1(n):
        return a["L1_xattn_" + n]

    def packed(m):
        k = m.shape[0] // P
        return m.reshape(k, P, m.shape[1]).transpose(1, 0, 2).reshape(P, -1)

    def padded(m, shape, at=0):
        out = np.zeros(shape, m.dtype)
        out[at:at + m.shape[0], :m.shape[1]] = m
        return out

    parts = {
        "qkv": packed(l0("w_qkv")), "ao": packed(l0("w_ao")), "q": packed(l0("w_q")), "kv": packed(l0("w_kv")),
        "co": packed(l0("w_co")), "w1": packed(l0("w1")), "w2": packed(l0("w2")),
        "maa1": packed(padded(l1("maa_w1"), (C, C))),
        "maa2": np.concatenate([padded(l1("maa_w2")[i], (P, C), i * ME % P) for i in range(MIX)], axis=1),
        "dec1": packed(l1("decay_w1")), "dec2": padded(l1("decay_w2"), (P, C)),
        "r": packed(l1("Wr").T), "k": packed(l1("Wk").T), "v": packed(l1("Wv").T), "g": packed(l1("Wg").T),
        "o": packed(l1("Wo").T), "fk": packed(l1("ffn_Wk").T), "fr": packed(l1("ffn_Wr").T),
        "fv": packed(l1("ffn_Wv").T)}
    weights = np.concatenate([parts[name] for name, _ in WEIGHTS], axis=1)
    vectors = {
        "ln1_s": l0("ln1_s"), "ln1_b": l0("ln1_b"), "bq0": l0("b_qkv")[0:C], "bk0": l0("b_qkv")[C:2 * C],
        "ln2_s": l0("ln2_s"), "ln2_b": l0("ln2_b"), "bq1": l0("b_q"), "bk1": l0("b_kv")[0:C],
        "ln3_s": l0("ln3_s"), "ln3_b": l0("ln3_b"), "b1": l0("b1"), "r1_w": l1("ln1_w"), "r1_b": l1("ln1_b"),
        "maa_x": l1("maa_x"), "stack": l1("maa_stack"), "td": l1("time_decay"), "u": l1("faaaa"),
        "r2_w": l1("ln2_w"), "r2_b": l1("ln2_b"), "fmk": l1("ffn_maa_k"), "fmr": l1("ffn_maa_r")}
    cols = np.concatenate([vectors[name].reshape(-1, P) for name, _ in COLS], axis=0)
    by_row = {"bv0": l0("b_qkv")[2 * C:], "ao": l0("b_ao"), "bv1": l0("b_kv")[C:], "co": l0("b_co"), "b2": l0("b2"),
              "gn_w": l1("gn_w"), "gn_b": l1("gn_b")}
    rows = np.stack([by_row[name] for name in ROWS])
    consts = np.zeros((P, K_END), np.float32)
    for p in range(P):
        consts[p, K_ID + p] = 1.0
        consts[p, K_SEL + p // RS] = 1.0
        consts[p, K_PAR + (p // HD) % 2] = 1.0 / HD ** 0.5
    consts[:, K_POW] = -0.5

    arrays = {"x": a["x"], "enc": a["ctx_2048"], "mask_self": a["mask_1x1xSxS2_fc1"].reshape(T, T),
              "mask_cross": a["mask_Bx1xSxS2_ff1"].reshape(B, T, T), "weights": weights, "cols": cols, "rows": rows,
              "consts": consts}
    nc = _bacc.Bacc("TRN2", target_bir_lowering=False, num_devices=1)
    args, ins = {}, {}
    for name, v in arrays.items():
        v = np.ascontiguousarray(v)
        ins[f"in_{name}"] = v
        args[name] = nc.dram_tensor(f"in_{name}", v.shape, mybir.dt.from_np(v.dtype), kind="ExternalInput").ap()
    args["out"] = nc.dram_tensor("out_0", (B, T, C), F32, kind="ExternalOutput").ap()
    build(nc, **args)
    r = _run(nc, [ins], core_ids=[0])
    return r.results[0]["out_0"]
```

```python
from contextlib import ExitStack

import numpy as np

import concourse.bass as bass
from concourse import mybir

F32 = mybir.dt.float32
I32 = mybir.dt.int32
ALU = mybir.AluOpType
ACT = mybir.ActivationFunctionType
AX_X = mybir.AxisListType.X

B, T, C = 16, 128, 256
P = 128
CT = C // P
NH, HD = 16, 16
RH, RS = 32, 8
F = 4 * C
FT = F // P
MIX, ME = 5, 32
DE = 64
GRP, GH = 4, 4
EPS = 1e-5
GELU_C, GELU_A = 0.7978845608028654, 0.044715

WEIGHTS = [("qkv", CT * 3 * C), ("ao", CT * C), ("q", CT * C), ("kv", CT * 2 * C), ("co", CT * C),
           ("w1", CT * F), ("w2", FT * C), ("maa1", CT * C), ("maa2", MIX * C), ("dec1", CT * DE), ("dec2", C),
           ("r", CT * C), ("k", CT * C), ("v", CT * C), ("g", CT * C),
           ("o", CT * C), ("fk", CT * C), ("fr", CT * C), ("fv", CT * C)]
W_AT, W_END = {}, 0
for _name, _n in WEIGHTS:
    W_AT[_name] = W_END
    W_END += _n
W_CUT1, W_CUT2 = W_AT["w1"], W_AT["o"]

COLS = [("ln1_s", 2), ("ln1_b", 2), ("bq0", 2), ("bk0", 2), ("ln2_s", 2), ("ln2_b", 2), ("bq1", 2), ("bk1", 2),
        ("ln3_s", 2), ("ln3_b", 2), ("b1", 8), ("r1_w", 2), ("r1_b", 2), ("maa_x", 2), ("stack", 10), ("td", 2),
        ("u", 2), ("r2_w", 2), ("r2_b", 2), ("fmk", 2), ("fmr", 2)]
C_AT, C_END = {}, 0
for _name, _n in COLS:
    C_AT[_name] = C_END
    C_END += _n
ROWS = ["bv0", "ao", "bv1", "co", "b2", "gn_w", "gn_b"]
K_ID, K_SEL, K_PAR, K_POW, K_END = 0, P, P + 32, P + 34, P + 35

MIX_TURNS = [(1, 0), (3, 2), (4,)]

SP_ORDER = [
    ("a_load", 0, 0), ("d_store", 0, 2)]
PE_ORDER = [
    ("d_vturn", 0, 2), ("d_vturn", 1, 2), ("a_turn", 0, 0), ("d_vturn", 2, 2), ("b_turn", 0, 1), ("a_val", 0, 0),
    ("d_vturn", 3, 2), ("a_key", 0, 0), ("a_query", 0, 0), ("b_mlp1", 0, 1), ("a_scores", (0, 0), 0), ("a_scores",
    (0, 1), 0), ("b_mlp1", 1, 1), ("d_own", 0, 2), ("a_scores", (0, 2), 0), ("a_enc_turn", 0, 0), ("a_scores", (0,
    3), 0), ("d_read", 0, 2), ("d_oturn", 0, 2), ("a_val", 1, 0), ("b_mlp2", 0, 1), ("a_prob_turn", (0, 0), 0),
    ("a_prob_turn", (0, 1), 0), ("a_key", 1, 0), ("a_prob_turn", (0, 2), 0), ("a_prob_turn", (0, 3), 0), ("b_turn",
    1, 1), ("a_pv", 0, 0), ("a_out", 0, 0), ("b_low1", 0, 1), ("b_low2", 0, 1), ("a_turn", 1, 0), ("b_low2", 1, 1),
    ("d_yturn", 0, 2), ("a_query", 1, 0), ("b_low2", 2, 1), ("d_out", 0, 2), ("b_decay1", 0, 1), ("a_scores", (1,
    0), 0), ("a_scores", (1, 1), 0), ("a_scores", (1, 2), 0), ("a_scores", (1, 3), 0), ("b_keyrec", 0, 1),
    ("d_turn", 0, 2), ("b_decay2", 0, 1), ("b_valgate", 0, 1), ("d_keyrec", 0, 2), ("a_prob_turn", (1, 0), 0),
    ("a_prob_turn", (1, 1), 0), ("a_prob_turn", (1, 2), 0), ("a_prob_turn", (1, 3), 0), ("a_pv", 1, 0), ("d_val", 0,
    2), ("a_out", 1, 0)]
DVE_ORDER = [
    ("a_stats", 0, 0), ("a_moments", 0, 0), ("a_variance", 0, 0), ("d_outer", 0, 2), ("b_stats", 0, 1),
    ("b_moments", 0, 1), ("a_normal", 0, 0), ("b_variance", 0, 1), ("d_outer", 1, 2), ("d_ruk", 0, 2), ("b_normal",
    0, 1), ("d_outer", 2, 2), ("d_scan", 0, 2), ("d_outer", 3, 2), ("d_scan", 1, 2), ("a_val", 0, 0), ("a_key", 0,
    0), ("d_rstate", 0, 2), ("a_mask", (0, 0), 0), ("a_mask", (0, 1), 0), ("b_hidden", 0, 1), ("b_hidden", 1, 1),
    ("b_affine", 0, 1), ("a_maxima", (0, 0), 0), ("d_own", 0, 2), ("b_affine", 1, 1), ("a_maxima", (0, 1), 0),
    ("a_mask", (0, 2), 0), ("a_mask", (0, 3), 0), ("a_inverse", (0, 0), 0), ("b_gelu", 0, 1), ("b_gelu", 1, 1),
    ("d_output", 0, 2), ("a_maxima", (0, 2), 0), ("d_means", 0, 2), ("a_inverse", (0, 1), 0), ("d_centre", 0, 2),
    ("a_maxima", (0, 3), 0), ("a_inverse", (0, 2), 0), ("d_spread", 0, 2), ("d_guess", 0, 2), ("d_guess", 1, 2),
    ("b_sum", 0, 1), ("a_inverse", (0, 3), 0), ("b_stats", 1, 1), ("d_guess", 2, 2), ("b_moments", 1, 1),
    ("b_variance", 1, 1), ("d_newton", (0, 0), 2), ("d_newton", (0, 1), 2), ("d_newton", (0, 2), 2), ("a_key", 1,
    0), ("b_normal", 1, 1), ("d_newton", (1, 0), 2), ("d_newton", (1, 1), 2), ("d_newton", (1, 2), 2), ("d_newton",
    (2, 0), 2), ("d_newton", (2, 1), 2), ("b_shift", 0, 1), ("b_mixed", 0, 1), ("d_newton", (2, 2), 2), ("d_norm",
    0, 2), ("d_weight", 0, 2), ("a_sum", 0, 0), ("a_stats", 1, 0), ("d_bias", 0, 2), ("a_moments", 1, 0),
    ("a_variance", 1, 0), ("a_val", 1, 0), ("a_normal", 1, 0), ("d_gated", 0, 2), ("b_streams", 0, 1), ("b_streams",
    1, 1), ("b_streams", 2, 1), ("d_sum", 0, 2), ("d_stats", 0, 2), ("a_mask", (1, 0), 0), ("a_mask", (1, 1), 0),
    ("d_moments", 0, 2), ("a_maxima", (1, 0), 0), ("d_variance", 0, 2), ("a_mask", (1, 2), 0), ("a_maxima", (1, 1),
    0), ("d_normal", 0, 2), ("a_mask", (1, 3), 0), ("a_maxima", (1, 2), 0), ("d_shift", 0, 2), ("a_inverse", (1, 0),
    0), ("a_inverse", (1, 1), 0), ("d_mixed", 0, 2), ("a_maxima", (1, 3), 0), ("a_inverse", (1, 2), 0),
    ("a_inverse", (1, 3), 0), ("d_mixing", 0, 2), ("d_final", 0, 2), ("b_gate", 0, 1), ("a_sum", 1, 0)]
ACT_ORDER = [
    ("a_scale", 0, 0), ("b_scale", 0, 1), ("a_query", 0, 0), ("b_square", 0, 1), ("b_square", 1, 1), ("a_enc_copy",
    0, 0), ("a_exps", (0, 0), 0), ("b_tanhs", 0, 1), ("d_ocopy", 0, 2), ("b_tanhs", 1, 1), ("a_exps", (0, 1), 0),
    ("a_exps", (0, 2), 0), ("a_exps", (0, 3), 0), ("a_prob_copy", (0, 0), 0), ("a_prob_copy", (0, 1), 0),
    ("a_prob_copy", (0, 2), 0), ("a_prob_copy", (0, 3), 0), ("b_scale", 1, 1), ("a_ctx_copy", 0, 0), ("b_low", 0,
    1), ("a_scale", 1, 0), ("d_ycopy", 0, 2), ("a_query", 1, 0), ("b_decay1", 0, 1), ("a_exps", (1, 0), 0),
    ("a_exps", (1, 1), 0), ("b_keyrec", 0, 1), ("d_scale", 0, 2), ("b_decay2", 0, 1), ("a_exps", (1, 2), 0),
    ("a_exps", (1, 3), 0), ("a_prob_copy", (1, 0), 0), ("a_prob_copy", (1, 1), 0), ("d_keyrec", 0, 2),
    ("a_prob_copy", (1, 2), 0), ("a_prob_copy", (1, 3), 0), ("b_valgate", 0, 1), ("a_ctx_copy", 1, 0), ("b_decays",
    0, 1)]
POOL_ORDER = [
    ("a_root", 0, 0), ("d_first_states", 0, 2), ("b_root", 0, 1), ("b_addbias", 0, 1), ("d_rstate", 0, 2),
    ("a_addmask", (0, 0), 0), ("d_before", 0, 2), ("a_addmask", (0, 1), 0), ("a_addbias", 0, 0), ("b_cubes", 0, 1),
    ("b_cubes", 1, 1), ("a_addmask", (0, 2), 0), ("a_addmask", (0, 3), 0), ("a_divide", (0, 0), 0), ("d_squares", 0,
    2), ("a_divide", (0, 1), 0), ("a_divide", (0, 2), 0), ("a_divide", (0, 3), 0), ("a_before", 0, 0), ("b_root", 1,
    1), ("a_root", 1, 0), ("b_addnorm", 0, 1), ("b_addnorm", 1, 1), ("b_addnorm", 2, 1), ("a_addmask", (1, 0), 0),
    ("a_addmask", (1, 1), 0), ("d_root", 0, 2), ("a_addmask", (1, 2), 0), ("a_addmask", (1, 3), 0), ("a_divide", (1,
    0), 0), ("a_divide", (1, 1), 0), ("a_divide", (1, 2), 0), ("a_divide", (1, 3), 0), ("d_relu2", 0, 2),
    ("a_addbias", 1, 0)]

LAG = max(lag for order in (SP_ORDER, PE_ORDER, DVE_ORDER, ACT_ORDER, POOL_ORDER) for _, _, lag in order)
PEEL = LAG + 1


def build(nc, x, enc, mask_self, mask_cross, weights, cols, rows, consts, out):
    with ExitStack() as ctx:
        def sb(name, shape):
            return ctx.enter_context(nc.sbuf_tensor(name, [P, *shape], F32))

        def pb(name, shape):
            return ctx.enter_context(nc.psum_tensor(name, [P, *shape], F32))

        X = sb("X", [B, C])
        MASK = sb("MASK", [B + 1, T])
        MADD = sb("MADD", [B + 1, T])
        S0 = sb("S0", [B, CT, RS])
        PREV = sb("PREV", [B, CT, 2])
        W = sb("W", [W_END])
        CRAW = sb("CRAW", [P])
        COL = sb("COL", [C_END])
        ROW = sb("ROW", [len(ROWS), C])
        CST = sb("CST", [K_END])
        QB = sb("QB", [2, 2, CT])
        A_ST, A_MV, A_RS = sb("A_ST", [6]), sb("A_MV", [2]), sb("A_RS", [1])
        A_N = sb("A_N", [C])
        A_LT = sb("A_LT", [CT, T])
        ENC = sb("ENC", [C])
        A_ET = sb("A_ET", [CT, T])
        QP = sb("QP", [2, CT, T])
        KT = sb("KT", [CT, T])
        VP = sb("VP", [NH // 2, 2, 2 * HD])
        SC = sb("SC", [GRP, GH, T])
        NMX, SUM, RINV = sb("NMX", [NH]), sb("SUM", [NH]), sb("RINV", [NH])
        PT = sb("PT", [GRP, GH, T])
        CTX = sb("CTX", [CT, T])
        B_ST, B_MV, B_RS = sb("B_ST", [6]), sb("B_MV", [2]), sb("B_RS", [1])
        B_N = sb("B_N", [C])
        B_LT = sb("B_LT", [CT, T])
        HX, HQ, HG = sb("HX", [FT, T]), sb("HQ", [FT, T]), sb("HG", [FT, T])
        XN, SX, XX = sb("XN", [CT, T + 1]), sb("SX", [CT, T]), sb("XX", [CT, T])
        MT = sb("MT", [CT, T])
        MX = sb("MX", [MIX, CT, T])
        DT, EW = sb("DT", [T]), sb("EW", [CT, T])
        TG = sb("TG", [C])
        W8 = sb("W8", [CT, RS, T])
        KR = sb("KR", [2, CT, T])
        V8 = sb("V8", [CT, RS, P // RS, RS])
        G = sb("G", [C])
        AJ = sb("AJ", [CT, RS, T])
        SS = sb("SS", [CT, RS, T])
        RK = sb("RK", [CT, T])
        O, OQ = sb("O", [C]), sb("OQ", [C])
        OH = sb("OH", [GH, T])
        CV = sb("CV", [C])
        GM, GV, GE = sb("GM", [RH]), sb("GV", [RH]), sb("GE", [RH])
        GY, GT = sb("GY", [RH]), sb("GT", [RH])
        Y = sb("Y", [C])
        YT = sb("YT", [CT, T])
        D_ST, D_MV, D_RS = sb("D_ST", [6]), sb("D_MV", [2]), sb("D_RS", [1])
        D_N = sb("D_N", [C])
        XM, SM, XK, XR = sb("XM", [CT, T + 1]), sb("SM", [CT, T]), sb("XK", [CT, T]), sb("XR", [CT, T])
        RL, KK = sb("RL", [CT, T]), sb("KK", [CT, T])
        RR = sb("RR", [C])

        PS_S = pb("PS_S", [3, GH, T])
        PS_T = pb("PS_T", [2, 512])
        PS_B = pb("PS_B", [2, 512])
        PS_D = pb("PS_D", [512])

        def sem(name):
            return ctx.enter_context(nc.semaphore(name))

        in_enc = sem("in_enc")
        a_stat = sem("a_stat")
        a_var = sem("a_var")
        a_rstd = sem("a_rstd")
        a_nrm = sem("a_nrm")
        a_lnps = sem("a_lnps")
        a_ln = sem("a_ln")
        a_bias = sem("a_bias")
        a_encps = sem("a_encps")
        a_enc = sem("a_enc")
        a_prev = sem("a_prev")
        a_kps = sem("a_kps")
        a_qps = sem("a_qps")
        a_v = sem("a_v")
        a_k = sem("a_k")
        a_q = sem("a_q")
        a_score = sem("a_score")
        a_masked = sem("a_masked")
        a_added = sem("a_added")
        a_max = sem("a_max")
        a_exp = sem("a_exp")
        a_inv = sem("a_inv")
        a_prob = sem("a_prob")
        a_turned = sem("a_turned")
        a_pt = sem("a_pt")
        a_pvps = sem("a_pvps")
        a_ctx = sem("a_ctx")
        a_ops = sem("a_ops")
        a_res = sem("a_res")
        b_stat = sem("b_stat")
        b_var = sem("b_var")
        b_rstd = sem("b_rstd")
        b_nrm = sem("b_nrm")
        b_lnps = sem("b_lnps")
        b_ln = sem("b_ln")
        b_bias = sem("b_bias")
        b_up = sem("b_up")
        b_hx = sem("b_hx")
        b_sq = sem("b_sq")
        b_aff = sem("b_aff")
        b_cube = sem("b_cube")
        b_tanh = sem("b_tanh")
        b_hg = sem("b_hg")
        b_dnps = sem("b_dnps")
        b_res = sem("b_res")
        b_first = sem("b_first")
        b_sx = sem("b_sx")
        b_xx = sem("b_xx")
        b_m1ps = sem("b_m1ps")
        b_mt = sem("b_mt")
        b_m2ps = sem("b_m2ps")
        b_mix = sem("b_mix")
        b_mx = sem("b_mx")
        b_d1ps = sem("b_d1ps")
        b_dt = sem("b_dt")
        b_d2ps = sem("b_d2ps")
        b_ew = sem("b_ew")
        b_w8 = sem("b_w8")
        b_krps = sem("b_krps")
        b_kr = sem("b_kr")
        b_vgps = sem("b_vgps")
        b_v = sem("b_v")
        b_tg = sem("b_tg")
        b_g = sem("b_g")
        d_s0 = sem("d_s0")
        d_vps = sem("d_vps")
        d_a = sem("d_a")
        d_s = sem("d_s")
        d_rs = sem("d_rs")
        d_rk = sem("d_rk")
        d_cps = sem("d_cps")
        d_cv = sem("d_cv")
        d_ops = sem("d_ops")
        d_oh = sem("d_oh")
        d_otps = sem("d_otps")
        d_o = sem("d_o")
        d_m = sem("d_m")
        d_cen = sem("d_cen")
        d_sq = sem("d_sq")
        d_v = sem("d_v")
        d_gr = sem("d_gr")
        d_n = sem("d_n")
        d_gw = sem("d_gw")
        d_gb = sem("d_gb")
        d_y = sem("d_y")
        d_yps = sem("d_yps")
        d_yt = sem("d_yt")
        d_wops = sem("d_wops")
        d_res = sem("d_res")
        d_stat = sem("d_stat")
        d_var = sem("d_var")
        d_rstd = sem("d_rstd")
        d_nrm = sem("d_nrm")
        d_lnps = sem("d_lnps")
        d_ln = sem("d_ln")
        d_first = sem("d_first")
        d_sx = sem("d_sx")
        d_xkr = sem("d_xkr")
        d_krps = sem("d_krps")
        d_relu = sem("d_relu")
        d_kk = sem("d_kk")
        d_rr = sem("d_rr")
        d_fps = sem("d_fps")
        d_f = sem("d_f")
        d_fin = sem("d_fin")
        in_first = sem("in_first")
        in_rest = sem("in_rest")
        in_wb = sem("in_wb")
        in_wd = sem("in_wd")
        set_col = sem("set_col")
        set_dve = sem("set_dve")
        set_pool = sem("set_pool")
        passed_dve = sem("passed_dve")
        passed_pool = sem("passed_pool")
        stored = sem("stored")

        IN_FIRST, IN_REST, IN_WB, IN_WD = 16 * 7, 16 * 4, 16, 16

        ident = CST[:, K_ID:K_ID + P]
        hsel = CST[:, K_SEL:K_SEL + P // RS]
        hsel32 = CST[:, K_SEL:K_SEL + 32]

        values, keys, turns, queries = (PS_S[:, k // 2].rearrange("p j n -> p (j n)")[:, k % 2 * C:(k % 2 + 1) * C]
                                        for k in range(4))

        def w(name, kt, n, lo, hi):
            at = W_AT[name] + kt * n
            return W[:, at + lo:at + hi]

        def col(name, k=0, n=1):
            return COL[:, C_AT[name] + k:C_AT[name] + k + n]

        def row(name):
            return ROW[:, ROWS.index(name), :]

        def over_tokens(ap, n, m=T):
            return ap.unsqueeze(2).to_broadcast([P, n, m])

        def over_heads(ap):
            return ap.unsqueeze(1).to_broadcast([P, GH, T])

        def heads(ap):
            return ap.rearrange("p (h d) -> p h d", d=RS)

        def tiles(ap):
            return ap.rearrange("p (t n) -> p t n", t=CT)

        def run(pieces, order, i):
            for name, arg, lag in order:
                if isinstance(i, int) and not 0 <= i - lag < B:
                    continue
                pieces[name](i - lag, arg)

        def later(b, a=0):
            return not (isinstance(b, int) and b == 0 and a == 0)

        def named(*functions):
            return {f.__name__: f for f in functions}

        block = ctx.enter_context(nc.Block())

        @block.sync
        def _(sp):
            sp.dma_start(CST[:, :], consts).then_inc(in_first, 16)
            sp.dma_start(CRAW[0:C_END, :], cols).then_inc(in_first, 16)
            sp.dma_start(X[:, 0, :], x[0]).then_inc(in_first, 16)
            sp.dma_start(W[:, 0:W_AT["ao"]], weights[:, 0:W_AT["ao"]]).then_inc(in_first, 16)
            sp.dma_start(MASK[:, B, :], mask_self).then_inc(in_first, 16)
            sp.dma_start(ROW[:, :, :], rows.unsqueeze(0).to_broadcast([P, len(ROWS), C])).then_inc(in_first, 16)
            sp.dma_start(W[:, W_AT["ao"]:W_CUT1], weights[:, W_AT["ao"]:W_CUT1]).then_inc(in_first, 16)
            sp.dma_start(MASK[:, 0:B, :], mask_cross.rearrange("b q k -> q b k")).then_inc(in_rest, 16)
            sp.dma_start(X[:, 1:B, :], x[1:B].rearrange("b s c -> s b c")).then_inc(in_rest, 16)
            sp.dma_start(W[:, W_CUT1:W_CUT2], weights[:, W_CUT1:W_CUT2]).then_inc(in_wb, 16)
            flat = enc[:, 2:2 + RS, :].rearrange("b s c -> b (s c)")
            with nc.allow_non_contiguous_dma(reason="32-byte pieces of the first states"):
                for t in range(CT):
                    sp.dma_start(S0[:, :, t, :],
                                 flat[:, t * P * RS:(t + 1) * P * RS].rearrange("b (p d) -> p b d", d=RS))\
                      .then_inc(in_rest, 16)
            sp.dma_start(W[:, W_CUT2:W_END], weights[:, W_CUT2:W_END]).then_inc(in_wd, 16)

            def d_store(b, _):
                sp.wait_ge(d_fin, b + 1)
                sp.dma_start(out[b], X[:, b, :]).then_inc(stored, 16)

            def a_load(b, _):
                sp.wait_ge(a_encps, b)
                sp.dma_start(ENC[:, :], enc[b]).then_inc(in_enc, 16)

            pieces = named(a_load, d_store)
            for i in range(PEEL):
                run(pieces, SP_ORDER, i)
            with sp.Fori(PEEL, B) as i:
                run(pieces, SP_ORDER, i)
            for i in range(B, B + LAG):
                run(pieces, SP_ORDER, i)
            sp.wait_ge(stored, 16 * B)

        @block.tensor
        def _(pe):
            pe.wait_ge(in_first, IN_FIRST)
            pe.transpose(PS_D[:, 0:C_END], CRAW[0:C_END, :], CST[0:C_END, K_ID:K_ID + C_END]).then_inc(set_col, 1)

            def turn(dst, src):
                for t in range(CT):
                    last = pe.transpose(dst[:, t * P:(t + 1) * P], src[:, t * P:(t + 1) * P], ident)
                return last

            def to_channels(dst, name, n, lo, rhs, count=CT):
                for m in range(count):
                    for kt in range(CT):
                        last = pe.matmul(dst[:, m * T:(m + 1) * T], w(name, kt, n, lo + m * P, lo + (m + 1) * P),
                                         rhs[:, kt, 0:T], start=(kt == 0), stop=(kt == CT - 1))
                return last

            def to_tokens(dst, name, n, lo, lhs, kts=CT):
                for kt in range(kts):
                    last = pe.matmul(dst, lhs[:, kt, 0:T], w(name, kt, n, lo, lo + C),
                                     start=(kt == 0), stop=(kt == kts - 1))
                return last

            def a_enc_turn(b, _):
                pe.wait_ge(in_enc, 16 * b + 16)
                pe.wait_ge(a_masked, 8 * b + 2)
                turn(turns, ENC).then_inc(a_encps, 1)

            def a_turn(b, a):
                pe.wait_ge(a_nrm, 2 * b + a + 1)
                if a:
                    pe.wait_ge(a_enc, b + 1)
                elif later(b):
                    pe.wait_ge(a_masked, 8 * b - 2)
                turn(turns, A_N).then_inc(a_lnps, 1)

            def a_val(b, a):
                pe.wait_ge(a_masked, 8 * b + 4 * a)
                if a:
                    pe.wait_ge(a_enc, b + 1)
                    to_tokens(values, "kv", 2 * C, C, A_ET)
                else:
                    pe.wait_ge(a_ln, 2 * b + 1)
                    to_tokens(values, "qkv", 3 * C, 2 * C, A_LT)

            def a_key(b, a):
                if a:
                    pe.wait_ge(a_enc, b + 1)
                    to_channels(keys, "kv", 2 * C, 0, A_ET).then_inc(a_kps, 1)
                else:
                    pe.wait_ge(a_ln, 2 * b + 1)
                    to_channels(keys, "qkv", 3 * C, C, A_LT).then_inc(a_kps, 1)

            def a_query(b, a):
                pe.wait_ge(a_ln, 2 * b + a + 1)
                if a:
                    to_channels(queries, "q", C, 0, A_LT).then_inc(a_qps, 1)
                else:
                    to_channels(queries, "qkv", 3 * C, 0, A_LT).then_inc(a_qps, 1)

            def a_scores(b, arg):
                a, g = arg
                if g == 0:
                    pe.wait_ge(a_v, 2 * b + a + 1)
                    pe.wait_ge(a_k, 2 * b + a + 1)
                    pe.wait_ge(a_q, 2 * b + a + 1)
                elif g == 3:
                    pe.wait_ge(a_masked, 8 * b + 4 * a + 1)
                for t in range(CT):
                    for par in range(2):
                        last = pe.matmul(PS_S[:, g % 3, 2 * t + par, :], QP[32 * g:32 * g + 32, par, t, :],
                                         KT[32 * g:32 * g + 32, t, :], start=True, stop=True)
                last.then_inc(a_score, 1)

            def a_prob_turn(b, arg):
                a, g = arg
                pe.wait_ge(a_prob, 8 * b + 4 * a + g + 1)
                if g == 0:
                    pe.wait_ge(a_ctx, 2 * b + a)
                elif g == 1:
                    pe.wait_ge(a_res, 2 * b + a)
                else:
                    pe.wait_ge(a_pt, 8 * b + 4 * a + g - 1)
                for j in range(GH):
                    last = pe.transpose(PS_T[:, g % 2, j * T:(j + 1) * T], SC[:, g, j, :], ident)
                last.then_inc(a_turned, 1)

            def a_pv(b, a):
                pe.wait_ge(a_pt, 8 * b + 4 * a + 4)
                for t in range(CT):
                    for par in range(2):
                        for g in range(GRP):
                            last = pe.matmul(PS_T[32 * g:32 * g + 32, 0, t * T:(t + 1) * T],
                                             VP[:, GRP * t + g, par, :], PT[:, g, 2 * t + par, :],
                                             start=(par == 0), stop=(par == 1), skip_group_check=True)
                last.then_inc(a_pvps, 1)

            def a_out(b, a):
                pe.wait_ge(a_ctx, 2 * b + a + 1)
                to_tokens(PS_T[:, 1, 0:C], "co" if a else "ao", C, 0, CTX).then_inc(a_ops, 1)

            def b_turn(b, k):
                pe.wait_ge(b_nrm, 2 * b + k + 1)
                if k == 0:
                    pe.wait_ge(b_g, b)
                    pe.wait_ge(b_v, b)
                    pe.wait_ge(b_ew, b)
                turn(PS_B[:, 0, 0:C], B_N).then_inc(b_lnps, 1)

            def b_mlp1(b, k):
                if k == 0:
                    pe.wait_ge(b_ln, 2 * b + 1)
                to_channels(PS_B[:, 1 - k, :], "w1", F, k * (F // 2), B_LT, FT // 2).then_inc(b_up, 1)

            def b_mlp2(b, _):
                pe.wait_ge(b_hg, 2 * b + 2)
                to_tokens(PS_B[:, 1, 0:C], "w2", C, 0, HG, FT).then_inc(b_dnps, 1)

            def b_low1(b, _):
                pe.wait_ge(b_xx, b + 1)
                to_channels(PS_B[:, 1, 0:C], "maa1", C, 0, XX).then_inc(b_m1ps, 1)

            def b_low2(b, n):
                if n == 0:
                    pe.wait_ge(b_mt, b + 1)
                elif n == 2:
                    pe.wait_ge(b_mix, 3 * b + 1)
                for k, i in enumerate(MIX_TURNS[n]):
                    for m in range(CT):
                        last = pe.matmul(PS_B[:, n % 2, k * C + m * T:k * C + (m + 1) * T],
                                         w("maa2", i, C, m * P, (m + 1) * P), MT[:, i * ME // P, :],
                                         start=True, stop=True)
                last.then_inc(b_m2ps, 1)

            def b_decay1(b, _):
                pe.wait_ge(b_mx, 3 * b + 1)
                pe.wait_ge(b_mix, 3 * b + 2)
                for kt in range(CT):
                    last = pe.matmul(PS_B[0:DE, 1, 0:T], w("dec1", kt, DE, 0, DE), MX[:, 1, kt, :],
                                     start=(kt == 0), stop=(kt == CT - 1))
                last.then_inc(b_d1ps, 1)

            def b_keyrec(b, _):
                pe.wait_ge(b_mx, 3 * b + 2)
                pe.wait_ge(b_mix, 3 * b + 3)
                to_channels(PS_B[:, 0, 0:C], "k", C, 0, MX[:, 0])
                to_channels(PS_B[:, 0, C:2 * C], "r", C, 0, MX[:, 3]).then_inc(b_krps, 1)

            def b_decay2(b, _):
                pe.wait_ge(b_dt, b + 1)
                for m in range(CT):
                    last = pe.matmul(PS_B[:, 1, m * T:(m + 1) * T], w("dec2", 0, C, m * P, (m + 1) * P)[0:DE],
                                     DT[0:DE, :], start=True, stop=True)
                last.then_inc(b_d2ps, 1)

            def b_valgate(b, _):
                pe.wait_ge(b_mx, 3 * b + 3)
                pe.wait_ge(b_kr, b + 1)
                to_tokens(PS_B[:, 0, 0:C], "v", C, 0, MX[:, 2])
                to_tokens(PS_B[:, 0, C:2 * C], "g", C, 0, MX[:, 4]).then_inc(b_vgps, 1)

            def d_vturn(b, n):
                t, half = n // 2, n % 2
                if n == 0:
                    pe.wait_ge(b_v, b + 1)
                    pe.wait_ge(d_f, b)
                else:
                    pe.wait_ge(d_a, 4 * b + n)
                for j in range(4):
                    last = pe.transpose(PS_D[:, j * T:(j + 1) * T],
                                        V8[:, t, 4 * half + j].rearrange("p h k -> p (h k)"), ident)
                last.then_inc(d_vps, 1)

            def d_own(b, _):
                pe.wait_ge(d_rk, b + 1)
                pe.wait_ge(d_a, 4 * b + 4)
                for t in range(CT):
                    last = pe.matmul(PS_D[:, t * (P // RS):(t + 1) * (P // RS)], RK[:, t, :], hsel,
                                     start=True, stop=True)
                last.then_inc(d_cps, 1)

            def d_read(b, _):
                pe.wait_ge(d_cv, b + 1)
                pe.wait_ge(d_rs, 2 * b + 2)
                for t in range(CT):
                    for half in range(2):
                        at = 32 * (2 * t + half)
                        last = pe.matmul(PS_D[at:at + 32, :], hsel32,
                                         SS[:, t, 4 * half:4 * half + 4, :].rearrange("p d n -> p (d n)"),
                                         start=True, stop=True, skip_group_check=True)
                last.then_inc(d_ops, 1)

            def d_oturn(b, _):
                pe.wait_ge(d_oh, b + 1)
                for j in range(4):
                    last = pe.transpose(PS_D[:, j * T:(j + 1) * T], OH[:, j, :], ident)
                last.then_inc(d_otps, 1)

            def d_yturn(b, _):
                pe.wait_ge(d_y, b + 1)
                turn(PS_D[:, 0:C], Y).then_inc(d_yps, 1)

            def d_out(b, _):
                pe.wait_ge(d_yt, b + 1)
                to_tokens(PS_D[:, 0:C], "o", C, 0, YT).then_inc(d_wops, 1)

            def d_turn(b, _):
                pe.wait_ge(d_nrm, b + 1)
                turn(PS_D[:, 0:C], D_N).then_inc(d_lnps, 1)

            def d_keyrec(b, _):
                pe.wait_ge(d_xkr, b + 1)
                to_channels(PS_D[:, 0:C], "fk", C, 0, XK)
                to_tokens(PS_D[:, C:2 * C], "fr", C, 0, XR).then_inc(d_krps, 1)

            def d_val(b, _):
                pe.wait_ge(d_kk, b + 1)
                pe.wait_ge(d_rr, b + 1)
                to_tokens(PS_D[:, 0:C], "fv", C, 0, KK).then_inc(d_fps, 1)

            pieces = named(a_enc_turn, a_turn, a_val, a_key, a_query, a_scores, a_prob_turn, a_pv, a_out,
                           b_turn, b_mlp1, b_mlp2, b_low1, b_low2, b_decay1, b_keyrec, b_decay2, b_valgate,
                           d_vturn, d_own, d_read, d_oturn, d_yturn, d_out, d_turn, d_keyrec, d_val)
            run(pieces, PE_ORDER, 0)
            pe.wait_ge(in_wb, IN_WB)
            pe.wait_ge(in_rest, IN_REST)
            run(pieces, PE_ORDER, 1)
            pe.wait_ge(in_wd, IN_WD)
            for i in range(2, PEEL):
                run(pieces, PE_ORDER, i)
            with pe.Fori(PEEL, B) as i:
                run(pieces, PE_ORDER, i)
            for i in range(B, B + LAG):
                run(pieces, PE_ORDER, i)

        @block.vector
        def _(dve):
            dve.memset(VP[:, :, :, :], 0.0)
            dve.memset(W8[:, :, :, 0:1], 0.0).then_inc(set_dve, 1)
            dve.wait_ge(set_col, 1)
            dve.tensor_copy(COL[:, :], PS_D[:, 0:C_END]).then_inc(set_dve, 1)
            dve.wait_ge(in_first, IN_FIRST)
            dve.wait_ge(set_dve, 2)
            for a in range(2):
                for par in range(2):
                    last = dve.tensor_scalar(QB[:, a, par, :], col(f"bq{a}", 0, 2), CST[:, K_PAR + par:K_PAR + par + 1],
                                             None, ALU.mult)
            last.then_inc(set_dve, 1)

            def row_stats(b, stat, ST):
                dve.sem_inc(passed_dve, 1)
                dve.bn_stats(ST[:, :], X[:, b, :]).then_inc(stat, 1)

            def moments(n, stat, ST, MV):
                dve.wait_ge(stat, 2 * n + 1)
                dve.sem_inc(passed_dve, 1)
                dve.bn_aggr(MV[:, :], ST[:, :]).then_inc(stat, 1)

            def variance(n, stat, var, ST, MV):
                dve.wait_ge(stat, 2 * n + 2)
                dve.tensor_scalar(ST[:, 0:1], MV[:, 1:2], EPS, None, ALU.add).then_inc(var, 1)

            def normalise(b, MV, RS_, N):
                return dve.tensor_scalar(N[:, :], X[:, b, :], MV[:, 0:1], RS_[:, 0:1], ALU.subtract, ALU.mult)

            def a_stats(b, a):
                if a:
                    dve.wait_ge(a_res, 2 * b + 1)
                row_stats(b, a_stat, A_ST)

            def a_moments(b, a):
                moments(2 * b + a, a_stat, A_ST, A_MV)

            def a_variance(b, a):
                variance(2 * b + a, a_stat, a_var, A_ST, A_MV)

            def a_normal(b, a):
                dve.wait_ge(a_rstd, 2 * b + a + 1)
                dve.wait_ge(a_lnps, 2 * b + a)
                normalise(b, A_MV, A_RS, A_N).then_inc(a_nrm, 1)

            def a_val(b, a):
                dve.wait_ge(a_kps, 2 * b + a + 1)
                dve.wait_ge(a_pvps, 2 * b + a)
                v = values.rearrange("p (h q d) -> p h q d", q=2, d=HD)
                bias = row(f"bv{a}").rearrange("p (h q d) -> p h q d", q=2, d=HD)
                for q in range(2):
                    last = dve.tensor_tensor(VP[:, :, q, q * HD:(q + 1) * HD], v[:, :, q, :], bias[:, :, q, :],
                                             ALU.add)
                last.then_inc(a_v, 1)

            def a_key(b, a):
                dve.wait_ge(a_kps, 2 * b + a + 1)
                dve.tensor_tensor(KT[:, :, :], tiles(keys), over_tokens(col(f"bk{a}", 0, 2), CT), ALU.add)\
                    .then_inc(a_k, 1)

            def a_mask(b, arg):
                a, g = arg
                dve.wait_ge(a_score, 8 * b + 4 * a + g + 1)
                if later(b, a):
                    dve.wait_ge(a_turned, 8 * b + 4 * a + g - 3)
                if not later(b) and a and g == 0:
                    dve.wait_ge(in_rest, IN_REST)
                mask = MASK[:, b, :] if a else MASK[:, B, :]
                dve.tensor_tensor(SC[:, g], PS_S[:, g % 3], over_heads(mask), ALU.mult).then_inc(a_masked, 1)

            def a_maxima(b, arg):
                a, g = arg
                dve.wait_ge(a_added, 8 * b + 4 * a + g + 1)
                dve.tensor_reduce(NMX[:, GH * g:GH * g + GH], SC[:, g], AX_X, ALU.max, negate=True)\
                    .then_inc(a_max, 1)

            def a_inverse(b, arg):
                a, g = arg
                dve.wait_ge(a_exp, 8 * b + 4 * a + g + 1)
                dve.reciprocal(RINV[:, GH * g:GH * g + GH], SUM[:, GH * g:GH * g + GH]).then_inc(a_inv, 1)

            def a_sum(b, a):
                dve.wait_ge(a_ops, 2 * b + a + 1)
                dve.wait_ge(a_bias, 2 * b + a + 1)
                dve.tensor_tensor(X[:, b, :], PS_T[:, 1, 0:C], X[:, b, :], ALU.add).then_inc(a_res, 1)

            def b_stats(b, k):
                if k:
                    dve.wait_ge(b_res, b + 1)
                else:
                    dve.wait_ge(a_res, 2 * b + 2)
                row_stats(b, b_stat, B_ST)

            def b_moments(b, k):
                moments(2 * b + k, b_stat, B_ST, B_MV)

            def b_variance(b, k):
                variance(2 * b + k, b_stat, b_var, B_ST, B_MV)

            def b_normal(b, k):
                dve.wait_ge(b_rstd, 2 * b + k + 1)
                normalise(b, B_MV, B_RS, B_N).then_inc(b_nrm, 1)

            def b_hidden(b, k):
                dve.wait_ge(b_up, 2 * b + k + 1)
                h = HX[:, k * FT // 2:(k + 1) * FT // 2, :]
                dve.tensor_tensor(h, PS_B[:, 1 - k, :].rearrange("p (m n) -> p m n", n=T),
                                  over_tokens(col("b1", k * FT // 2, FT // 2), FT // 2), ALU.add).then_inc(b_hx, 1)

            def b_affine(b, k):
                h = slice(k * FT // 2, (k + 1) * FT // 2)
                dve.wait_ge(b_sq, 2 * b + k + 1)
                dve.tensor_scalar(HQ[:, h, :], HQ[:, h, :], GELU_A * GELU_C, GELU_C, ALU.mult, ALU.add)\
                    .then_inc(b_aff, 1)

            def b_gelu(b, k):
                h = slice(k * FT // 2, (k + 1) * FT // 2)
                dve.wait_ge(b_tanh, 2 * b + k + 1)
                dve.scalar_tensor_tensor(HG[:, h, :], HQ[:, h, :], 1.0, HX[:, h, :], ALU.add, ALU.mult)\
                    .then_inc(b_hg, 1)

            def b_sum(b, _):
                dve.wait_ge(b_dnps, b + 1)
                dve.wait_ge(b_bias, b + 1)
                dve.tensor_tensor(X[:, b, :], PS_B[:, 1, 0:C], X[:, b, :], ALU.add).then_inc(b_res, 1)

            def b_shift(b, _):
                dve.wait_ge(b_first, b + 1)
                dve.wait_ge(b_ln, 2 * b + 2)
                dve.tensor_tensor(SX[:, :, :], XN[:, :, 0:T], XN[:, :, 1:T + 1], ALU.subtract).then_inc(b_sx, 1)

            def b_mixed(b, _):
                dve.wait_ge(b_sx, b + 1)
                for t in range(CT):
                    last = dve.scalar_tensor_tensor(XX[:, t, :], SX[:, t, :], col("maa_x", t), XN[:, t, 1:T + 1],
                                                    ALU.mult, ALU.add)
                last.then_inc(b_xx, 1)

            def b_streams(b, n):
                dve.wait_ge(b_m2ps, 3 * b + n + 1)
                for k, i in enumerate(MIX_TURNS[n]):
                    for t in range(CT):
                        at = k * C + t * T
                        last = dve.scalar_tensor_tensor(MX[:, i, t, :], PS_B[:, n % 2, at:at + T], col("stack", 2 * i + t),
                                                        SX[:, t, :], ALU.add, ALU.mult)
                last.then_inc(b_mix, 1)

            def b_gate(b, _):
                dve.wait_ge(b_tg, b + 1)
                dve.wait_ge(d_y, b)
                dve.scalar_tensor_tensor(G[:, :], TG[:, :], 1.0, PS_B[:, 0, C:2 * C], ALU.add, ALU.mult)\
                    .then_inc(b_g, 1)

            def d_outer(b, n):
                t, half = n // 2, n % 2
                dve.wait_ge(d_vps, 4 * b + n + 1)
                if n == 0:
                    dve.wait_ge(b_kr, b + 1)
                v = PS_D[:, :].rearrange("p (d n) -> p d n", n=T)
                k = KR[:, 0, t, 0:T - 1].unsqueeze(1).to_broadcast([P, 4, T - 1])
                dve.tensor_tensor(AJ[:, t, 4 * half:4 * half + 4, 1:T], v[:, :, 0:T - 1], k, ALU.mult)\
                    .then_inc(d_a, 1)

            def d_scan(b, t):
                if t == 0:
                    dve.wait_ge(d_s0, b + 1)
                    dve.wait_ge(b_w8, b + 1)
                dve.wait_ge(d_a, 4 * b + 2 * t + 2)
                dve.tensor_tensor_scan(SS[:, t].rearrange("p d n -> p (d n)"), W8[:, t].rearrange("p d n -> p (d n)"),
                                       AJ[:, t].rearrange("p d n -> p (d n)"), 0.0, ALU.mult, ALU.add)\
                    .then_inc(d_s, 1)

            def d_ruk(b, _):
                dve.wait_ge(b_kr, b + 1)
                for k in range(CT):
                    last = dve.scalar_tensor_tensor(RK[:, k, :], KR[:, 1, k, :], col("u", k), KR[:, 0, k, :],
                                                    ALU.mult, ALU.mult)
                last.then_inc(d_rk, 1)

            def d_rstate(b, _):
                dve.wait_ge(d_s, 2 * b + 1)
                r = KR[:, 1, 0, :].unsqueeze(1).to_broadcast([P, RS, T])
                dve.tensor_tensor(SS[:, 0], SS[:, 0], r, ALU.mult).then_inc(d_rs, 1)

            def d_own(b, _):
                dve.wait_ge(d_cps, b + 1)
                n = P // RS
                for t in range(CT):
                    last = dve.tensor_tensor(heads(CV[:, t * P:(t + 1) * P]),
                                             V8[:, t, :, :, 0].rearrange("p d h -> p h d"),
                                             over_tokens(PS_D[:, t * n:(t + 1) * n], n, RS), ALU.mult)
                last.then_inc(d_cv, 1)

            def d_output(b, _):
                dve.wait_ge(d_otps, b + 1)
                o = PS_D[:, :].rearrange("p (j t e h) -> p t h e j", j=4, t=CT, e=2)
                for t in range(CT):
                    last = dve.tensor_tensor(O[:, t * P:(t + 1) * P].rearrange("p (h e j) -> p h e j", e=2, j=4),
                                             o[:, t, 0:P // RS],
                                             CV[:, t * P:(t + 1) * P].rearrange("p (h e j) -> p h e j", e=2, j=4),
                                             ALU.add)
                last.then_inc(d_o, 1)

            def d_means(b, _):
                dve.wait_ge(d_o, b + 1)
                dve.tensor_reduce(GM[:, :], heads(O[:, :]), AX_X, ALU.add).then_inc(d_m, 1)

            def d_centre(b, _):
                dve.wait_ge(d_m, b + 1)
                dve.scalar_tensor_tensor(heads(O[:, :]), over_tokens(GM[:, :], RH, RS), -1.0 / RS, heads(O[:, :]),
                                         ALU.mult, ALU.add).then_inc(d_cen, 1)

            def d_spread(b, _):
                dve.wait_ge(d_sq, b + 1)
                dve.tensor_reduce(GV[:, :], heads(OQ[:, :]), AX_X, ALU.add).then_inc(d_v, 1)

            def d_guess(b, step):
                if step == 0:
                    dve.wait_ge(d_v, b + 1)
                    dve.tensor_scalar(GE[:, :], GV[:, :], 1.0 / RS, EPS, ALU.mult, ALU.add).then_inc(d_gr, 1)
                elif step == 1:
                    dve.wait_ge(d_gr, 12 * b + 1)
                    dve.tensor_scalar(GT[:, :].bitcast(I32), GE[:, :].bitcast(I32), 1, None,
                                      ALU.logical_shift_right).then_inc(d_gr, 1)
                else:
                    dve.wait_ge(d_gr, 12 * b + 2)
                    dve.tensor_scalar(GY[:, :].bitcast(I32), GT[:, :].bitcast(I32), -1.0, float(0x5F3759DF),
                                      ALU.mult, ALU.add).then_inc(d_gr, 1)

            def d_newton(b, arg):
                n, step = arg
                dve.wait_ge(d_gr, 12 * b + 3 * n + step + 3)
                if step == 0:
                    dve.scalar_tensor_tensor(GT[:, :], GY[:, :], -0.5, GE[:, :], ALU.mult, ALU.mult)\
                        .then_inc(d_gr, 1)
                elif step == 1:
                    dve.tensor_tensor(GT[:, :], GT[:, :], GY[:, :], ALU.mult).then_inc(d_gr, 1)
                else:
                    dve.scalar_tensor_tensor(GY[:, :], GT[:, :], 1.5, GY[:, :], ALU.add, ALU.mult)\
                        .then_inc(d_gr, 1)

            def d_norm(b, _):
                dve.wait_ge(d_gr, 12 * b + 12)
                dve.tensor_tensor(heads(O[:, :]), heads(O[:, :]), over_tokens(GY[:, :], RH, RS), ALU.mult)\
                    .then_inc(d_n, 1)

            def d_weight(b, _):
                dve.wait_ge(d_n, b + 1)
                dve.tensor_tensor(O[:, :], O[:, :], row("gn_w"), ALU.mult).then_inc(d_gw, 1)

            def d_bias(b, _):
                dve.wait_ge(d_gw, b + 1)
                dve.tensor_tensor(O[:, :], O[:, :], row("gn_b"), ALU.add).then_inc(d_gb, 1)

            def d_gated(b, _):
                dve.wait_ge(d_gb, b + 1)
                dve.wait_ge(b_g, b + 1)
                dve.scalar_tensor_tensor(Y[:, :], O[:, :], 0.5, G[:, :], ALU.mult, ALU.mult).then_inc(d_y, 1)

            def d_sum(b, _):
                dve.wait_ge(d_wops, b + 1)
                dve.tensor_tensor(X[:, b, :], PS_D[:, 0:C], X[:, b, :], ALU.add).then_inc(d_res, 1)

            def d_stats(b, _):
                dve.wait_ge(d_res, b + 1)
                row_stats(b, d_stat, D_ST)

            def d_moments(b, _):
                moments(b, d_stat, D_ST, D_MV)

            def d_variance(b, _):
                variance(b, d_stat, d_var, D_ST, D_MV)

            def d_normal(b, _):
                dve.wait_ge(d_rstd, b + 1)
                normalise(b, D_MV, D_RS, D_N).then_inc(d_nrm, 1)

            def d_shift(b, _):
                dve.wait_ge(d_first, b + 1)
                dve.wait_ge(d_ln, b + 1)
                dve.tensor_tensor(SM[:, :, :], XM[:, :, 0:T], XM[:, :, 1:T + 1], ALU.subtract).then_inc(d_sx, 1)

            def d_mixed(b, _):
                dve.wait_ge(d_sx, b + 1)
                for dst, name in ((XK, "fmk"), (XR, "fmr")):
                    for t in range(CT):
                        last = dve.scalar_tensor_tensor(dst[:, t, :], SM[:, t, :], col(name, t), XM[:, t, 1:T + 1],
                                                        ALU.mult, ALU.add)
                last.then_inc(d_xkr, 1)

            def d_mixing(b, _):
                dve.wait_ge(d_rr, b + 1)
                dve.wait_ge(d_fps, b + 1)
                dve.scalar_tensor_tensor(RR[:, :], RR[:, :], 1.0, PS_D[:, 0:C], ALU.add, ALU.mult).then_inc(d_f, 1)

            def d_final(b, _):
                dve.wait_ge(d_f, b + 1)
                dve.scalar_tensor_tensor(X[:, b, :], RR[:, :], 0.5, X[:, b, :], ALU.mult, ALU.add)\
                    .then_inc(d_fin, 1)

            pieces = named(a_stats, a_moments, a_variance, a_normal, a_val, a_key, a_mask, a_maxima, a_inverse, a_sum,
                           b_stats, b_moments, b_variance, b_normal, b_hidden, b_affine, b_gelu, b_sum, b_shift,
                           b_mixed, b_streams, b_gate, d_outer, d_scan, d_ruk, d_rstate, d_own, d_output, d_means,
                           d_centre, d_spread, d_guess, d_newton, d_norm, d_weight, d_bias, d_gated, d_sum, d_stats,
                           d_moments, d_variance, d_normal, d_shift, d_mixed, d_mixing, d_final)
            run(pieces, DVE_ORDER, 0)
            dve.wait_ge(in_rest, IN_REST)
            for i in range(1, PEEL):
                run(pieces, DVE_ORDER, i)
            with dve.Fori(PEEL, B) as i:
                run(pieces, DVE_ORDER, i)
            for i in range(B, B + LAG):
                run(pieces, DVE_ORDER, i)

        @block.scalar
        def _(act):
            act.wait_ge(in_first, IN_FIRST)
            act.wait_ge(set_dve, 3)

            def turned(dst, src, s, bias):
                for t in range(CT):
                    last = act.activation(dst[:, t, :], src[:, t * T:(t + 1) * T], ACT.Identity,
                                          bias=col(bias, t), scale=col(s, t))
                return last

            def a_enc_copy(b, _):
                act.wait_ge(a_encps, b + 1)
                act.wait_ge(a_prev, b)
                act.activation(A_ET[:, :, :], tiles(turns), ACT.Copy).then_inc(a_enc, 1)

            def a_scale(b, a):
                act.wait_ge(a_lnps, 2 * b + a + 1)
                turned(A_LT, turns, f"ln{a + 1}_s", f"ln{a + 1}_b").then_inc(a_ln, 1)

            def a_query(b, a):
                act.wait_ge(a_qps, 2 * b + a + 1)
                for par in range(2):
                    for t in range(CT):
                        last = act.activation(QP[:, par, t, :], queries[:, t * T:(t + 1) * T], ACT.Identity,
                                              bias=QB[:, a, par, t:t + 1], scale=CST[:, K_PAR + par:K_PAR + par + 1])
                last.then_inc(a_q, 1)

            def a_exps(b, arg):
                a, g = arg
                act.wait_ge(a_max, 8 * b + 4 * a + g + 1)
                for j in range(GH):
                    h = GH * g + j
                    last = act.activation(SC[:, g, j, :], SC[:, g, j, :], ACT.Exp, bias=NMX[:, h:h + 1],
                                          accum_out=SUM[:, h:h + 1])
                last.then_inc(a_exp, 1)

            def a_prob_copy(b, arg):
                a, g = arg
                act.wait_ge(a_turned, 8 * b + 4 * a + g + 1)
                act.activation(PT[:, g], PS_T[:, g % 2].rearrange("p (j n) -> p j n", n=T), ACT.Copy)\
                    .then_inc(a_pt, 1)

            def a_ctx_copy(b, a):
                act.wait_ge(a_pvps, 2 * b + a + 1)
                act.activation(CTX[:, :, :], tiles(PS_T[:, 0, 0:C]), ACT.Copy).then_inc(a_ctx, 1)

            def b_scale(b, k):
                act.wait_ge(b_lnps, 2 * b + k + 1)
                if k:
                    turned(XN[:, :, 1:T + 1], PS_B[:, 0], "r1_w", "r1_b").then_inc(b_ln, 1)
                else:
                    turned(B_LT, PS_B[:, 0], "ln3_s", "ln3_b").then_inc(b_ln, 1)

            def b_square(b, k):
                h = slice(k * FT // 2, (k + 1) * FT // 2)
                act.wait_ge(b_hx, 2 * b + k + 1)
                act.activation(HQ[:, h, :], HX[:, h, :], ACT.Square).then_inc(b_sq, 1)

            def b_tanhs(b, k):
                h = slice(k * FT // 2, (k + 1) * FT // 2)
                act.wait_ge(b_cube, 2 * b + k + 1)
                act.activation(HQ[:, h, :], HQ[:, h, :], ACT.Tanh).then_inc(b_tanh, 1)

            def b_low(b, _):
                act.wait_ge(b_m1ps, b + 1)
                act.activation(MT[:, :, :], tiles(PS_B[:, 1, 0:C]), ACT.Tanh).then_inc(b_mt, 1)

            def b_decay1(b, _):
                act.wait_ge(b_d1ps, b + 1)
                act.activation(DT[0:DE, :], PS_B[0:DE, 1, 0:T], ACT.Tanh).then_inc(b_dt, 1)

            def b_keyrec(b, _):
                act.wait_ge(b_krps, b + 1)
                act.wait_ge(d_rs, 2 * b)
                act.wait_ge(d_rk, b)
                act.activation(KR[:, :, :, :].rearrange("p a t n -> p (a t n)"), PS_B[:, 0, :], ACT.Copy)\
                    .then_inc(b_kr, 1)

            def b_decay2(b, _):
                act.wait_ge(b_d2ps, b + 1)
                for t in range(CT):
                    last = act.activation(EW[:, t, :], PS_B[:, 1, t * T:(t + 1) * T], ACT.Exp, bias=col("td", t))
                last.then_inc(b_ew, 1)

            def b_decays(b, _):
                act.wait_ge(b_ew, b + 1)
                act.wait_ge(d_s, 2 * b)
                for t in range(CT):
                    e = EW[:, t, 0:T - 1].unsqueeze(1).to_broadcast([P, RS, T - 1])
                    last = act.activation(W8[:, t, :, 1:T], e, ACT.Exp, scale=-1.0)
                last.then_inc(b_w8, 1)

            def b_valgate(b, _):
                act.wait_ge(b_vgps, b + 1)
                act.wait_ge(d_cv, b)
                for t in range(CT):
                    v = heads(PS_B[:, 0, t * P:(t + 1) * P]).rearrange("p h d -> p d h").unsqueeze(3)
                    last = act.activation(V8[:, t], v.to_broadcast([P, RS, P // RS, RS]), ACT.Copy)
                last.then_inc(b_v, 1)
                act.activation(TG[:, :], PS_B[:, 0, C:2 * C], ACT.Tanh, scale=0.5).then_inc(b_tg, 1)

            def d_ocopy(b, _):
                act.wait_ge(d_ops, b + 1)
                act.activation(OH[:, :, :].rearrange("p j n -> p (j n)"), PS_D[:, :], ACT.Copy).then_inc(d_oh, 1)

            def d_ycopy(b, _):
                act.wait_ge(d_yps, b + 1)
                act.activation(YT[:, :, :], tiles(PS_D[:, 0:C]), ACT.Copy).then_inc(d_yt, 1)

            def d_scale(b, _):
                act.wait_ge(d_lnps, b + 1)
                turned(XM[:, :, 1:T + 1], PS_D[:, 0:C], "r2_w", "r2_b").then_inc(d_ln, 1)

            def d_keyrec(b, _):
                act.wait_ge(d_krps, b + 1)
                act.activation(RL[:, :, :], tiles(PS_D[:, 0:C]), ACT.Relu).then_inc(d_relu, 1)
                act.activation(RR[:, :], PS_D[:, C:2 * C], ACT.Tanh, scale=0.5).then_inc(d_rr, 1)

            pieces = named(a_enc_copy, a_scale, a_query, a_exps, a_prob_copy, a_ctx_copy,
                           b_scale, b_square, b_tanhs, b_low, b_decay1, b_keyrec, b_decay2, b_decays, b_valgate,
                           d_ocopy, d_ycopy, d_scale, d_keyrec)
            for i in range(PEEL):
                run(pieces, ACT_ORDER, i)
            with act.Fori(PEEL, B) as i:
                run(pieces, ACT_ORDER, i)
            for i in range(B, B + LAG):
                run(pieces, ACT_ORDER, i)

        @block.gpsimd
        def _(pool):
            pool.wait_ge(in_first, IN_FIRST)
            pool.tensor_scalar(MADD[:, B, :], MASK[:, B, :], -1.0, 1.0, ALU.mult, ALU.add).then_inc(set_pool, 1)
            pool.wait_ge(set_pool, 1)
            pool.tensor_scalar(MADD[:, B, :], MADD[:, B, :], -10000.0, 0.0, ALU.mult, ALU.add)\
                .then_inc(set_pool, 1)

            def inverse_root(ST, RS_):
                return pool.tensor_tensor(RS_[:, 0:1], ST[:, 0:1], CST[:, K_POW:K_POW + 1], ALU.pow)

            def a_root(b, a):
                pool.wait_ge(a_var, 2 * b + a + 1)
                inverse_root(A_ST, A_RS).then_inc(a_rstd, 1)

            def a_addbias(b, a):
                pool.wait_ge(a_nrm, 2 * b + a + 1)
                pool.sem_inc(passed_pool, 1)
                pool.tensor_tensor(X[:, b, :], X[:, b, :], row("co" if a else "ao"), ALU.add).then_inc(a_bias, 1)

            def a_before(b, _):
                pool.wait_ge(a_enc, b + 1)
                pool.tensor_copy(PREV[:, b, :, :], A_ET[:, :, 0:2]).then_inc(a_prev, 1)

            def a_addmask(b, arg):
                a, g = arg
                if not later(b) and a and g == 0:
                    pool.wait_ge(in_rest, IN_REST)
                    pool.tensor_scalar(MADD[:, 0:B, :], MASK[:, 0:B, :], -1.0, 1.0, ALU.mult, ALU.add)\
                        .then_inc(set_pool, 1)
                    pool.wait_ge(set_pool, 3)
                    pool.tensor_scalar(MADD[:, 0:B, :], MADD[:, 0:B, :], -10000.0, 0.0, ALU.mult, ALU.add)\
                        .then_inc(set_pool, 1)
                    pool.wait_ge(set_pool, 4)
                pool.wait_ge(a_masked, 8 * b + 4 * a + g + 1)
                if a:
                    pool.sem_inc(passed_pool, 1)
                    pool.tensor_tensor(SC[:, g], SC[:, g], over_heads(MADD[:, b, :]), ALU.add).then_inc(a_added, 1)
                else:
                    pool.tensor_tensor(SC[:, g], SC[:, g], over_heads(MADD[:, B, :]), ALU.add).then_inc(a_added, 1)

            def a_divide(b, arg):
                a, g = arg
                pool.wait_ge(a_inv, 8 * b + 4 * a + g + 1)
                pool.tensor_tensor(SC[:, g], SC[:, g], over_tokens(RINV[:, GH * g:GH * g + GH], GH), ALU.mult)\
                    .then_inc(a_prob, 1)

            def b_root(b, k):
                pool.wait_ge(b_var, 2 * b + k + 1)
                inverse_root(B_ST, B_RS).then_inc(b_rstd, 1)

            def b_addbias(b, _):
                pool.wait_ge(b_nrm, 2 * b + 1)
                pool.sem_inc(passed_pool, 1)
                pool.tensor_tensor(X[:, b, :], X[:, b, :], row("b2"), ALU.add).then_inc(b_bias, 1)
                pool.wait_ge(b_sx, b)
                pool.wait_ge(a_prev, b + 1)
                pool.tensor_copy(XN[:, :, 0:1], PREV[:, b, :, 1:2]).then_inc(b_first, 1)

            def b_cubes(b, k):
                h = slice(k * FT // 2, (k + 1) * FT // 2)
                pool.wait_ge(b_aff, 2 * b + k + 1)
                pool.tensor_tensor(HQ[:, h, :], HQ[:, h, :], HX[:, h, :], ALU.mult).then_inc(b_cube, 1)

            def b_addnorm(b, n):
                pool.wait_ge(b_mix, 3 * b + n + 1)
                for i in MIX_TURNS[n]:
                    last = pool.tensor_tensor(MX[:, i], MX[:, i], XN[:, :, 1:T + 1], ALU.add)
                last.then_inc(b_mx, 1)

            def d_first_states(b, _):
                pool.wait_ge(d_s, 2 * b)
                pool.tensor_copy(AJ[:, :, :, 0:1], S0[:, b, :, :].unsqueeze(3)).then_inc(d_s0, 1)

            def d_rstate(b, _):
                pool.wait_ge(d_s, 2 * b + 2)
                r = KR[:, 1, 1, :].unsqueeze(1).to_broadcast([P, RS, T])
                pool.tensor_tensor(SS[:, 1], SS[:, 1], r, ALU.mult).then_inc(d_rs, 1)

            def d_squares(b, _):
                pool.wait_ge(d_cen, b + 1)
                pool.tensor_tensor(OQ[:, :], O[:, :], O[:, :], ALU.mult).then_inc(d_sq, 1)

            def d_root(b, _):
                pool.wait_ge(d_var, b + 1)
                inverse_root(D_ST, D_RS).then_inc(d_rstd, 1)

            def d_before(b, _):
                pool.wait_ge(d_sx, b)
                pool.tensor_copy(XM[:, :, 0:1], PREV[:, b, :, 0:1]).then_inc(d_first, 1)

            def d_relu2(b, _):
                pool.wait_ge(d_relu, b + 1)
                pool.tensor_tensor(KK[:, :, :], RL[:, :, :], RL[:, :, :], ALU.mult).then_inc(d_kk, 1)

            pieces = named(a_root, a_addbias, a_before, a_addmask, a_divide, b_root, b_addbias, b_cubes, b_addnorm,
                           d_first_states, d_rstate, d_squares, d_root, d_before, d_relu2)
            run(pieces, POOL_ORDER, 0)
            pool.wait_ge(in_wb, IN_WB)
            w2 = W[:, W_AT["w2"]:W_AT["w2"] + FT * C]
            pool.tensor_scalar(w2, w2, 0.5, 0.0, ALU.mult, ALU.add).then_inc(set_pool, 1)
            for i in range(1, PEEL):
                run(pieces, POOL_ORDER, i)
            with pool.Fori(PEEL, B) as i:
                run(pieces, POOL_ORDER, i)
            for i in range(B, B + LAG):
                run(pieces, POOL_ORDER, i)


def kernel(**inputs):
    import concourse.bacc as _bacc
    from concourse.bass_utils import run_bass_kernel_spmd as _run

    a = {k: np.asarray(v) for k, v in inputs.items()}

    def l0(n):
        return a["L0_xattn_" + n]

    def l1(n):
        return a["L1_xattn_" + n]

    def packed(m):
        k = m.shape[0] // P
        return m.reshape(k, P, m.shape[1]).transpose(1, 0, 2).reshape(P, -1)

    def padded(m, shape, at=0):
        out = np.zeros(shape, m.dtype)
        out[at:at + m.shape[0], :m.shape[1]] = m
        return out

    parts = {
        "qkv": packed(l0("w_qkv")), "ao": packed(l0("w_ao")), "q": packed(l0("w_q")), "kv": packed(l0("w_kv")),
        "co": packed(l0("w_co")), "w1": packed(l0("w1")), "w2": packed(l0("w2")),
        "maa1": packed(padded(l1("maa_w1"), (C, C))),
        "maa2": np.concatenate([padded(l1("maa_w2")[i], (P, C), i * ME % P) for i in range(MIX)], axis=1),
        "dec1": packed(l1("decay_w1")), "dec2": padded(l1("decay_w2"), (P, C)),
        "r": packed(l1("Wr").T), "k": packed(l1("Wk").T), "v": packed(l1("Wv").T), "g": packed(l1("Wg").T),
        "o": packed(l1("Wo").T), "fk": packed(l1("ffn_Wk").T), "fr": packed(l1("ffn_Wr").T),
        "fv": packed(l1("ffn_Wv").T)}
    weights = np.concatenate([parts[name] for name, _ in WEIGHTS], axis=1)
    vectors = {
        "ln1_s": l0("ln1_s"), "ln1_b": l0("ln1_b"), "bq0": l0("b_qkv")[0:C], "bk0": l0("b_qkv")[C:2 * C],
        "ln2_s": l0("ln2_s"), "ln2_b": l0("ln2_b"), "bq1": l0("b_q"), "bk1": l0("b_kv")[0:C],
        "ln3_s": l0("ln3_s"), "ln3_b": l0("ln3_b"), "b1": l0("b1"), "r1_w": l1("ln1_w"), "r1_b": l1("ln1_b"),
        "maa_x": l1("maa_x"), "stack": l1("maa_stack"), "td": l1("time_decay"), "u": l1("faaaa"),
        "r2_w": l1("ln2_w"), "r2_b": l1("ln2_b"), "fmk": l1("ffn_maa_k"), "fmr": l1("ffn_maa_r")}
    cols = np.concatenate([vectors[name].reshape(-1, P) for name, _ in COLS], axis=0)
    by_row = {"bv0": l0("b_qkv")[2 * C:], "ao": l0("b_ao"), "bv1": l0("b_kv")[C:], "co": l0("b_co"), "b2": l0("b2"),
              "gn_w": l1("gn_w"), "gn_b": l1("gn_b")}
    rows = np.stack([by_row[name] for name in ROWS])
    consts = np.zeros((P, K_END), np.float32)
    for p in range(P):
        consts[p, K_ID + p] = 1.0
        consts[p, K_SEL + p // RS] = 1.0
        consts[p, K_PAR + (p // HD) % 2] = 1.0 / HD ** 0.5
    consts[:, K_POW] = -0.5

    arrays = {"x": a["x"], "enc": a["ctx_2048"], "mask_self": a["mask_1x1xSxS2_fc1"].reshape(T, T),
              "mask_cross": a["mask_Bx1xSxS2_ff1"].reshape(B, T, T), "weights": weights, "cols": cols, "rows": rows,
              "consts": consts}
    nc = _bacc.Bacc("TRN2", target_bir_lowering=False, num_devices=1)
    args, ins = {}, {}
    for name, v in arrays.items():
        v = np.ascontiguousarray(v)
        ins[f"in_{name}"] = v
        args[name] = nc.dram_tensor(f"in_{name}", v.shape, mybir.dt.from_np(v.dtype), kind="ExternalInput").ap()
    args["out"] = nc.dram_tensor("out_0", (B, T, C), F32, kind="ExternalOutput").ap()
    build(nc, **args)
    r = _run(nc, [ins], core_ids=[0])
    return r.results[0]["out_0"]
```

```python
from contextlib import ExitStack

import numpy as np

import concourse.bass as bass
from concourse import mybir

F32 = mybir.dt.float32
I32 = mybir.dt.int32
ALU = mybir.AluOpType
ACT = mybir.ActivationFunctionType
AX_X = mybir.AxisListType.X

B, T, C = 16, 128, 256
P = 128
CT = C // P
NH, HD = 16, 16
RH, RS = 32, 8
F = 4 * C
FT = F // P
MIX, ME = 5, 32
DE = 64
GRP, GH = 4, 4
EPS = 1e-5
GELU_C, GELU_A = 0.7978845608028654, 0.044715

WEIGHTS = [("qkv", CT * 3 * C), ("ao", CT * C), ("q", CT * C), ("kv", CT * 2 * C), ("co", CT * C),
           ("w1", CT * F), ("w2", FT * C), ("maa1", CT * C), ("maa2", MIX * C), ("dec1", CT * DE), ("dec2", C),
           ("r", CT * C), ("k", CT * C), ("v", CT * C), ("g", CT * C),
           ("o", CT * C), ("fk", CT * C), ("fr", CT * C), ("fv", CT * C)]
W_AT, W_END = {}, 0
for _name, _n in WEIGHTS:
    W_AT[_name] = W_END
    W_END += _n
W_CUT1, W_CUT2 = W_AT["w1"], W_AT["o"]

COLS = [("ln1_s", 2), ("ln1_b", 2), ("bq0", 2), ("bk0", 2), ("ln2_s", 2), ("ln2_b", 2), ("bq1", 2), ("bk1", 2),
        ("ln3_s", 2), ("ln3_b", 2), ("b1", 8), ("r1_w", 2), ("r1_b", 2), ("maa_x", 2), ("stack", 10), ("td", 2),
        ("u", 2), ("r2_w", 2), ("r2_b", 2), ("fmk", 2), ("fmr", 2)]
C_AT, C_END = {}, 0
for _name, _n in COLS:
    C_AT[_name] = C_END
    C_END += _n
ROWS = ["bv0", "ao", "bv1", "co", "b2", "gn_w", "gn_b"]
K_ID, K_SEL, K_PAR, K_POW, K_END = 0, P, P + 32, P + 34, P + 35

MIX_TURNS = [(1, 0), (3, 2), (4,)]

SP_ORDER = [
    ("a_load", 0, 0), ("d_store", 0, 4)]
PE_ORDER = [
    ("a_val", 1, 1), ("b_keyrec", 0, 3), ("b_keyrec", 1, 3), ("a_prob_turn", (0, 0), 1), ("b_decay2", 0, 3),
    ("b_valgate", 0, 3), ("a_prob_turn", (0, 1), 1), ("b_valgate", 1, 3), ("a_prob_turn", (0, 2), 1),
    ("a_prob_turn", (0, 3), 1), ("a_key", 1, 1), ("a_pv", 0, 1), ("d_yturn", 0, 4), ("a_out", 0, 1),
    ("b_turn", 0, 2), ("d_out", 0, 4), ("b_mlp1", 0, 2), ("a_turn", 1, 1), ("d_turn", 0, 4), ("a_query", 1, 1),
    ("b_mlp1", 1, 2), ("d_keyrec", 0, 4), ("a_scores", (1, 0), 1), ("d_keyrec", 1, 4), ("a_scores", (1, 1), 1),
    ("a_scores", (1, 2), 1), ("a_scores", (1, 3), 1), ("d_val", 0, 4), ("a_turn", 0, 0), ("b_mlp2", 0, 2),
    ("d_vturn", 0, 3), ("b_mlp2", 1, 2), ("d_vturn", 1, 3), ("a_val", 0, 0), ("a_key", 0, 0), ("d_vturn", 2, 3),
    ("a_prob_turn", (1, 0), 1), ("a_prob_turn", (1, 1), 1), ("b_turn", 1, 2), ("d_vturn", 3, 3),
    ("a_prob_turn", (1, 2), 1), ("a_prob_turn", (1, 3), 1), ("a_query", 0, 0), ("d_own", 0, 3), ("a_pv", 1, 1),
    ("b_low1", 0, 2), ("a_scores", (0, 0), 0), ("a_scores", (0, 1), 0), ("b_low2", 0, 2),
    ("a_scores", (0, 2), 0), ("a_scores", (0, 3), 0), ("b_low2", 1, 2), ("d_read", 0, 3), ("b_low2", 2, 2),
    ("a_enc_turn", 0, 0), ("d_oturn", 0, 3), ("a_out", 1, 1), ("b_decay1", 0, 2)]
DVE_ORDER = [
    ("d_newton", (0, 1), 4), ("a_inverse", (0, 3), 1), ("b_moments", 0, 2), ("d_newton", (0, 2), 4),
    ("d_newton", (1, 0), 4), ("d_newton", (1, 1), 4), ("d_newton", (1, 2), 4), ("d_newton", (2, 0), 4),
    ("d_newton", (2, 1), 4), ("d_newton", (2, 2), 4), ("d_gated", 0, 4), ("b_normal", 0, 2), ("b_gate", 0, 3),
    ("a_sum", 0, 1), ("a_stats", 1, 1), ("a_moments", 1, 1), ("d_sum", 0, 4), ("d_stats", 0, 4),
    ("d_moments", 0, 4), ("a_normal", 1, 1), ("a_stats", 0, 0), ("d_normal", 0, 4), ("a_val", 1, 1),
    ("b_hidden", 0, 2), ("d_ruk", 0, 3), ("d_shift", 0, 4), ("d_mixed", 0, 4), ("a_key", 1, 1),
    ("a_moments", 0, 0), ("b_cubes", 0, 2), ("d_mixed", 1, 4), ("a_normal", 0, 0), ("b_hidden", 1, 2),
    ("a_mask", (1, 0), 1), ("b_cubes", 1, 2), ("b_gelu", 0, 2), ("a_mask", (1, 1), 1), ("a_maxima", (1, 0), 1),
    ("b_gelu", 1, 2), ("a_mask", (1, 2), 1), ("a_maxima", (1, 1), 1), ("d_mixing", 0, 4), ("a_mask", (1, 3), 1),
    ("a_inverse", (1, 0), 1), ("a_maxima", (1, 2), 1), ("d_outer", 0, 3), ("a_maxima", (1, 3), 1),
    ("a_inverse", (1, 1), 1), ("b_sum", 0, 2), ("b_stats", 1, 2), ("b_moments", 1, 2), ("d_outer", 1, 3),
    ("a_inverse", (1, 2), 1), ("b_normal", 1, 2), ("a_inverse", (1, 3), 1), ("d_outer", 2, 3), ("d_scan", 0, 3),
    ("d_outer", 3, 3), ("b_shift", 0, 2), ("a_key", 0, 0), ("b_mixed", 0, 2), ("d_scan", 1, 3), ("a_val", 0, 0),
    ("d_rstate", 0, 3), ("a_mask", (0, 0), 0), ("a_mask", (0, 1), 0), ("d_own", 0, 3), ("b_streams", 0, 2),
    ("a_maxima", (0, 0), 0), ("a_mask", (0, 2), 0), ("a_maxima", (0, 1), 0), ("a_mask", (0, 3), 0),
    ("b_streams", 1, 2), ("b_streams", 2, 2), ("a_maxima", (0, 2), 0), ("d_output", 0, 3), ("d_means", 0, 3),
    ("a_inverse", (0, 0), 0), ("a_inverse", (0, 1), 0), ("d_final", 0, 4), ("a_maxima", (0, 3), 0),
    ("d_centre", 0, 3), ("a_sum", 1, 1), ("b_stats", 0, 1), ("d_spread", 0, 3), ("a_inverse", (0, 2), 0),
    ("d_guess", 0, 3), ("d_guess", 1, 3), ("d_guess", 2, 3), ("d_newton", (0, 0), 3)]
ACT_ORDER = [
    ("a_exps", (0, 2, 0), 1), ("a_exps", (0, 2, 1), 1), ("a_exps", (0, 3, 0), 1), ("b_keyrec", 0, 3),
    ("a_exps", (0, 3, 1), 1), ("a_prob_copy", (0, 0), 1), ("a_prob_copy", (0, 1), 1), ("b_decay2", 0, 3),
    ("a_prob_copy", (0, 2), 1), ("a_prob_copy", (0, 3), 1), ("b_values", 0, 3), ("b_values", 1, 3),
    ("a_ctx_copy", 0, 1), ("b_gatetanh", 0, 3), ("d_ycopy", 0, 4), ("b_scale", 0, 2), ("b_decays", 0, 3),
    ("a_scale", 1, 1), ("d_scale", 0, 4), ("b_square", 0, 2), ("a_query", (1, 0), 1), ("a_query", (1, 1), 1),
    ("b_tanhs", 0, 2), ("b_square", 1, 2), ("d_keyrec", 0, 4), ("b_tanhs", 1, 2), ("a_exps", (1, 0, 0), 1),
    ("a_exps", (1, 0, 1), 1), ("a_exps", (1, 1, 0), 1), ("a_scale", 0, 0), ("a_exps", (1, 1, 1), 1),
    ("a_exps", (1, 2, 0), 1), ("a_exps", (1, 2, 1), 1), ("a_exps", (1, 3, 0), 1), ("a_exps", (1, 3, 1), 1),
    ("a_prob_copy", (1, 0), 1), ("a_prob_copy", (1, 1), 1), ("b_scale", 1, 2), ("a_prob_copy", (1, 2), 1),
    ("a_prob_copy", (1, 3), 1), ("a_query", (0, 0), 0), ("a_query", (0, 1), 0), ("b_low", 0, 2),
    ("a_ctx_copy", 1, 1), ("a_exps", (0, 0, 0), 0), ("a_exps", (0, 0, 1), 0), ("d_ocopy", 0, 3),
    ("a_exps", (0, 1, 0), 0), ("a_exps", (0, 1, 1), 0), ("a_enc_copy", 0, 0), ("b_decay1", 0, 2)]
POOL_ORDER = [
    ("a_divide", (0, 0), 1), ("d_squares", 0, 4), ("a_divide", (0, 1), 1), ("a_divide", (0, 2), 1),
    ("a_divide", (0, 3), 1), ("d_norm", 0, 4), ("d_first_states", 0, 3), ("d_weight", 0, 4), ("d_bias", 0, 4),
    ("b_root", 0, 2), ("b_addbias", 0, 2), ("a_root", 1, 1), ("d_root", 0, 4), ("a_before", 0, 1),
    ("a_root", 0, 0), ("d_before", 0, 3), ("a_addbias", 1, 1), ("a_addbias", 0, 0), ("a_addmask", (1, 0), 1),
    ("d_relu2", 0, 4), ("a_addmask", (1, 1), 1), ("a_addmask", (1, 2), 1), ("a_addmask", (1, 3), 1),
    ("a_divide", (1, 0), 1), ("a_divide", (1, 1), 1), ("b_root", 1, 2), ("a_divide", (1, 2), 1),
    ("a_divide", (1, 3), 1), ("d_rstate", 0, 3), ("a_addmask", (0, 0), 0), ("a_addmask", (0, 1), 0),
    ("b_addnorm", 0, 2), ("a_addmask", (0, 2), 0), ("a_addmask", (0, 3), 0), ("b_addnorm", 1, 2),
    ("b_addnorm", 2, 2)]

LAG = max(lag for order in (SP_ORDER, PE_ORDER, DVE_ORDER, ACT_ORDER, POOL_ORDER) for _, _, lag in order)
PEEL = LAG + 1


def build(nc, x, enc, mask_self, mask_cross, weights, cols, rows, consts, out):
    with ExitStack() as ctx:
        def sb(name, shape):
            return ctx.enter_context(nc.sbuf_tensor(name, [P, *shape], F32))

        def pb(name, shape):
            return ctx.enter_context(nc.psum_tensor(name, [P, *shape], F32))

        X = sb("X", [B, C])
        MASK = sb("MASK", [B + 1, T])
        MADD = sb("MADD", [B + 1, T])
        S0 = sb("S0", [B, CT, RS])
        PREV = sb("PREV", [B, CT, 2])
        W = sb("W", [W_END])
        CRAW = sb("CRAW", [P])
        COL = sb("COL", [C_END])
        ROW = sb("ROW", [len(ROWS), C])
        CST = sb("CST", [K_END])
        QB = sb("QB", [2, 2, CT])
        A_ST, A_MV, A_RS = sb("A_ST", [6]), sb("A_MV", [2]), sb("A_RS", [1])
        A_N = sb("A_N", [C])
        A_LT = sb("A_LT", [CT, T])
        ENC = sb("ENC", [C])
        A_ET = sb("A_ET", [CT, T])
        QP = sb("QP", [2, CT, T])
        KT = sb("KT", [CT, T])
        VP = sb("VP", [NH // 2, 2, 2 * HD])
        SC = sb("SC", [GRP, GH, T])
        NMX, SUM, RINV = sb("NMX", [NH]), sb("SUM", [NH]), sb("RINV", [NH])
        PT = sb("PT", [GRP, GH, T])
        CTX = sb("CTX", [CT, T])
        B_ST, B_MV, B_RS = sb("B_ST", [6]), sb("B_MV", [2]), sb("B_RS", [1])
        B_N = sb("B_N", [C])
        B_LT = sb("B_LT", [CT, T])
        HX, HQ, HG = sb("HX", [FT, T]), sb("HQ", [FT, T]), sb("HG", [FT, T])
        XN, SX, XX = sb("XN", [CT, T + 1]), sb("SX", [CT, T]), sb("XX", [CT, T])
        MT = sb("MT", [CT, T])
        MX = sb("MX", [MIX, CT, T])
        DT, EW = sb("DT", [T]), sb("EW", [CT, T])
        TG = sb("TG", [C])
        W8 = sb("W8", [CT, RS, T])
        KR = sb("KR", [2, CT, T])
        V8 = sb("V8", [CT, RS, P // RS, RS])
        G = sb("G", [C])
        AJ = sb("AJ", [CT, RS, T])
        SS = sb("SS", [CT, RS, T])
        RK = sb("RK", [CT, T])
        O, OQ = sb("O", [C]), sb("OQ", [C])
        OH = sb("OH", [GH, T])
        CV = sb("CV", [C])
        GM, GV, GE = sb("GM", [RH]), sb("GV", [RH]), sb("GE", [RH])
        GY, GT = sb("GY", [RH]), sb("GT", [RH])
        Y = sb("Y", [C])
        YT = sb("YT", [CT, T])
        D_ST, D_MV, D_RS = sb("D_ST", [6]), sb("D_MV", [2]), sb("D_RS", [1])
        D_N = sb("D_N", [C])
        XM, SM, XK, XR = sb("XM", [CT, T + 1]), sb("SM", [CT, T]), sb("XK", [CT, T]), sb("XR", [CT, T])
        RL, KK = sb("RL", [CT, T]), sb("KK", [CT, T])
        RR = sb("RR", [C])

        PS_S = pb("PS_S", [3, GH, T])
        PS_T = pb("PS_T", [2, 512])
        PS_B = pb("PS_B", [2, 512])
        PS_D = pb("PS_D", [512])

        def sem(name):
            return ctx.enter_context(nc.semaphore(name))

        in_enc = sem("in_enc")
        a_stat = sem("a_stat")
        a_var = sem("a_var")
        a_eps = sem("a_eps")
        a_rstd = sem("a_rstd")
        a_nrm = sem("a_nrm")
        a_lnps = sem("a_lnps")
        a_ln = sem("a_ln")
        a_bias = sem("a_bias")
        a_encps = sem("a_encps")
        a_enc = sem("a_enc")
        a_prev = sem("a_prev")
        a_kps = sem("a_kps")
        a_qps = sem("a_qps")
        a_v = sem("a_v")
        a_k = sem("a_k")
        a_q = sem("a_q")
        a_score = sem("a_score")
        a_masked = sem("a_masked")
        a_added = sem("a_added")
        a_max = sem("a_max")
        a_exp = sem("a_exp")
        a_inv = sem("a_inv")
        a_prob = sem("a_prob")
        a_turned = sem("a_turned")
        a_pt = sem("a_pt")
        a_pvps = sem("a_pvps")
        a_ctx = sem("a_ctx")
        a_ops = sem("a_ops")
        a_res = sem("a_res")
        b_stat = sem("b_stat")
        b_var = sem("b_var")
        b_eps = sem("b_eps")
        b_rstd = sem("b_rstd")
        b_nrm = sem("b_nrm")
        b_lnps = sem("b_lnps")
        b_ln = sem("b_ln")
        b_bias = sem("b_bias")
        b_up = sem("b_up")
        b_hx = sem("b_hx")
        b_sq = sem("b_sq")
        b_cube = sem("b_cube")
        b_tanh = sem("b_tanh")
        b_hg = sem("b_hg")
        b_dnps = sem("b_dnps")
        b_res = sem("b_res")
        b_first = sem("b_first")
        b_sx = sem("b_sx")
        b_xx = sem("b_xx")
        b_m1ps = sem("b_m1ps")
        b_mt = sem("b_mt")
        b_m2ps = sem("b_m2ps")
        b_mix = sem("b_mix")
        b_mx = sem("b_mx")
        b_d1ps = sem("b_d1ps")
        b_dt = sem("b_dt")
        b_d2ps = sem("b_d2ps")
        b_ew = sem("b_ew")
        b_w8 = sem("b_w8")
        b_krps = sem("b_krps")
        b_kr = sem("b_kr")
        b_vgps = sem("b_vgps")
        b_v = sem("b_v")
        b_tg = sem("b_tg")
        b_g = sem("b_g")
        d_s0 = sem("d_s0")
        d_vps = sem("d_vps")
        d_a = sem("d_a")
        d_s = sem("d_s")
        d_rs = sem("d_rs")
        d_rk = sem("d_rk")
        d_cps = sem("d_cps")
        d_cv = sem("d_cv")
        d_ops = sem("d_ops")
        d_oh = sem("d_oh")
        d_otps = sem("d_otps")
        d_o = sem("d_o")
        d_m = sem("d_m")
        d_cen = sem("d_cen")
        d_sq = sem("d_sq")
        d_v = sem("d_v")
        d_gr = sem("d_gr")
        d_n = sem("d_n")
        d_gw = sem("d_gw")
        d_gb = sem("d_gb")
        d_y = sem("d_y")
        d_yps = sem("d_yps")
        d_yt = sem("d_yt")
        d_wops = sem("d_wops")
        d_res = sem("d_res")
        d_stat = sem("d_stat")
        d_var = sem("d_var")
        d_eps = sem("d_eps")
        d_rstd = sem("d_rstd")
        d_nrm = sem("d_nrm")
        d_lnps = sem("d_lnps")
        d_ln = sem("d_ln")
        d_first = sem("d_first")
        d_sx = sem("d_sx")
        d_xkr = sem("d_xkr")
        d_krps = sem("d_krps")
        d_relu = sem("d_relu")
        d_kk = sem("d_kk")
        d_rr = sem("d_rr")
        d_fps = sem("d_fps")
        d_f = sem("d_f")
        d_fin = sem("d_fin")
        in_first = sem("in_first")
        in_wq = sem("in_wq")
        in_rows = sem("in_rows")
        in_wa = sem("in_wa")
        in_rest = sem("in_rest")
        in_states = sem("in_states")
        in_wb = sem("in_wb")
        in_wd = sem("in_wd")
        set_col = sem("set_col")
        set_dve = sem("set_dve")
        set_w2 = sem("set_w2")
        set_self = sem("set_self")
        set_cross = sem("set_cross")
        passed_dve = sem("passed_dve")
        passed_pool = sem("passed_pool")
        stored = sem("stored")

        IN_FIRST, IN_WQ, IN_ROWS, IN_WA, IN_REST, IN_STATES, IN_WB, IN_WD = (16 * n for n in (3, 1, 2, 1, 2, 2, 1, 1))

        ident = CST[:, K_ID:K_ID + P]
        hsel = CST[:, K_SEL:K_SEL + P // RS]
        hsel32 = CST[:, K_SEL:K_SEL + 32]

        values, keys, turns, queries = (PS_S[:, k // 2].rearrange("p j n -> p (j n)")[:, k % 2 * C:(k % 2 + 1) * C]
                                        for k in range(4))

        def w(name, kt, n, lo, hi):
            at = W_AT[name] + kt * n
            return W[:, at + lo:at + hi]

        def col(name, k=0, n=1):
            return COL[:, C_AT[name] + k:C_AT[name] + k + n]

        def row(name):
            return ROW[:, ROWS.index(name), :]

        def over_tokens(ap, n, m=T):
            return ap.unsqueeze(2).to_broadcast([P, n, m])

        def over_heads(ap):
            return ap.unsqueeze(1).to_broadcast([P, GH, T])

        def heads(ap):
            return ap.rearrange("p (h d) -> p h d", d=RS)

        def tiles(ap):
            return ap.rearrange("p (t n) -> p t n", t=CT)

        def run(pieces, order, i):
            for name, arg, lag in order:
                if isinstance(i, int) and not 0 <= i - lag < B:
                    continue
                pieces[name](i - lag, arg)

        def later(b, a=0):
            return not (isinstance(b, int) and b == 0 and a == 0)

        def named(*functions):
            return {f.__name__: f for f in functions}

        block = ctx.enter_context(nc.Block())

        @block.sync
        def _(sp):
            sp.dma_start(X[:, 0, :], x[0]).then_inc(in_first, 16)
            sp.dma_start(CST[:, :], consts).then_inc(in_first, 16)
            sp.dma_start(CRAW[0:C_END, :], cols).then_inc(in_first, 16)
            sp.dma_start(W[:, 0:W_AT["ao"]], weights[:, 0:W_AT["ao"]]).then_inc(in_wq, 16)
            sp.dma_start(ROW[:, :, :], rows.unsqueeze(0).to_broadcast([P, len(ROWS), C])).then_inc(in_rows, 16)
            sp.dma_start(MASK[:, B, :], mask_self).then_inc(in_rows, 16)
            sp.dma_start(W[:, W_AT["ao"]:W_CUT1], weights[:, W_AT["ao"]:W_CUT1]).then_inc(in_wa, 16)
            sp.dma_start(ENC[:, :], enc[0]).then_inc(in_enc, 16)
            sp.dma_start(MASK[:, 0:B, :], mask_cross.rearrange("b q k -> q b k")).then_inc(in_rest, 16)
            sp.dma_start(X[:, 1:B, :], x[1:B].rearrange("b s c -> s b c")).then_inc(in_rest, 16)
            sp.dma_start(W[:, W_CUT1:W_CUT2], weights[:, W_CUT1:W_CUT2]).then_inc(in_wb, 16)
            flat = enc[:, 2:2 + RS, :].rearrange("b s c -> b (s c)")
            with nc.allow_non_contiguous_dma(reason="32-byte pieces of the first states"):
                for t in range(CT):
                    sp.dma_start(S0[:, :, t, :],
                                 flat[:, t * P * RS:(t + 1) * P * RS].rearrange("b (p d) -> p b d", d=RS))\
                      .then_inc(in_states, 16)
            sp.dma_start(W[:, W_CUT2:W_END], weights[:, W_CUT2:W_END]).then_inc(in_wd, 16)

            def d_store(b, _):
                sp.wait_ge(d_fin, b + 1)
                sp.dma_start(out[b], X[:, b, :]).then_inc(stored, 16)

            def a_load(b, _):
                if later(b):
                    sp.wait_ge(a_encps, b)
                    sp.dma_start(ENC[:, :], enc[b]).then_inc(in_enc, 16)

            pieces = named(a_load, d_store)
            for i in range(PEEL):
                run(pieces, SP_ORDER, i)
            with sp.Fori(PEEL, B) as i:
                run(pieces, SP_ORDER, i)
            for i in range(B, B + LAG):
                run(pieces, SP_ORDER, i)
            sp.wait_ge(stored, 16 * B)

        @block.tensor
        def _(pe):
            pe.wait_ge(in_first, IN_FIRST)
            pe.transpose(PS_D[:, 0:C_END], CRAW[0:C_END, :], CST[0:C_END, K_ID:K_ID + C_END]).then_inc(set_col, 1)

            def turn(dst, src):
                for t in range(CT):
                    last = pe.transpose(dst[:, t * P:(t + 1) * P], src[:, t * P:(t + 1) * P], ident)
                return last

            def to_channels(dst, name, n, lo, rhs, count=CT):
                for m in range(count):
                    for kt in range(CT):
                        last = pe.matmul(dst[:, m * T:(m + 1) * T], w(name, kt, n, lo + m * P, lo + (m + 1) * P),
                                         rhs[:, kt, 0:T], start=(kt == 0), stop=(kt == CT - 1))
                return last

            def to_tokens(dst, name, n, lo, lhs):
                for kt in range(CT):
                    last = pe.matmul(dst, lhs[:, kt, 0:T], w(name, kt, n, lo, lo + C),
                                     start=(kt == 0), stop=(kt == CT - 1))
                return last

            def a_enc_turn(b, _):
                pe.wait_ge(in_enc, 16 * b + 16)
                pe.wait_ge(a_masked, 8 * b + 2)
                turn(turns, ENC).then_inc(a_encps, 1)

            def a_turn(b, a):
                pe.wait_ge(a_nrm, 2 * b + a + 1)
                if a:
                    pe.wait_ge(a_enc, b + 1)
                elif later(b):
                    pe.wait_ge(a_masked, 8 * b - 2)
                turn(turns, A_N).then_inc(a_lnps, 1)

            def a_val(b, a):
                pe.wait_ge(a_masked, 8 * b + 4 * a)
                if a:
                    if not later(b):
                        pe.wait_ge(in_wa, IN_WA)
                    pe.wait_ge(a_enc, b + 1)
                    to_tokens(values, "kv", 2 * C, C, A_ET)
                else:
                    if not later(b):
                        pe.wait_ge(in_wq, IN_WQ)
                    pe.wait_ge(a_ln, 2 * b + 1)
                    to_tokens(values, "qkv", 3 * C, 2 * C, A_LT)

            def a_key(b, a):
                if a:
                    pe.wait_ge(a_enc, b + 1)
                    to_channels(keys, "kv", 2 * C, 0, A_ET).then_inc(a_kps, 1)
                else:
                    pe.wait_ge(a_ln, 2 * b + 1)
                    to_channels(keys, "qkv", 3 * C, C, A_LT).then_inc(a_kps, 1)

            def a_query(b, a):
                pe.wait_ge(a_ln, 2 * b + a + 1)
                if a:
                    to_channels(queries, "q", C, 0, A_LT).then_inc(a_qps, 1)
                else:
                    to_channels(queries, "qkv", 3 * C, 0, A_LT).then_inc(a_qps, 1)

            def a_scores(b, arg):
                a, g = arg
                if g == 0:
                    pe.wait_ge(a_v, 2 * b + a + 1)
                    pe.wait_ge(a_k, 2 * b + a + 1)
                    pe.wait_ge(a_q, 4 * b + 2 * a + 2)
                elif g == 3:
                    pe.wait_ge(a_masked, 8 * b + 4 * a + 1)
                for t in range(CT):
                    for par in range(2):
                        last = pe.matmul(PS_S[:, g % 3, 2 * t + par, :], QP[32 * g:32 * g + 32, par, t, :],
                                         KT[32 * g:32 * g + 32, t, :], start=True, stop=True)
                last.then_inc(a_score, 1)

            def a_prob_turn(b, arg):
                a, g = arg
                pe.wait_ge(a_prob, 8 * b + 4 * a + g + 1)
                if g == 0:
                    pe.wait_ge(a_ctx, 2 * b + a)
                elif g == 1:
                    pe.wait_ge(a_res, 2 * b + a)
                else:
                    pe.wait_ge(a_pt, 8 * b + 4 * a + g - 1)
                for j in range(GH):
                    last = pe.transpose(PS_T[:, g % 2, j * T:(j + 1) * T], SC[:, g, j, :], ident)
                last.then_inc(a_turned, 1)

            def a_pv(b, a):
                pe.wait_ge(a_pt, 8 * b + 4 * a + 4)
                for t in range(CT):
                    for par in range(2):
                        for g in range(GRP):
                            last = pe.matmul(PS_T[32 * g:32 * g + 32, 0, t * T:(t + 1) * T],
                                             VP[:, GRP * t + g, par, :], PT[:, g, 2 * t + par, :],
                                             start=(par == 0), stop=(par == 1), skip_group_check=True)
                last.then_inc(a_pvps, 1)

            def a_out(b, a):
                pe.wait_ge(a_ctx, 2 * b + a + 1)
                if not later(b, a):
                    pe.wait_ge(in_wa, IN_WA)
                to_tokens(PS_T[:, 1, 0:C], "co" if a else "ao", C, 0, CTX).then_inc(a_ops, 1)

            def b_turn(b, k):
                pe.wait_ge(b_nrm, 2 * b + k + 1)
                if k == 0:
                    pe.wait_ge(b_g, b)
                    pe.wait_ge(b_v, 2 * b)
                    pe.wait_ge(b_ew, b)
                turn(PS_B[:, 0, 0:C], B_N).then_inc(b_lnps, 1)

            def b_mlp1(b, k):
                if not later(b, k):
                    pe.wait_ge(in_wb, IN_WB)
                if k == 0:
                    pe.wait_ge(b_ln, 2 * b + 1)
                to_channels(PS_B[:, 1 - k, :], "w1", F, k * (F // 2), B_LT, FT // 2).then_inc(b_up, 1)

            def b_mlp2(b, k):
                if not later(b, k):
                    pe.wait_ge(set_w2, 1)
                pe.wait_ge(b_hg, 2 * b + k + 1)
                for kt in range(k * FT // 2, (k + 1) * FT // 2):
                    last = pe.matmul(PS_B[:, 1, 0:C], HG[:, kt, :], w("w2", kt, C, 0, C),
                                     start=(kt == 0), stop=(kt == FT - 1))
                if k:
                    last.then_inc(b_dnps, 1)

            def b_low1(b, _):
                pe.wait_ge(b_xx, b + 1)
                to_channels(PS_B[:, 1, 0:C], "maa1", C, 0, XX).then_inc(b_m1ps, 1)

            def b_low2(b, n):
                if n == 0:
                    pe.wait_ge(b_mt, b + 1)
                elif n == 2:
                    pe.wait_ge(b_mix, 3 * b + 1)
                for k, i in enumerate(MIX_TURNS[n]):
                    for m in range(CT):
                        last = pe.matmul(PS_B[:, n % 2, k * C + m * T:k * C + (m + 1) * T],
                                         w("maa2", i, C, m * P, (m + 1) * P), MT[:, i * ME // P, :],
                                         start=True, stop=True)
                last.then_inc(b_m2ps, 1)

            def b_decay1(b, _):
                pe.wait_ge(b_mx, 3 * b + 1)
                pe.wait_ge(b_mix, 3 * b + 2)
                for kt in range(CT):
                    last = pe.matmul(PS_B[0:DE, 1, 0:T], w("dec1", kt, DE, 0, DE), MX[:, 1, kt, :],
                                     start=(kt == 0), stop=(kt == CT - 1))
                last.then_inc(b_d1ps, 1)

            def b_keyrec(b, k):
                if k:
                    to_channels(PS_B[:, 0, C:2 * C], "r", C, 0, MX[:, 3]).then_inc(b_krps, 1)
                else:
                    pe.wait_ge(b_mx, 3 * b + 2)
                    pe.wait_ge(b_mix, 3 * b + 3)
                    to_channels(PS_B[:, 0, 0:C], "k", C, 0, MX[:, 0])

            def b_decay2(b, _):
                pe.wait_ge(b_dt, b + 1)
                for m in range(CT):
                    last = pe.matmul(PS_B[:, 1, m * T:(m + 1) * T], w("dec2", 0, C, m * P, (m + 1) * P)[0:DE],
                                     DT[0:DE, :], start=True, stop=True)
                last.then_inc(b_d2ps, 1)

            def b_valgate(b, k):
                if k:
                    to_tokens(PS_B[:, 0, C:2 * C], "g", C, 0, MX[:, 4]).then_inc(b_vgps, 1)
                else:
                    pe.wait_ge(b_mx, 3 * b + 3)
                    pe.wait_ge(b_kr, b + 1)
                    to_tokens(PS_B[:, 0, 0:C], "v", C, 0, MX[:, 2])

            def d_vturn(b, n):
                t, half = n // 2, n % 2
                if n == 0:
                    pe.wait_ge(b_v, 2 * b + 1)
                    pe.wait_ge(d_f, b)
                else:
                    pe.wait_ge(d_a, 4 * b + n)
                    if n == 2:
                        pe.wait_ge(b_v, 2 * b + 2)
                for j in range(4):
                    last = pe.transpose(PS_D[:, j * T:(j + 1) * T],
                                        V8[:, t, 4 * half + j].rearrange("p h k -> p (h k)"), ident)
                last.then_inc(d_vps, 1)

            def d_own(b, _):
                pe.wait_ge(d_rk, b + 1)
                pe.wait_ge(d_a, 4 * b + 4)
                for t in range(CT):
                    last = pe.matmul(PS_D[:, t * (P // RS):(t + 1) * (P // RS)], RK[:, t, :], hsel,
                                     start=True, stop=True)
                last.then_inc(d_cps, 1)

            def d_read(b, _):
                pe.wait_ge(d_cv, b + 1)
                pe.wait_ge(d_rs, 2 * b + 2)
                for t in range(CT):
                    for half in range(2):
                        at = 32 * (2 * t + half)
                        last = pe.matmul(PS_D[at:at + 32, :], hsel32,
                                         SS[:, t, 4 * half:4 * half + 4, :].rearrange("p d n -> p (d n)"),
                                         start=True, stop=True, skip_group_check=True)
                last.then_inc(d_ops, 1)

            def d_oturn(b, _):
                pe.wait_ge(d_oh, b + 1)
                for j in range(4):
                    last = pe.transpose(PS_D[:, j * T:(j + 1) * T], OH[:, j, :], ident)
                last.then_inc(d_otps, 1)

            def d_yturn(b, _):
                pe.wait_ge(d_y, b + 1)
                turn(PS_D[:, 0:C], Y).then_inc(d_yps, 1)

            def d_out(b, _):
                pe.wait_ge(d_yt, b + 1)
                if not later(b):
                    pe.wait_ge(in_wd, IN_WD)
                to_tokens(PS_D[:, 0:C], "o", C, 0, YT).then_inc(d_wops, 1)

            def d_turn(b, _):
                pe.wait_ge(d_nrm, b + 1)
                turn(PS_D[:, 0:C], D_N).then_inc(d_lnps, 1)

            def d_keyrec(b, k):
                pe.wait_ge(d_xkr, 2 * b + k + 1)
                if k:
                    to_tokens(PS_D[:, C:2 * C], "fr", C, 0, XR).then_inc(d_krps, 1)
                else:
                    to_channels(PS_D[:, 0:C], "fk", C, 0, XK)

            def d_val(b, _):
                pe.wait_ge(d_kk, b + 1)
                pe.wait_ge(d_rr, b + 1)
                to_tokens(PS_D[:, 0:C], "fv", C, 0, KK).then_inc(d_fps, 1)

            pieces = named(a_enc_turn, a_turn, a_val, a_key, a_query, a_scores, a_prob_turn, a_pv, a_out,
                           b_turn, b_mlp1, b_mlp2, b_low1, b_low2, b_decay1, b_keyrec, b_decay2, b_valgate,
                           d_vturn, d_own, d_read, d_oturn, d_yturn, d_out, d_turn, d_keyrec, d_val)
            for i in range(PEEL):
                run(pieces, PE_ORDER, i)
            with pe.Fori(PEEL, B) as i:
                run(pieces, PE_ORDER, i)
            for i in range(B, B + LAG):
                run(pieces, PE_ORDER, i)

        @block.vector
        def _(dve):
            dve.memset(VP[:, :, :, :], 0.0)
            dve.memset(W8[:, :, :, 0:1], 0.0).then_inc(set_dve, 1)
            dve.wait_ge(set_col, 1)
            dve.tensor_copy(COL[:, :], PS_D[:, 0:C_END]).then_inc(set_dve, 1)
            dve.wait_ge(in_first, IN_FIRST)
            dve.wait_ge(set_dve, 2)
            for a in range(2):
                for par in range(2):
                    last = dve.tensor_scalar(QB[:, a, par, :], col(f"bq{a}", 0, 2), CST[:, K_PAR + par:K_PAR + par + 1],
                                             None, ALU.mult)
            last.then_inc(set_dve, 1)

            def row_stats(b, stat, ST):
                dve.sem_inc(passed_dve, 1)
                dve.bn_stats(ST[:, :], X[:, b, :]).then_inc(stat, 1)

            def moments(n, stat, var, ST, MV):
                dve.wait_ge(stat, n + 1)
                dve.sem_inc(passed_dve, 1)
                dve.bn_aggr(MV[:, :], ST[:, :]).then_inc(var, 1)

            def normalise(b, MV, RS_, N):
                return dve.tensor_scalar(N[:, :], X[:, b, :], MV[:, 0:1], RS_[:, 0:1], ALU.subtract, ALU.mult)

            def a_stats(b, a):
                if a:
                    dve.wait_ge(a_res, 2 * b + 1)
                elif isinstance(b, int) and b == 1:
                    dve.wait_ge(in_rest, IN_REST)
                dve.wait_ge(a_var, 2 * b + a)
                row_stats(b, a_stat, A_ST)

            def a_moments(b, a):
                dve.wait_ge(a_nrm, 2 * b + a)
                moments(2 * b + a, a_stat, a_var, A_ST, A_MV)

            def a_normal(b, a):
                dve.wait_ge(a_rstd, 2 * b + a + 1)
                dve.wait_ge(a_lnps, 2 * b + a)
                normalise(b, A_MV, A_RS, A_N).then_inc(a_nrm, 1)

            def a_val(b, a):
                if not later(b, a):
                    dve.wait_ge(in_rows, IN_ROWS)
                dve.wait_ge(a_kps, 2 * b + a + 1)
                dve.wait_ge(a_pvps, 2 * b + a)
                v = values.rearrange("p (h q d) -> p h q d", q=2, d=HD)
                bias = row(f"bv{a}").rearrange("p (h q d) -> p h q d", q=2, d=HD)
                for q in range(2):
                    last = dve.tensor_tensor(VP[:, :, q, q * HD:(q + 1) * HD], v[:, :, q, :], bias[:, :, q, :],
                                             ALU.add)
                last.then_inc(a_v, 1)

            def a_key(b, a):
                dve.wait_ge(a_kps, 2 * b + a + 1)
                dve.tensor_tensor(KT[:, :, :], tiles(keys), over_tokens(col(f"bk{a}", 0, 2), CT), ALU.add)\
                    .then_inc(a_k, 1)

            def a_mask(b, arg):
                a, g = arg
                dve.wait_ge(a_score, 8 * b + 4 * a + g + 1)
                if later(b, a):
                    dve.wait_ge(a_turned, 8 * b + 4 * a + g - 3)
                if not later(b) and a and g == 0:
                    dve.wait_ge(in_rest, IN_REST)
                mask = MASK[:, b, :] if a else MASK[:, B, :]
                dve.tensor_tensor(SC[:, g], PS_S[:, g % 3], over_heads(mask), ALU.mult).then_inc(a_masked, 1)

            def a_maxima(b, arg):
                a, g = arg
                dve.wait_ge(a_added, 8 * b + 4 * a + g + 1)
                dve.tensor_reduce(NMX[:, GH * g:GH * g + GH], SC[:, g], AX_X, ALU.max, negate=True)\
                    .then_inc(a_max, 1)

            def a_inverse(b, arg):
                a, g = arg
                dve.wait_ge(a_exp, 8 * b + 4 * a + g + 1)
                dve.reciprocal(RINV[:, GH * g:GH * g + GH], SUM[:, GH * g:GH * g + GH]).then_inc(a_inv, 1)

            def a_sum(b, a):
                dve.wait_ge(a_ops, 2 * b + a + 1)
                dve.wait_ge(a_bias, 2 * b + a + 1)
                dve.tensor_tensor(X[:, b, :], PS_T[:, 1, 0:C], X[:, b, :], ALU.add).then_inc(a_res, 1)

            def b_stats(b, k):
                if k:
                    dve.wait_ge(b_res, b + 1)
                else:
                    dve.wait_ge(a_res, 2 * b + 2)
                dve.wait_ge(b_var, 2 * b + k)
                row_stats(b, b_stat, B_ST)

            def b_moments(b, k):
                dve.wait_ge(b_nrm, 2 * b + k)
                moments(2 * b + k, b_stat, b_var, B_ST, B_MV)

            def b_normal(b, k):
                dve.wait_ge(b_rstd, 2 * b + k + 1)
                normalise(b, B_MV, B_RS, B_N).then_inc(b_nrm, 1)

            def b_hidden(b, k):
                dve.wait_ge(b_up, 2 * b + k + 1)
                h = HX[:, k * FT // 2:(k + 1) * FT // 2, :]
                dve.tensor_tensor(h, PS_B[:, 1 - k, :].rearrange("p (m n) -> p m n", n=T),
                                  over_tokens(col("b1", k * FT // 2, FT // 2), FT // 2), ALU.add).then_inc(b_hx, 1)

            def b_cubes(b, k):
                h = slice(k * FT // 2, (k + 1) * FT // 2)
                dve.wait_ge(b_sq, 2 * b + k + 1)
                dve.scalar_tensor_tensor(HQ[:, h, :], HQ[:, h, :], GELU_C, HX[:, h, :], ALU.add, ALU.mult)\
                    .then_inc(b_cube, 1)

            def b_gelu(b, k):
                h = slice(k * FT // 2, (k + 1) * FT // 2)
                dve.wait_ge(b_tanh, 2 * b + k + 1)
                dve.scalar_tensor_tensor(HG[:, h, :], HQ[:, h, :], 1.0, HX[:, h, :], ALU.add, ALU.mult)\
                    .then_inc(b_hg, 1)

            def b_sum(b, _):
                dve.wait_ge(b_dnps, b + 1)
                dve.wait_ge(b_bias, b + 1)
                dve.tensor_tensor(X[:, b, :], PS_B[:, 1, 0:C], X[:, b, :], ALU.add).then_inc(b_res, 1)

            def b_shift(b, _):
                dve.wait_ge(b_first, b + 1)
                dve.wait_ge(b_ln, 2 * b + 2)
                dve.tensor_tensor(SX[:, :, :], XN[:, :, 0:T], XN[:, :, 1:T + 1], ALU.subtract).then_inc(b_sx, 1)

            def b_mixed(b, _):
                dve.wait_ge(b_sx, b + 1)
                for t in range(CT):
                    last = dve.scalar_tensor_tensor(XX[:, t, :], SX[:, t, :], col("maa_x", t), XN[:, t, 1:T + 1],
                                                    ALU.mult, ALU.add)
                last.then_inc(b_xx, 1)

            def b_streams(b, n):
                dve.wait_ge(b_m2ps, 3 * b + n + 1)
                for k, i in enumerate(MIX_TURNS[n]):
                    for t in range(CT):
                        at = k * C + t * T
                        last = dve.scalar_tensor_tensor(MX[:, i, t, :], PS_B[:, n % 2, at:at + T], col("stack", 2 * i + t),
                                                        SX[:, t, :], ALU.add, ALU.mult)
                last.then_inc(b_mix, 1)

            def b_gate(b, _):
                dve.wait_ge(b_tg, b + 1)
                dve.wait_ge(b_v, 2 * b + 2)
                dve.wait_ge(d_y, b)
                dve.scalar_tensor_tensor(G[:, :], TG[:, :], 1.0, PS_B[:, 0, C:2 * C], ALU.add, ALU.mult)\
                    .then_inc(b_g, 1)

            def d_outer(b, n):
                t, half = n // 2, n % 2
                dve.wait_ge(d_vps, 4 * b + n + 1)
                if n == 0:
                    dve.wait_ge(b_kr, b + 1)
                v = PS_D[:, :].rearrange("p (d n) -> p d n", n=T)
                k = KR[:, 0, t, 0:T - 1].unsqueeze(1).to_broadcast([P, 4, T - 1])
                dve.tensor_tensor(AJ[:, t, 4 * half:4 * half + 4, 1:T], v[:, :, 0:T - 1], k, ALU.mult)\
                    .then_inc(d_a, 1)

            def d_scan(b, t):
                if t == 0:
                    dve.wait_ge(d_s0, b + 1)
                    dve.wait_ge(b_w8, b + 1)
                dve.wait_ge(d_a, 4 * b + 2 * t + 2)
                dve.tensor_tensor_scan(SS[:, t].rearrange("p d n -> p (d n)"), W8[:, t].rearrange("p d n -> p (d n)"),
                                       AJ[:, t].rearrange("p d n -> p (d n)"), 0.0, ALU.mult, ALU.add)\
                    .then_inc(d_s, 1)

            def d_ruk(b, _):
                dve.wait_ge(b_kr, b + 1)
                for k in range(CT):
                    last = dve.scalar_tensor_tensor(RK[:, k, :], KR[:, 1, k, :], col("u", k), KR[:, 0, k, :],
                                                    ALU.mult, ALU.mult)
                last.then_inc(d_rk, 1)

            def d_rstate(b, _):
                dve.wait_ge(d_s, 2 * b + 1)
                r = KR[:, 1, 0, :].unsqueeze(1).to_broadcast([P, RS, T])
                dve.tensor_tensor(SS[:, 0], SS[:, 0], r, ALU.mult).then_inc(d_rs, 1)

            def d_own(b, _):
                dve.wait_ge(d_cps, b + 1)
                n = P // RS
                for t in range(CT):
                    last = dve.tensor_tensor(heads(CV[:, t * P:(t + 1) * P]),
                                             V8[:, t, :, :, 0].rearrange("p d h -> p h d"),
                                             over_tokens(PS_D[:, t * n:(t + 1) * n], n, RS), ALU.mult)
                last.then_inc(d_cv, 1)

            def d_output(b, _):
                dve.wait_ge(d_otps, b + 1)
                o = PS_D[:, :].rearrange("p (j t e h) -> p t h e j", j=4, t=CT, e=2)
                for t in range(CT):
                    last = dve.tensor_tensor(O[:, t * P:(t + 1) * P].rearrange("p (h e j) -> p h e j", e=2, j=4),
                                             o[:, t, 0:P // RS],
                                             CV[:, t * P:(t + 1) * P].rearrange("p (h e j) -> p h e j", e=2, j=4),
                                             ALU.add)
                last.then_inc(d_o, 1)

            def d_means(b, _):
                dve.wait_ge(d_o, b + 1)
                dve.tensor_reduce(GM[:, :], heads(O[:, :]), AX_X, ALU.add).then_inc(d_m, 1)

            def d_centre(b, _):
                dve.wait_ge(d_m, b + 1)
                dve.scalar_tensor_tensor(heads(O[:, :]), over_tokens(GM[:, :], RH, RS), -1.0 / RS, heads(O[:, :]),
                                         ALU.mult, ALU.add).then_inc(d_cen, 1)

            def d_spread(b, _):
                dve.wait_ge(d_sq, b + 1)
                dve.tensor_reduce(GV[:, :], heads(OQ[:, :]), AX_X, ALU.add).then_inc(d_v, 1)

            def d_guess(b, step):
                if step == 0:
                    dve.wait_ge(d_v, b + 1)
                    dve.tensor_scalar(GE[:, :], GV[:, :], 1.0 / RS, EPS, ALU.mult, ALU.add).then_inc(d_gr, 1)
                elif step == 1:
                    dve.wait_ge(d_gr, 12 * b + 1)
                    dve.tensor_scalar(GT[:, :].bitcast(I32), GE[:, :].bitcast(I32), 1, None,
                                      ALU.logical_shift_right).then_inc(d_gr, 1)
                else:
                    dve.wait_ge(d_gr, 12 * b + 2)
                    dve.tensor_scalar(GY[:, :].bitcast(I32), GT[:, :].bitcast(I32), -1.0, float(0x5F3759DF),
                                      ALU.mult, ALU.add).then_inc(d_gr, 1)

            def d_newton(b, arg):
                n, step = arg
                dve.wait_ge(d_gr, 12 * b + 3 * n + step + 3)
                if step == 0:
                    dve.scalar_tensor_tensor(GT[:, :], GY[:, :], -0.5, GE[:, :], ALU.mult, ALU.mult)\
                        .then_inc(d_gr, 1)
                elif step == 1:
                    dve.tensor_tensor(GT[:, :], GT[:, :], GY[:, :], ALU.mult).then_inc(d_gr, 1)
                else:
                    dve.scalar_tensor_tensor(GY[:, :], GT[:, :], 1.5, GY[:, :], ALU.add, ALU.mult)\
                        .then_inc(d_gr, 1)

            def d_gated(b, _):
                dve.wait_ge(d_gb, b + 1)
                dve.wait_ge(b_g, b + 1)
                dve.scalar_tensor_tensor(Y[:, :], O[:, :], 0.5, G[:, :], ALU.mult, ALU.mult).then_inc(d_y, 1)

            def d_sum(b, _):
                dve.wait_ge(d_wops, b + 1)
                dve.tensor_tensor(X[:, b, :], PS_D[:, 0:C], X[:, b, :], ALU.add).then_inc(d_res, 1)

            def d_stats(b, _):
                dve.wait_ge(d_res, b + 1)
                dve.wait_ge(d_var, b)
                row_stats(b, d_stat, D_ST)

            def d_moments(b, _):
                dve.wait_ge(d_nrm, b)
                moments(b, d_stat, d_var, D_ST, D_MV)

            def d_normal(b, _):
                dve.wait_ge(d_rstd, b + 1)
                normalise(b, D_MV, D_RS, D_N).then_inc(d_nrm, 1)

            def d_shift(b, _):
                dve.wait_ge(d_first, b + 1)
                dve.wait_ge(d_ln, b + 1)
                dve.tensor_tensor(SM[:, :, :], XM[:, :, 0:T], XM[:, :, 1:T + 1], ALU.subtract).then_inc(d_sx, 1)

            def d_mixed(b, k):
                dve.wait_ge(d_sx, b + 1)
                dst, name = ((XK, "fmk"), (XR, "fmr"))[k]
                for t in range(CT):
                    last = dve.scalar_tensor_tensor(dst[:, t, :], SM[:, t, :], col(name, t), XM[:, t, 1:T + 1],
                                                    ALU.mult, ALU.add)
                last.then_inc(d_xkr, 1)

            def d_mixing(b, _):
                dve.wait_ge(d_rr, b + 1)
                dve.wait_ge(d_fps, b + 1)
                dve.scalar_tensor_tensor(RR[:, :], RR[:, :], 1.0, PS_D[:, 0:C], ALU.add, ALU.mult).then_inc(d_f, 1)

            def d_final(b, _):
                dve.wait_ge(d_f, b + 1)
                dve.scalar_tensor_tensor(X[:, b, :], RR[:, :], 0.5, X[:, b, :], ALU.mult, ALU.add)\
                    .then_inc(d_fin, 1)

            pieces = named(a_stats, a_moments, a_normal, a_val, a_key, a_mask, a_maxima, a_inverse, a_sum,
                           b_stats, b_moments, b_normal, b_hidden, b_cubes, b_gelu, b_sum, b_shift,
                           b_mixed, b_streams, b_gate, d_outer, d_scan, d_ruk, d_rstate, d_own, d_output, d_means,
                           d_centre, d_spread, d_guess, d_newton, d_gated, d_sum, d_stats,
                           d_moments, d_normal, d_shift, d_mixed, d_mixing, d_final)
            for i in range(PEEL):
                run(pieces, DVE_ORDER, i)
            with dve.Fori(PEEL, B) as i:
                run(pieces, DVE_ORDER, i)
            for i in range(B, B + LAG):
                run(pieces, DVE_ORDER, i)

        @block.scalar
        def _(act):
            act.wait_ge(in_first, IN_FIRST)
            act.wait_ge(set_dve, 3)

            def turned(dst, src, s, bias):
                for t in range(CT):
                    last = act.activation(dst[:, t, :], src[:, t * T:(t + 1) * T], ACT.Identity,
                                          bias=col(bias, t), scale=col(s, t))
                return last

            def a_enc_copy(b, _):
                act.wait_ge(a_encps, b + 1)
                act.wait_ge(a_prev, b)
                act.activation(A_ET[:, :, :], tiles(turns), ACT.Copy).then_inc(a_enc, 1)

            def a_scale(b, a):
                act.wait_ge(a_lnps, 2 * b + a + 1)
                turned(A_LT, turns, f"ln{a + 1}_s", f"ln{a + 1}_b").then_inc(a_ln, 1)

            def a_query(b, arg):
                a, par = arg
                act.wait_ge(a_qps, 2 * b + a + 1)
                for t in range(CT):
                    last = act.activation(QP[:, par, t, :], queries[:, t * T:(t + 1) * T], ACT.Identity,
                                          bias=QB[:, a, par, t:t + 1], scale=CST[:, K_PAR + par:K_PAR + par + 1])
                last.then_inc(a_q, 1)

            def a_exps(b, arg):
                a, g, half = arg
                act.wait_ge(a_max, 8 * b + 4 * a + g + 1)
                for j in range(half * GH // 2, (half + 1) * GH // 2):
                    h = GH * g + j
                    last = act.activation(SC[:, g, j, :], SC[:, g, j, :], ACT.Exp, bias=NMX[:, h:h + 1],
                                          accum_out=SUM[:, h:h + 1])
                if half:
                    last.then_inc(a_exp, 1)

            def a_prob_copy(b, arg):
                a, g = arg
                act.wait_ge(a_turned, 8 * b + 4 * a + g + 1)
                act.activation(PT[:, g], PS_T[:, g % 2].rearrange("p (j n) -> p j n", n=T), ACT.Copy)\
                    .then_inc(a_pt, 1)

            def a_ctx_copy(b, a):
                act.wait_ge(a_pvps, 2 * b + a + 1)
                act.activation(CTX[:, :, :], tiles(PS_T[:, 0, 0:C]), ACT.Copy).then_inc(a_ctx, 1)

            def b_scale(b, k):
                act.wait_ge(b_lnps, 2 * b + k + 1)
                if k:
                    turned(XN[:, :, 1:T + 1], PS_B[:, 0], "r1_w", "r1_b").then_inc(b_ln, 1)
                else:
                    turned(B_LT, PS_B[:, 0], "ln3_s", "ln3_b").then_inc(b_ln, 1)

            def b_square(b, k):
                h = slice(k * FT // 2, (k + 1) * FT // 2)
                act.wait_ge(b_hx, 2 * b + k + 1)
                act.activation(HQ[:, h, :], HX[:, h, :], ACT.Square, scale=(GELU_A * GELU_C) ** 0.5)\
                    .then_inc(b_sq, 1)

            def b_tanhs(b, k):
                h = slice(k * FT // 2, (k + 1) * FT // 2)
                act.wait_ge(b_cube, 2 * b + k + 1)
                act.activation(HQ[:, h, :], HQ[:, h, :], ACT.Tanh).then_inc(b_tanh, 1)

            def b_low(b, _):
                act.wait_ge(b_m1ps, b + 1)
                act.activation(MT[:, :, :], tiles(PS_B[:, 1, 0:C]), ACT.Tanh).then_inc(b_mt, 1)

            def b_decay1(b, _):
                act.wait_ge(b_d1ps, b + 1)
                act.activation(DT[0:DE, :], PS_B[0:DE, 1, 0:T], ACT.Tanh).then_inc(b_dt, 1)

            def b_keyrec(b, _):
                act.wait_ge(b_krps, b + 1)
                act.wait_ge(d_rs, 2 * b)
                act.wait_ge(d_rk, b)
                act.activation(KR[:, :, :, :].rearrange("p a t n -> p (a t n)"), PS_B[:, 0, :], ACT.Copy)\
                    .then_inc(b_kr, 1)

            def b_decay2(b, _):
                act.wait_ge(b_d2ps, b + 1)
                for t in range(CT):
                    last = act.activation(EW[:, t, :], PS_B[:, 1, t * T:(t + 1) * T], ACT.Exp, bias=col("td", t))
                last.then_inc(b_ew, 1)

            def b_decays(b, _):
                act.wait_ge(b_ew, b + 1)
                act.wait_ge(d_s, 2 * b)
                for t in range(CT):
                    e = EW[:, t, 0:T - 1].unsqueeze(1).to_broadcast([P, RS, T - 1])
                    last = act.activation(W8[:, t, :, 1:T], e, ACT.Exp, scale=-1.0)
                last.then_inc(b_w8, 1)

            def b_values(b, t):
                act.wait_ge(b_vgps, b + 1)
                act.wait_ge(d_cv, b)
                v = heads(PS_B[:, 0, t * P:(t + 1) * P]).rearrange("p h d -> p d h").unsqueeze(3)
                act.activation(V8[:, t], v.to_broadcast([P, RS, P // RS, RS]), ACT.Copy).then_inc(b_v, 1)

            def b_gatetanh(b, _):
                act.wait_ge(b_vgps, b + 1)
                act.wait_ge(b_g, b)
                act.activation(TG[:, :], PS_B[:, 0, C:2 * C], ACT.Tanh, scale=0.5).then_inc(b_tg, 1)

            def d_ocopy(b, _):
                act.wait_ge(d_ops, b + 1)
                act.activation(OH[:, :, :].rearrange("p j n -> p (j n)"), PS_D[:, :], ACT.Copy).then_inc(d_oh, 1)

            def d_ycopy(b, _):
                act.wait_ge(d_yps, b + 1)
                act.activation(YT[:, :, :], tiles(PS_D[:, 0:C]), ACT.Copy).then_inc(d_yt, 1)

            def d_scale(b, _):
                act.wait_ge(d_lnps, b + 1)
                turned(XM[:, :, 1:T + 1], PS_D[:, 0:C], "r2_w", "r2_b").then_inc(d_ln, 1)

            def d_keyrec(b, _):
                act.wait_ge(d_krps, b + 1)
                act.activation(RL[:, :, :], tiles(PS_D[:, 0:C]), ACT.Relu).then_inc(d_relu, 1)
                act.activation(RR[:, :], PS_D[:, C:2 * C], ACT.Tanh, scale=0.5).then_inc(d_rr, 1)

            pieces = named(a_enc_copy, a_scale, a_query, a_exps, a_prob_copy, a_ctx_copy,
                           b_scale, b_square, b_tanhs, b_low, b_decay1, b_keyrec, b_decay2, b_decays, b_values,
                           b_gatetanh, d_ocopy, d_ycopy, d_scale, d_keyrec)
            for i in range(PEEL):
                run(pieces, ACT_ORDER, i)
            with act.Fori(PEEL, B) as i:
                run(pieces, ACT_ORDER, i)
            for i in range(B, B + LAG):
                run(pieces, ACT_ORDER, i)

        @block.gpsimd
        def _(pool):
            pool.wait_ge(in_first, IN_FIRST)

            def inverse_root(n, eps, MV, RS_):
                pool.sem_inc(passed_pool, 1)
                pool.tensor_scalar(RS_[:, 0:1], MV[:, 1:2], 1.0, EPS, ALU.mult, ALU.add).then_inc(eps, 1)
                pool.wait_ge(eps, n + 1)
                return pool.tensor_tensor(RS_[:, 0:1], RS_[:, 0:1], CST[:, K_POW:K_POW + 1], ALU.pow)

            def a_root(b, a):
                pool.wait_ge(a_var, 2 * b + a + 1)
                inverse_root(2 * b + a, a_eps, A_MV, A_RS).then_inc(a_rstd, 1)

            def a_addbias(b, a):
                pool.wait_ge(a_nrm, 2 * b + a + 1)
                if not later(b, a):
                    pool.wait_ge(in_rows, IN_ROWS)
                pool.sem_inc(passed_pool, 1)
                pool.tensor_tensor(X[:, b, :], X[:, b, :], row("co" if a else "ao"), ALU.add).then_inc(a_bias, 1)

            def a_before(b, _):
                pool.wait_ge(a_enc, b + 1)
                pool.tensor_copy(PREV[:, b, :, :], A_ET[:, :, 0:2]).then_inc(a_prev, 1)

            def a_addmask(b, arg):
                a, g = arg
                if not later(b, a) and g == 0:
                    pool.wait_ge(in_rows, IN_ROWS)
                    pool.tensor_scalar(MADD[:, B, :], MASK[:, B, :], -1.0, 1.0, ALU.mult, ALU.add)\
                        .then_inc(set_self, 1)
                    pool.wait_ge(set_self, 1)
                    pool.tensor_scalar(MADD[:, B, :], MADD[:, B, :], -10000.0, 0.0, ALU.mult, ALU.add)\
                        .then_inc(set_self, 1)
                    pool.wait_ge(set_self, 2)
                if not later(b) and a and g == 0:
                    pool.wait_ge(in_rest, IN_REST)
                    pool.tensor_scalar(MADD[:, 0:B, :], MASK[:, 0:B, :], -1.0, 1.0, ALU.mult, ALU.add)\
                        .then_inc(set_cross, 1)
                    pool.wait_ge(set_cross, 1)
                    pool.tensor_scalar(MADD[:, 0:B, :], MADD[:, 0:B, :], -10000.0, 0.0, ALU.mult, ALU.add)\
                        .then_inc(set_cross, 1)
                    pool.wait_ge(set_cross, 2)
                pool.wait_ge(a_masked, 8 * b + 4 * a + g + 1)
                if a:
                    pool.sem_inc(passed_pool, 1)
                    pool.tensor_tensor(SC[:, g], SC[:, g], over_heads(MADD[:, b, :]), ALU.add).then_inc(a_added, 1)
                else:
                    pool.tensor_tensor(SC[:, g], SC[:, g], over_heads(MADD[:, B, :]), ALU.add).then_inc(a_added, 1)

            def a_divide(b, arg):
                a, g = arg
                pool.wait_ge(a_inv, 8 * b + 4 * a + g + 1)
                pool.tensor_tensor(SC[:, g], SC[:, g], over_tokens(RINV[:, GH * g:GH * g + GH], GH), ALU.mult)\
                    .then_inc(a_prob, 1)

            def b_root(b, k):
                pool.wait_ge(b_var, 2 * b + k + 1)
                inverse_root(2 * b + k, b_eps, B_MV, B_RS).then_inc(b_rstd, 1)
                if not later(b, k):
                    pool.wait_ge(in_wb, IN_WB)
                    w2 = W[:, W_AT["w2"]:W_AT["w2"] + FT * C]
                    pool.tensor_scalar(w2, w2, 0.5, 0.0, ALU.mult, ALU.add).then_inc(set_w2, 1)

            def b_addbias(b, _):
                pool.wait_ge(b_nrm, 2 * b + 1)
                pool.sem_inc(passed_pool, 1)
                pool.tensor_tensor(X[:, b, :], X[:, b, :], row("b2"), ALU.add).then_inc(b_bias, 1)
                pool.wait_ge(b_sx, b)
                pool.wait_ge(a_prev, b + 1)
                pool.tensor_copy(XN[:, :, 0:1], PREV[:, b, :, 1:2]).then_inc(b_first, 1)

            def b_addnorm(b, n):
                pool.wait_ge(b_mix, 3 * b + n + 1)
                for i in MIX_TURNS[n]:
                    last = pool.tensor_tensor(MX[:, i], MX[:, i], XN[:, :, 1:T + 1], ALU.add)
                last.then_inc(b_mx, 1)

            def d_first_states(b, _):
                if not later(b):
                    pool.wait_ge(in_states, IN_STATES)
                pool.wait_ge(d_s, 2 * b)
                pool.tensor_copy(AJ[:, :, :, 0:1], S0[:, b, :, :].unsqueeze(3)).then_inc(d_s0, 1)

            def d_rstate(b, _):
                pool.wait_ge(d_s, 2 * b + 2)
                r = KR[:, 1, 1, :].unsqueeze(1).to_broadcast([P, RS, T])
                pool.tensor_tensor(SS[:, 1], SS[:, 1], r, ALU.mult).then_inc(d_rs, 1)

            def d_squares(b, _):
                pool.wait_ge(d_cen, b + 1)
                pool.tensor_tensor(OQ[:, :], O[:, :], O[:, :], ALU.mult).then_inc(d_sq, 1)

            def d_norm(b, _):
                pool.wait_ge(d_gr, 12 * b + 12)
                pool.tensor_tensor(heads(O[:, :]), heads(O[:, :]), over_tokens(GY[:, :], RH, RS), ALU.mult)\
                    .then_inc(d_n, 1)

            def d_weight(b, _):
                pool.wait_ge(d_n, b + 1)
                pool.tensor_tensor(O[:, :], O[:, :], row("gn_w"), ALU.mult).then_inc(d_gw, 1)

            def d_bias(b, _):
                pool.wait_ge(d_gw, b + 1)
                pool.tensor_tensor(O[:, :], O[:, :], row("gn_b"), ALU.add).then_inc(d_gb, 1)

            def d_root(b, _):
                pool.wait_ge(d_var, b + 1)
                inverse_root(b, d_eps, D_MV, D_RS).then_inc(d_rstd, 1)

            def d_before(b, _):
                pool.wait_ge(d_sx, b)
                pool.tensor_copy(XM[:, :, 0:1], PREV[:, b, :, 0:1]).then_inc(d_first, 1)

            def d_relu2(b, _):
                pool.wait_ge(d_relu, b + 1)
                pool.tensor_tensor(KK[:, :, :], RL[:, :, :], RL[:, :, :], ALU.mult).then_inc(d_kk, 1)

            pieces = named(a_root, a_addbias, a_before, a_addmask, a_divide, b_root, b_addbias, b_addnorm,
                           d_first_states, d_rstate, d_squares, d_norm, d_weight, d_bias, d_root, d_before, d_relu2)
            for i in range(PEEL):
                run(pieces, POOL_ORDER, i)
            with pool.Fori(PEEL, B) as i:
                run(pieces, POOL_ORDER, i)
            for i in range(B, B + LAG):
                run(pieces, POOL_ORDER, i)


def kernel(**inputs):
    import concourse.bacc as _bacc
    from concourse.bass_utils import run_bass_kernel_spmd as _run

    a = {k: np.asarray(v) for k, v in inputs.items()}

    def l0(n):
        return a["L0_xattn_" + n]

    def l1(n):
        return a["L1_xattn_" + n]

    def packed(m):
        k = m.shape[0] // P
        return m.reshape(k, P, m.shape[1]).transpose(1, 0, 2).reshape(P, -1)

    def padded(m, shape, at=0):
        out = np.zeros(shape, m.dtype)
        out[at:at + m.shape[0], :m.shape[1]] = m
        return out

    parts = {
        "qkv": packed(l0("w_qkv")), "ao": packed(l0("w_ao")), "q": packed(l0("w_q")), "kv": packed(l0("w_kv")),
        "co": packed(l0("w_co")), "w1": packed(l0("w1")), "w2": packed(l0("w2")),
        "maa1": packed(padded(l1("maa_w1"), (C, C))),
        "maa2": np.concatenate([padded(l1("maa_w2")[i], (P, C), i * ME % P) for i in range(MIX)], axis=1),
        "dec1": packed(l1("decay_w1")), "dec2": padded(l1("decay_w2"), (P, C)),
        "r": packed(l1("Wr").T), "k": packed(l1("Wk").T), "v": packed(l1("Wv").T), "g": packed(l1("Wg").T),
        "o": packed(l1("Wo").T), "fk": packed(l1("ffn_Wk").T), "fr": packed(l1("ffn_Wr").T),
        "fv": packed(l1("ffn_Wv").T)}
    weights = np.concatenate([parts[name] for name, _ in WEIGHTS], axis=1)
    vectors = {
        "ln1_s": l0("ln1_s"), "ln1_b": l0("ln1_b"), "bq0": l0("b_qkv")[0:C], "bk0": l0("b_qkv")[C:2 * C],
        "ln2_s": l0("ln2_s"), "ln2_b": l0("ln2_b"), "bq1": l0("b_q"), "bk1": l0("b_kv")[0:C],
        "ln3_s": l0("ln3_s"), "ln3_b": l0("ln3_b"), "b1": l0("b1"), "r1_w": l1("ln1_w"), "r1_b": l1("ln1_b"),
        "maa_x": l1("maa_x"), "stack": l1("maa_stack"), "td": l1("time_decay"), "u": l1("faaaa"),
        "r2_w": l1("ln2_w"), "r2_b": l1("ln2_b"), "fmk": l1("ffn_maa_k"), "fmr": l1("ffn_maa_r")}
    cols = np.concatenate([vectors[name].reshape(-1, P) for name, _ in COLS], axis=0)
    by_row = {"bv0": l0("b_qkv")[2 * C:], "ao": l0("b_ao"), "bv1": l0("b_kv")[C:], "co": l0("b_co"), "b2": l0("b2"),
              "gn_w": l1("gn_w"), "gn_b": l1("gn_b")}
    rows = np.stack([by_row[name] for name in ROWS])
    consts = np.zeros((P, K_END), np.float32)
    for p in range(P):
        consts[p, K_ID + p] = 1.0
        consts[p, K_SEL + p // RS] = 1.0
        consts[p, K_PAR + (p // HD) % 2] = 1.0 / HD ** 0.5
    consts[:, K_POW] = -0.5

    arrays = {"x": a["x"], "enc": a["ctx_2048"], "mask_self": a["mask_1x1xSxS2_fc1"].reshape(T, T),
              "mask_cross": a["mask_Bx1xSxS2_ff1"].reshape(B, T, T), "weights": weights, "cols": cols, "rows": rows,
              "consts": consts}
    nc = _bacc.Bacc("TRN2", target_bir_lowering=False, num_devices=1)
    args, ins = {}, {}
    for name, v in arrays.items():
        v = np.ascontiguousarray(v)
        ins[f"in_{name}"] = v
        args[name] = nc.dram_tensor(f"in_{name}", v.shape, mybir.dt.from_np(v.dtype), kind="ExternalInput").ap()
    args["out"] = nc.dram_tensor("out_0", (B, T, C), F32, kind="ExternalOutput").ap()
    build(nc, **args)
    r = _run(nc, [ins], core_ids=[0])
    return r.results[0]["out_0"]
```
